# Optimizing a Trainium2 kernel written in Bass

```python
import numpy as np
import jax
import jax.numpy as jnp

def _softmax(x, axis=-1):
    return jax.nn.softmax(x, axis=axis)
def _gelu(x):
    return jax.nn.gelu(x, approximate=True)
def _silu(x):
    return jax.nn.silu(x)
def _sigmoid(x):
    return jax.nn.sigmoid(x)
def _layernorm(x, axis=-1, eps=1e-5):
    m = jnp.mean(x, axis=axis, keepdims=True)
    v = jnp.var(x, axis=axis, keepdims=True)
    return (x - m) / jnp.sqrt(v + eps)
def _scatter_add(tgt, idx, src, axis=0):
    return tgt.at[idx].add(src)
def _segment_sum(src, seg, n):
    return jax.ops.segment_sum(src, seg, n)

kernel_name = 'mk_metaformer_d1_conv_nchw128_1ccf2a'

def setup_inputs(seed: int = 0):
    np.random.seed(seed)
    _w = jnp.asarray
    def _rec_inputs():
        import jax
        import jax.numpy as jnp
        _gk = jax.random.key(seed)
        x = -0.0005153 + 1.001 * jax.random.normal(jax.random.fold_in(_gk, 1), (8, 128, 56, 56), jnp.float32)
        return x
    x = _rec_inputs()
    def _L0_conv_setup():
        import jax, jax.numpy as jnp
        import numpy as np
        NW = 7
        HEADS = 8
        QK = 128
        DIM = 128
        TOPK = 4
        SCALE = QK ** (-0.5)

        def _forward(x, W_qkv, b_qkv, lepe_w, lepe_b, W_o, b_o):
            N, C, H, W = x.shape
            hh, ww = (H // NW, W // NW)
            p2, w2 = (NW * NW, hh * ww)
            hd = DIM // HEADS
            xh = x.transpose(0, 2, 3, 1)
            xw = xh.reshape(N, NW, hh, NW, ww, C).transpose(0, 1, 3, 2, 4, 5)
            xw = xw.reshape(N, p2, hh, ww, C)
            proj = xw @ W_qkv + b_qkv
            q = proj[..., :QK]
            kv = proj[..., QK:]
            q_pix = q.reshape(N, p2, w2, QK)
            kv_pix = kv.reshape(N, p2, w2, QK + DIM)
            q_win = jax.lax.stop_gradient(q.mean((2, 3)))
            k_win = jax.lax.stop_gradient(kv[..., :QK].mean((2, 3)))
            v_img = kv[..., QK:].reshape(N, NW, NW, hh, ww, C)
            v_img = v_img.transpose(0, 5, 1, 3, 2, 4).reshape(N, C, H, W)
            lepe = jax.lax.conv_general_dilated(v_img, lepe_w, window_strides=(1, 1), padding='SAME', feature_group_count=C, dimension_numbers=('NCHW', 'OIHW', 'NCHW')) + lepe_b[None, :, None, None]
            lepe = lepe.transpose(0, 2, 3, 1)
            logit = jnp.einsum('npc,nqc->npq', q_win * SCALE, k_win)
            topk_logit, r_idx = jax.lax.top_k(logit, TOPK)
            r_weight = jax.nn.softmax(topk_logit, axis=-1)
            kv_sel = jax.vmap(lambda kvn, idx: kvn[idx])(kv_pix, r_idx)
            k_sel = kv_sel[..., :QK].reshape(N * p2, TOPK * w2, HEADS, hd).transpose(0, 2, 1, 3)
            v_sel = kv_sel[..., QK:].reshape(N * p2, TOPK * w2, HEADS, hd).transpose(0, 2, 1, 3)
            q_h = q_pix.reshape(N * p2, w2, HEADS, hd).transpose(0, 2, 1, 3)
            attn = jax.nn.softmax(jnp.einsum('bmqc,bmkc->bmqk', q_h * SCALE, k_sel), axis=-1)
            o = jnp.einsum('bmqk,bmkc->bmqc', attn, v_sel)
            o = o.transpose(0, 2, 1, 3).reshape(N, NW, NW, hh, ww, C)
            o = o.transpose(0, 1, 3, 2, 4, 5).reshape(N, H, W, C)
            out = (o + lepe) @ W_o + b_o
            return out.transpose(0, 3, 1, 2)
        key = jax.random.key(seed)
        ks = jax.random.split(key, 8)
        N, C, H, W = (8, DIM, 56, 56)
        x = jax.random.normal(ks[0], (N, C, H, W), dtype=jnp.float32)
        W_qkv = jax.random.normal(ks[1], (DIM, 2 * QK + DIM), dtype=jnp.float32) * DIM ** (-0.5)
        b_qkv = jnp.zeros((2 * QK + DIM,), dtype=jnp.float32)
        lepe_w = jax.random.normal(ks[2], (DIM, 1, 3, 3), dtype=jnp.float32) * 0.1
        lepe_b = jnp.zeros((DIM,), dtype=jnp.float32)
        W_o = jax.random.normal(ks[3], (DIM, DIM), dtype=jnp.float32) * DIM ** (-0.5)
        b_o = jnp.zeros((DIM,), dtype=jnp.float32)
        return {'x': x, 'W_qkv': W_qkv, 'b_qkv': b_qkv, 'lepe_w': lepe_w, 'lepe_b': lepe_b, 'W_o': W_o, 'b_o': b_o}
    _L0_conv_all = _L0_conv_setup()
    _L0_conv_in = {k: v for k, v in _L0_conv_all.items() if k in ('W_qkv', 'b_qkv', 'lepe_w', 'lepe_b', 'W_o', 'b_o', )}
    del _L0_conv_all

    def _L0_ffn_setup():
        import jax, jax.numpy as jnp
        import numpy as np
        PADDED_SL = 8192
        TEMPERATURE = 1.0
        SIGMA_POW = 0.25

        def _stu_conv(phi, u, n):
            b, sl, d = u.shape
            sgn = jnp.where(jnp.arange(sl) % 2 == 0, 1.0, -1.0).astype(u.dtype)
            sgn3 = sgn[None, :, None]
            Vf = jnp.fft.rfft(phi, n=n, axis=0)
            Uf_p = jnp.fft.rfft(u, n=n, axis=1)
            Uf_m = jnp.fft.rfft(u * sgn3, n=n, axis=1)
            U_plus = jnp.fft.irfft(Vf[None, :, :, None] * Uf_p[:, :, None, :], n=n, axis=1)[:, :sl]
            U_minus = jnp.fft.irfft(Vf[None, :, :, None] * Uf_m[:, :, None, :], n=n, axis=1)[:, :sl]
            U_minus = U_minus * sgn[None, :, None, None]
            return (U_plus, U_minus)

        def _compute_spectral(u, sigma, phi, Mpp, Mpm):
            U_plus, U_minus = _stu_conv(phi, u, PADDED_SL)
            s = sigma ** SIGMA_POW
            out = jnp.einsum('btkd,k,kde->bte', U_plus, s, Mpp)
            out = out + jnp.einsum('btkd,k,kde->bte', U_minus, s, Mpm)
            return out

        def _compute_ar_u(Mu, u):
            sl = u.shape[1]
            out = jnp.zeros(u.shape[:2] + (Mu.shape[-1],), dtype=u.dtype)
            for i in range(Mu.shape[0]):
                ui = jnp.pad(u, ((0, 0), (i, 0), (0, 0)))[:, :sl]
                out = out + jnp.einsum('btd,de->bte', ui, Mu[i])
            return out

        def _stu(u, sigma, phi, Mu, Mpp, Mpm):
            return _compute_spectral(u, sigma, phi, Mpp, Mpm) + _compute_ar_u(Mu, u)
        key = jax.random.key(seed)
        ks = jax.random.split(key, 8)
        b, sl, d, K, k_u = (2, 4096, 128, 16, 3)
        x = jax.random.normal(ks[0], (b, sl, d), dtype=jnp.float32)
        sigma = jax.random.uniform(ks[1], (K,), dtype=jnp.float32, minval=0.001, maxval=1.0)
        phi = jax.random.normal(ks[2], (sl, K), dtype=jnp.float32) / np.sqrt(sl)
        M_u = jax.random.normal(ks[3], (4, k_u, d, d), dtype=jnp.float32) * 0.02
        M_phi_plus = jax.random.normal(ks[4], (4, K, d, d), dtype=jnp.float32) * 0.02
        M_phi_minus = jax.random.normal(ks[5], (4, K, d, d), dtype=jnp.float32) * 0.02
        log_weights = jnp.ones((4,), dtype=jnp.float32)
        u01 = jax.random.uniform(ks[6], (4,), dtype=jnp.float32, minval=1e-06, maxval=1.0 - 1e-06)
        gumbel = -jnp.log(-jnp.log(u01))
        return {'x': x, 'sigma': sigma, 'phi': phi, 'M_u': M_u, 'M_phi_plus': M_phi_plus, 'M_phi_minus': M_phi_minus, 'log_weights': log_weights, 'gumbel': gumbel}
    _L0_ffn_all = _L0_ffn_setup()
    _L0_ffn_in = {k: v for k, v in _L0_ffn_all.items() if k in ('sigma', 'phi', 'M_u', 'M_phi_plus', 'M_phi_minus', 'log_weights', 'gumbel', )}
    del _L0_ffn_all

    return {
        "x": x,
        "L0_conv_W_qkv": _L0_conv_in["W_qkv"],
        "L0_conv_b_qkv": _L0_conv_in["b_qkv"],
        "L0_conv_lepe_w": _L0_conv_in["lepe_w"],
        "L0_conv_lepe_b": _L0_conv_in["lepe_b"],
        "L0_conv_W_o": _L0_conv_in["W_o"],
        "L0_conv_b_o": _L0_conv_in["b_o"],
        "L0_ffn_sigma": _L0_ffn_in["sigma"],
        "L0_ffn_phi": _L0_ffn_in["phi"],
        "L0_ffn_M_u": _L0_ffn_in["M_u"],
        "L0_ffn_M_phi_plus": _L0_ffn_in["M_phi_plus"],
        "L0_ffn_M_phi_minus": _L0_ffn_in["M_phi_minus"],
        "L0_ffn_log_weights": _L0_ffn_in["log_weights"],
        "L0_ffn_gumbel": _L0_ffn_in["gumbel"],
    }

def reference(x, L0_conv_W_qkv, L0_conv_b_qkv, L0_conv_lepe_w, L0_conv_lepe_b, L0_conv_W_o, L0_conv_b_o, L0_ffn_sigma, L0_ffn_phi, L0_ffn_M_u, L0_ffn_M_phi_plus, L0_ffn_M_phi_minus, L0_ffn_log_weights, L0_ffn_gumbel):
    import jax
    import jax.numpy as jnp
    def _L0_conv_ref(x, W_qkv, b_qkv, lepe_w, lepe_b, W_o, b_o):
        import jax, jax.numpy as jnp
        import numpy as np
        NW = 7
        HEADS = 8
        QK = 128
        DIM = 128
        TOPK = 4
        SCALE = QK ** (-0.5)

        def _forward(x, W_qkv, b_qkv, lepe_w, lepe_b, W_o, b_o):
            N, C, H, W = x.shape
            hh, ww = (H // NW, W // NW)
            p2, w2 = (NW * NW, hh * ww)
            hd = DIM // HEADS
            xh = x.transpose(0, 2, 3, 1)
            xw = xh.reshape(N, NW, hh, NW, ww, C).transpose(0, 1, 3, 2, 4, 5)
            xw = xw.reshape(N, p2, hh, ww, C)
            proj = xw @ W_qkv + b_qkv
            q = proj[..., :QK]
            kv = proj[..., QK:]
            q_pix = q.reshape(N, p2, w2, QK)
            kv_pix = kv.reshape(N, p2, w2, QK + DIM)
            q_win = jax.lax.stop_gradient(q.mean((2, 3)))
            k_win = jax.lax.stop_gradient(kv[..., :QK].mean((2, 3)))
            v_img = kv[..., QK:].reshape(N, NW, NW, hh, ww, C)
            v_img = v_img.transpose(0, 5, 1, 3, 2, 4).reshape(N, C, H, W)
            lepe = jax.lax.conv_general_dilated(v_img, lepe_w, window_strides=(1, 1), padding='SAME', feature_group_count=C, dimension_numbers=('NCHW', 'OIHW', 'NCHW')) + lepe_b[None, :, None, None]
            lepe = lepe.transpose(0, 2, 3, 1)
            logit = jnp.einsum('npc,nqc->npq', q_win * SCALE, k_win)
            topk_logit, r_idx = jax.lax.top_k(logit, TOPK)
            r_weight = jax.nn.softmax(topk_logit, axis=-1)
            kv_sel = jax.vmap(lambda kvn, idx: kvn[idx])(kv_pix, r_idx)
            k_sel = kv_sel[..., :QK].reshape(N * p2, TOPK * w2, HEADS, hd).transpose(0, 2, 1, 3)
            v_sel = kv_sel[..., QK:].reshape(N * p2, TOPK * w2, HEADS, hd).transpose(0, 2, 1, 3)
            q_h = q_pix.reshape(N * p2, w2, HEADS, hd).transpose(0, 2, 1, 3)
            attn = jax.nn.softmax(jnp.einsum('bmqc,bmkc->bmqk', q_h * SCALE, k_sel), axis=-1)
            o = jnp.einsum('bmqk,bmkc->bmqc', attn, v_sel)
            o = o.transpose(0, 2, 1, 3).reshape(N, NW, NW, hh, ww, C)
            o = o.transpose(0, 1, 3, 2, 4, 5).reshape(N, H, W, C)
            out = (o + lepe) @ W_o + b_o
            return out.transpose(0, 3, 1, 2)
        return _forward(x, W_qkv, b_qkv, lepe_w, lepe_b, W_o, b_o)

    def _L0_ffn_ref(x, sigma, phi, M_u, M_phi_plus, M_phi_minus, log_weights, gumbel):
        import jax, jax.numpy as jnp
        import numpy as np
        PADDED_SL = 8192
        TEMPERATURE = 1.0
        SIGMA_POW = 0.25

        def _stu_conv(phi, u, n):
            b, sl, d = u.shape
            sgn = jnp.where(jnp.arange(sl) % 2 == 0, 1.0, -1.0).astype(u.dtype)
            sgn3 = sgn[None, :, None]
            Vf = jnp.fft.rfft(phi, n=n, axis=0)
            Uf_p = jnp.fft.rfft(u, n=n, axis=1)
            Uf_m = jnp.fft.rfft(u * sgn3, n=n, axis=1)
            U_plus = jnp.fft.irfft(Vf[None, :, :, None] * Uf_p[:, :, None, :], n=n, axis=1)[:, :sl]
            U_minus = jnp.fft.irfft(Vf[None, :, :, None] * Uf_m[:, :, None, :], n=n, axis=1)[:, :sl]
            U_minus = U_minus * sgn[None, :, None, None]
            return (U_plus, U_minus)

        def _compute_spectral(u, sigma, phi, Mpp, Mpm):
            U_plus, U_minus = _stu_conv(phi, u, PADDED_SL)
            s = sigma ** SIGMA_POW
            out = jnp.einsum('btkd,k,kde->bte', U_plus, s, Mpp)
            out = out + jnp.einsum('btkd,k,kde->bte', U_minus, s, Mpm)
            return out

        def _compute_ar_u(Mu, u):
            sl = u.shape[1]
            out = jnp.zeros(u.shape[:2] + (Mu.shape[-1],), dtype=u.dtype)
            for i in range(Mu.shape[0]):
                ui = jnp.pad(u, ((0, 0), (i, 0), (0, 0)))[:, :sl]
                out = out + jnp.einsum('btd,de->bte', ui, Mu[i])
            return out

        def _stu(u, sigma, phi, Mu, Mpp, Mpm):
            return _compute_spectral(u, sigma, phi, Mpp, Mpm) + _compute_ar_u(Mu, u)
        T = x.shape[1]
        outs = []
        for i, frac in enumerate((1, 2, 4, 8)):
            xi = x[:, :T // frac]
            si = _stu(xi, sigma, phi, M_u[i], M_phi_plus[i], M_phi_minus[i])
            si = jnp.pad(si, ((0, 0), (0, T - si.shape[1]), (0, 0)))
            outs.append(si)
        y_soft = jax.nn.softmax((log_weights + gumbel) / TEMPERATURE)
        y_hard = jax.nn.one_hot(jnp.argmax(y_soft), 4, dtype=y_soft.dtype)
        weights = y_hard - jax.lax.stop_gradient(y_soft) + y_soft
        stacked = jnp.stack(outs, axis=-1)
        return jnp.sum(stacked * weights, axis=-1)

    def _gn(v, G=32, eps=1e-5):
        B_, C_, H_, W_ = v.shape
        g = v.reshape(B_, G, C_ // G, H_, W_)
        m = jnp.mean(g, axis=(2, 3, 4), keepdims=True)
        s = jnp.var(g, axis=(2, 3, 4), keepdims=True)
        return ((g - m) / jnp.sqrt(s + eps)).reshape(v.shape)

    def _ln_c(v, eps=1e-6):
        m = jnp.mean(v, axis=1, keepdims=True)
        s = jnp.var(v, axis=1, keepdims=True)
        return (v - m) / jnp.sqrt(s + eps)

    def _ln_t(v, eps=1e-5):
        m = jnp.mean(v, axis=-1, keepdims=True)
        s = jnp.var(v, axis=-1, keepdims=True)
        return (v - m) / jnp.sqrt(s + eps)

    def _to_tokens(v):
        B_, C_, H_, W_ = v.shape
        return v.reshape(B_, C_, H_ * W_).transpose(0, 2, 1)
    def _from_tokens(t, like):
        B_, C_, H_, W_ = like.shape
        return t.transpose(0, 2, 1).reshape(B_, C_, H_, W_)

    x = x + _L0_conv_ref(_ln_c(x), L0_conv_W_qkv, L0_conv_b_qkv, L0_conv_lepe_w, L0_conv_lepe_b, L0_conv_W_o, L0_conv_b_o)
    t = _to_tokens(x)
    t = t + _L0_ffn_ref(_ln_t(t), L0_ffn_sigma, L0_ffn_phi, L0_ffn_M_u, L0_ffn_M_phi_plus, L0_ffn_M_phi_minus, L0_ffn_log_weights, L0_ffn_gumbel)
    x = _from_tokens(t, x)
    return x


_drawn_inputs = setup_inputs


def setup_inputs(seed=0):
    import zlib

    import numpy as np

    out = dict(_drawn_inputs(seed))
    spreads = {'L0_conv_b_qkv': (0.0, 0.1),
     'L0_conv_lepe_b': (0.0, 0.1),
     'L0_conv_b_o': (0.0, 0.1),
     'L0_ffn_log_weights': (1.0, 0.2)}
    factors = {}
    for name, (base, spread) in spreads.items():
        noise = np.random.default_rng([zlib.crc32(name.encode()), seed]).standard_normal(out[name].shape)
        drawn = base * np.exp(spread * noise) if base else spread * noise
        out[name] = jnp.asarray(drawn.astype(out[name].dtype))
    for name, factor in factors.items():
        out[name] = (out[name] * factor).astype(out[name].dtype)
    return out
```

```python
from contextlib import ExitStack

import concourse.bass as bass
import numpy as np
from concourse import mybir

F32 = mybir.dt.float32
BF16 = mybir.dt.bfloat16
U32 = mybir.dt.uint32
ALU = mybir.AluOpType
ACT = mybir.ActivationFunctionType
AX = mybir.AxisListType

NIMG, C, HW = 8, 128, 56
T = HW * HW
NW = 7
WS = HW // NW
NWIN, WT = NW * NW, WS * WS
ROW = NW * WT
TOPK, HEADS, HD = 4, 8, 16
NHP = HEADS // 2
SCALE = float(C) ** -0.5
EPS_C, EPS_T = 1e-6, 1e-5

R = 8
N1 = T // R
NF2 = 2 * N1
NT, N1T = 4, N1 // 4
FT, NFT = 100, 4
NF = FT * NFT
FC = 8
NCH = NF // FC
KF, COPIES = 19, 6
KP = KF * COPIES
RX = 2 * R - 1

FREE = 1
BUF = [0, 1, 0, 1, 0, 1, 2]


def constants():
    c = {}
    c["ident"] = np.eye(C, dtype=np.float32)
    c["mean_mat"] = np.full((C, C), 1.0 / C, np.float32)
    c["head_parity"] = np.stack([(np.arange(C) // HD) % 2 == h for h in range(2)], 1).astype(np.float32)
    n, f = np.arange(N1), np.arange(NF)
    live = (f <= NF2 // 2)
    ang = 2 * np.pi * ((n[:, None] * f[None]) % NF2) / NF2
    fwd = np.stack([np.cos(ang), -np.sin(ang)], 1) * live
    c["dft"] = fwd.reshape(NT, N1T, 2, NF).transpose(1, 0, 2, 3).reshape(N1T, NT * 2 * NF).astype(np.float32)
    amp = np.where((f == 0) | (f == NF2 // 2), 1.0, 2.0) * live / NF2
    inv = np.stack([np.cos(ang.T), -np.sin(ang.T)], 1) * amp[:, None, None]
    c["idft"] = inv.reshape(NFT, FT, 2, N1).transpose(1, 0, 2, 3).reshape(FT, NFT * 2 * N1).astype(np.float32)
    th = 2 * np.pi * f / NF2
    c["twist"] = np.broadcast_to(np.stack([np.cos(th), np.sin(th)]).astype(np.float32)[None], (C, 2, NF)).reshape(C, 2 * NF).copy()
    delta = np.zeros((N1T, NT, R, 3), np.float32)
    for j in range(3):
        delta[0, 0, j, j] = 1.0
    c["delta"] = delta.reshape(N1T, NT * R * 3)
    lvl_v, lvl_m = [0, 0, 0, 1, 1, 2], [0, 1, 2, 0, 1, 0]
    part = np.zeros((KP, 4), np.float32)
    for cpy in range(COPIES):
        rows = slice(cpy * KF, (cpy + 1) * KF)
        part[rows, 0] = -1.0 if lvl_v[cpy] >= 1 else 0.0
        part[rows, 1] = -1.0 if lvl_v[cpy] == 2 else 0.0
        part[rows, 2] = -1.0 if lvl_m[cpy] >= 1 else 0.0
        part[rows, 3] = -1.0 if lvl_m[cpy] == 2 else 0.0
    c["part"] = part
    sel = np.zeros((128, 2, COPIES, KF), np.float32)
    for s in range(2):
        for i in range(4):
            for k in range(16):
                sel[s * 64 + i * 16 + k, 0, :, k] = 1.0
                sel[s * 64 + i * 16 + k, 1, :, k] = 1.0 if s == 0 else -1.0
    c["sel"] = sel.reshape(128, 2 * KP)
    selu = np.zeros((12, COPIES, KF), np.float32)
    for i in range(4):
        for j in range(3):
            selu[i * 3 + j, :, 16 + j] = 1.0
    c["sel_u"] = selu.reshape(12, KP)
    own = np.zeros((128, 8), np.float32)
    for p in range(128):
        own[p, (p // 16) % 4] = 1.0
    for p in range(12):
        own[p, 4 + p // 3] = 1.0
    c["own_variant"] = own
    return c


def attention_and_dft(nc, x_d, wqkv_d, bqkv_d, lepe_w_d, lepe_b_d, wo_d, bo_d, cst, x2_d, spec_d, route_d):
    with ExitStack() as ctx:
        def sb(name, shape, dt=F32):
            return ctx.enter_context(nc.sbuf_tensor(name, shape, dt))

        def sem(name):
            return ctx.enter_context(nc.semaphore(name))

        xs = sb("xs", [C, T])
        xn = sb("xn", [C, T])
        xc = sb("xc", [C, 2, ROW])
        sq = sb("sq", [C, 2, ROW])
        std = sb("std", [C, 2, ROW])
        rstd = sb("rstd", [C, 2, ROW])
        qT = sb("qT", [C, T])
        kT = sb("kT", [C, T])
        vpad = sb("vpad", [C, HW + 2, HW + 2])
        vtok = sb("vtok", [WT, NWIN, C])
        oT = sb("oT", [C, T])
        utok = sb("utok", [N1T, NT, R, C])
        wqkv = sb("wqkv", [C, 3 * C])
        wo = sb("wo", [C, C])
        bq, bk, bv, bo, lb = (sb(n, [C, 1]) for n in ("bq", "bk", "bv", "bo", "lb"))
        bqs = sb("bqs", [C, 1])
        bvrow = sb("bvrow", [C, C])
        lw = sb("lw", [C, 9])
        ident = sb("ident", [C, C])
        mean_mat = sb("mean_mat", [C, C])
        hpar = sb("hpar", [C, 2])
        epsc = sb("epsc", [C, 2])
        dft = sb("dft", [N1T, NT, 2, NF])
        qsum = sb("qsum", [C, NWIN])
        ksum = sb("ksum", [C, NWIN])
        logit = sb("logit", [NWIN, NWIN])
        top = sb("top", [NWIN, 8])
        topi = sb("topi", [NWIN, 8], U32)
        route = sb("route", [1, NWIN * TOPK], U32)
        ksel = sb("ksel", [C, 3, TOPK * WT])
        vsel = sb("vsel", [C, 3, 2, C])
        qz = sb("qz", [C, 3, 2, WT])
        nmax = sb("nmax", [C, 3, NHP])
        rsum = sb("rsum", [C, 3, NHP])
        rinv = sb("rinv", [C, 3, NHP])
        prob = sb("prob", [C, 3, NHP, TOPK * WT])
        probT = sb("probT", [C, 2, 2, 2, C])
        otok = sb("otok", [WT, C])
        ustage = sb("ustage", [FT, 2, R * C])
        ps = ctx.enter_context(nc.psum_tensor("ps", [C, 8, 512], F32))

        consts_loaded, x_loaded, ready0, x2_stored = map(sem, ("consts_loaded", "x_loaded", "ready0", "x2_stored"))
        mean_ready, centered, squared, var_ready, std_ready, recip_done, normed = map(
            sem, ("mean_ready", "centered", "squared", "var_ready", "std_ready", "recip_done", "normed"))
        qkv_ready, q_done, k_done, v_done, vt_done, sums_done = map(
            sem, ("qkv_ready", "q_done", "k_done", "v_done", "vt_done", "sums_done"))
        logit_ready, topk_step, route_stored, route_loaded = map(
            sem, ("logit_ready", "topk_step", "route_stored", "route_loaded"))
        gathered, s_ready, max_done, exp_done, t_ready, t_evac0, t_evac1 = map(
            sem, ("gathered", "s_ready", "max_done", "exp_done", "t_ready", "t_evac0", "t_evac1"))
        pv_done, rinv_done, o_evac, ot_ready, ot_evac, lepe_done = map(
            sem, ("pv_done", "rinv_done", "o_evac", "ot_ready", "ot_evac", "lepe_done"))
        proj_ready, x2_ready, tr_ready, ut_evac0, ut_evac1 = map(
            sem, ("proj_ready", "x2_ready", "tr_ready", "ut_evac0", "ut_evac1"))
        dft_ready, u_evac0, u_evac1 = map(sem, ("dft_ready", "u_evac0", "u_evac1"))
        passed = sem("passed")
        v_gathered = [sem(f"v_gathered{u}") for u in range(3)]
        u_stored = [sem("u_stored0"), sem("u_stored1")]

        NCONST = 17

        def values_there(b, g, i):
            row = NW * b + g
            return 64 * (row + 1) if BUF[i] == 2 else 64 * (3 * row + i // 2 + 1)

        def image(v, k):
            return v[:, k * ROW:(k + 1) * ROW]

        def by_window(v):
            return v.rearrange("p (y n x) -> p n y x", y=WS, n=NW)

        def by_image(v):
            return v.rearrange("p (n y x) -> p y n x", y=WS, n=NW)

        def alone(eng):
            eng.sem_inc(passed, 1)

        with nc.Block() as block:
            @block.sync
            def _(sp):
                for s in (x2_stored, route_stored, *u_stored):
                    sp.sem_inc(s, 16 * FREE)
                loads = [
                    (wqkv[:], wqkv_d), (wo[:], wo_d),
                    (bq[:], bqkv_d[0:C].unsqueeze(1)), (bk[:], bqkv_d[C:2 * C].unsqueeze(1)),
                    (bv[:], bqkv_d[2 * C:3 * C].unsqueeze(1)), (bo[:], bo_d.unsqueeze(1)),
                    (lb[:], lepe_b_d.unsqueeze(1)), (lw[:], lepe_w_d),
                    (bvrow[:], bqkv_d[2 * C:3 * C].partition_broadcast(C)),
                    (ident[:], cst["ident"]), (mean_mat[:], cst["mean_mat"]), (hpar[:], cst["head_parity"]),
                    (dft[:].rearrange("p a b c -> p (a b c)"), cst["dft"]),
                ]
                for dst, src in loads:
                    sp.dma_start(dst, src).then_inc(consts_loaded, 16)
                assert len(loads) == 13

                def gather_values(b, w, i):
                    sp.wait_ge(pv_done, NWIN * b + w + 1)
                    for j in range(TOPK):
                        n = sp.value_load(route[0:1, bass.ds(w * TOPK + j, 1)], min_val=0, max_val=NWIN - 1)
                        sp.dma_start(vsel[(j % 2) * WT:(j % 2 + 1) * WT, BUF[i], j // 2, :],
                                     vtok[:, bass.ds(n, 1), :].rearrange("p a c -> p (a c)")).then_inc(v_gathered[BUF[i]], 16)

                with sp.Fori(0, NIMG) as b:
                    sp.wait_ge(normed, 14 * b + FREE)
                    alone(sp)
                    sp.wait_ge(x2_stored, 16 * b + 16 * FREE)
                    sp.dma_start(xs[:], x_d[bass.ds(b, 1)].rearrange("a c t -> (a c) t")).then_inc(x_loaded, 16)
                    sp.wait_ge(topk_step, 3 * b + 3)
                    sp.dma_start(route_d[bass.ds(b, 1)].rearrange("a (w j) -> (a w) j", j=TOPK), topi[:, 0:TOPK]).then_inc(route_stored, 16)
                    sp.wait_ge(route_stored, 16 * b + 16 + 16 * FREE)
                    sp.dma_start(route[:], route_d[bass.ds(b, 1)]).then_inc(route_loaded, 16)
                    sp.wait_ge(route_loaded, 16 * b + 16)
                    alone(sp)
                    sp.wait_ge(vt_done, 14 * b + 14)
                    alone(sp)
                    with sp.Fori(0, NW) as g:
                        for i in range(NW):
                            gather_values(b, g * NW + i, i)
                    sp.wait_ge(x2_ready, 7 * b + 7)
                    sp.dma_start(x2_d[bass.ds(b, 1)].rearrange("a c t -> (a c) t"), xs[:]).then_inc(x2_stored, 16)
                    for s in range(2 * NFT):
                        ft, c = s // 2, s % 2
                        sp.wait_ge(u_evac0, 8 * b + s + 1 + FREE)
                        sp.wait_ge(u_evac1, 8 * b + s + 1 + FREE)
                        sp.dma_start(spec_d[ft * FT:(ft + 1) * FT, c, bass.ds(b, 1), :].rearrange("f a n -> f (a n)"),
                                     ustage[:, s % 2, :]).then_inc(u_stored[s % 2], 16)
                sp.wait_ge(x2_stored, 16 * NIMG + 16 * FREE)
                for s in range(2):
                    sp.wait_ge(u_stored[s], 16 * NFT * NIMG + 16 * FREE)

            @block.gpsimd
            def _(pool):
                nc.gpsimd.memset(vpad[:], 0.0).then_inc(ready0, 1)
                nc.gpsimd.memset(epsc[:, 0:1], EPS_C).then_inc(ready0, 1)
                nc.gpsimd.memset(epsc[:, 1:2], EPS_T).then_inc(ready0, 1)
                pool.wait_ge(consts_loaded, 16 * 13)

                def gather(b, w, i):
                    u = BUF[i]
                    gw = NWIN * b + w
                    pool.wait_ge(pv_done, gw + 1)
                    for h in range(2):
                        nc.gpsimd.tensor_tensor(qz[:, u, h, :], qT[:, bass.ds(w * WT, WT)],
                                                hpar[:, h:h + 1].to_broadcast([C, WT]), ALU.mult)
                    for j in range(TOPK):
                        n = pool.value_load(route[0:1, bass.ds(w * TOPK + j, 1)], min_val=0, max_val=NWIN - 1)
                        last = nc.gpsimd.tensor_copy(ksel[:, u, j * WT:(j + 1) * WT], kT[:, bass.ds(n * WT, WT)])
                    last.then_inc(gathered, 1)

                with pool.Fori(0, NIMG) as b:
                    pool.wait_ge(route_loaded, 16 * b + 16)
                    pool.wait_ge(q_done, 7 * b + 7)
                    pool.wait_ge(sums_done, 14 * b + 14)
                    alone(pool)
                    with pool.Fori(0, NW) as g:
                        for i in range(NW):
                            gather(b, g * NW + i, i)

            @block.tensor
            def _(pe):
                pe.sem_inc(pv_done, 2)
                pe.sem_inc(ot_ready, FREE)
                pe.wait_ge(consts_loaded, 16 * 13)

                def layer_norm(b, which):
                    for k in range(NW + 1):
                        if k < NW:
                            n = 14 * b + 7 * which + k
                            if which:
                                pe.wait_ge(x2_ready, 7 * b + k + 1)
                            if k >= 2:
                                pe.wait_ge(centered, n - 1)
                            nc.tensor.matmul(ps[:, k % 2, 0:ROW], mean_mat[:], image(xs, k),
                                             start=True, stop=True).then_inc(mean_ready, 1)
                        if k >= 1:
                            m, j = 14 * b + 7 * which + k - 1, k - 1
                            pe.wait_ge(squared, m + 1)
                            if j >= 2:
                                pe.wait_ge(std_ready, m - 1)
                            nc.tensor.matmul(ps[:, 2 + j % 2, 0:ROW], mean_mat[:], sq[:, j % 2, :],
                                             start=True, stop=True).then_inc(var_ready, 1)

                def scores(b, w, i, hps):
                    u, gw = BUF[i], NWIN * b + w
                    pe.wait_ge(gathered, gw + 1)
                    for hp in hps:
                        pe.wait_ge(exp_done, 4 * gw + hp - 3 + 4)
                        rows = slice(32 * hp, 32 * hp + 32)
                        nc.tensor.matmul(ps[:, hp, 0:TOPK * WT], qz[rows, u, :, :], ksel[rows, u, :],
                                         start=True, stop=True).then_inc(s_ready, 1)

                def transposes(b, w, i, a):
                    u, gw = BUF[i], NWIN * b + w
                    pe.wait_ge(exp_done, 4 * gw + 2 * a + 2 + 4)
                    if a == 0:
                        pe.wait_ge(t_evac0, gw + FREE)
                    else:
                        pe.wait_ge(t_evac1, gw + FREE)
                    for h in range(2):
                        for kt in range(2):
                            last = nc.tensor.transpose(ps[:, 4 + a, (2 * h + kt) * C:(2 * h + kt + 1) * C],
                                                       prob[:, u, 2 * a + h, kt * C:(kt + 1) * C], ident[:])
                    last.then_inc(t_ready, 1)

                def out_transpose(b, w):
                    gw = NWIN * b + w
                    pe.wait_ge(o_evac, gw + 1 + FREE)
                    pe.wait_ge(ot_evac, gw + FREE)
                    nc.tensor.matmul(ps[:, 7, 0:WT], otok[:], ident[0:WT, 0:WT], start=True, stop=True).then_inc(ot_ready, 1)

                def values(b, g, i):
                    u, gw = BUF[i], NWIN * b + NW * g + i
                    pe.wait_ge(v_gathered[u], values_there(b, g, i))
                    pe.wait_ge(o_evac, gw + FREE)
                    for hp in range(NHP):
                        if hp == 0:
                            pe.wait_ge(t_evac0, gw + 1 + FREE)
                        if hp == 2:
                            pe.wait_ge(t_evac1, gw + 1 + FREE)
                        for kt in range(2):
                            last = nc.tensor.matmul(ps[:, 6, 32 * hp:32 * hp + 32], probT[:, hp // 2, hp % 2, kt, :],
                                                    vsel[:, u, kt, 32 * hp:32 * hp + 32], start=(kt == 0), stop=(kt == 1))
                    last.then_inc(pv_done, 1)

                def window_row(b, g, final):
                    for i in range(NW):
                        w = g * NW + i
                        more = not (final and i == NW - 1)
                        if more:
                            scores(b, w + 1, (i + 1) % NW, (0, 1))
                        transposes(b, w, i, 0)
                        if more:
                            scores(b, w + 1, (i + 1) % NW, (2, 3))
                        transposes(b, w, i, 1)
                        if i > 0:
                            out_transpose(b, w - 1)
                        values(b, g, i)
                        if i == NW - 1:
                            out_transpose(b, w)

                with pe.Fori(0, NIMG) as b:
                    pe.wait_ge(x_loaded, 16 * b + 16)
                    pe.wait_ge(u_evac0, 8 * b + FREE)
                    pe.wait_ge(u_evac1, 8 * b + FREE)
                    layer_norm(b, 0)
                    for k in range(NW):
                        p = 4 * (k % 2)
                        xk = xn[:, k * ROW:(k + 1) * ROW]
                        if k == 0:
                            pe.wait_ge(normed, 14 * b + 7 + FREE)
                        if k >= 2:
                            pe.wait_ge(vt_done, 14 * b + 2 * k - 2)
                            pe.wait_ge(k_done, 7 * b + k - 1)
                            pe.wait_ge(v_done, 7 * b + k - 1)
                        nc.tensor.matmul(ps[:, p, 0:ROW], wqkv[:, 0:C], xk, start=True, stop=True).then_inc(qkv_ready, 1)
                        nc.tensor.matmul(ps[:, p + 1, 0:ROW], wqkv[:, C:2 * C], xk, start=True, stop=True).then_inc(qkv_ready, 1)
                        nc.tensor.matmul(ps[:, p + 2, 0:ROW], wqkv[:, 2 * C:], by_image(xk), start=True, stop=True).then_inc(qkv_ready, 1)
                        for part, (first, n, bank) in enumerate(((0, 4, p + 3), (4, 3, p))):
                            if part == 1:
                                pe.wait_ge(q_done, 7 * b + k + 1)
                            for i in range(n):
                                win = xk[:, (first + i) * WT:(first + i + 1) * WT]
                                last = nc.tensor.matmul(ps[0:WT, bank, i * C:(i + 1) * C], win, wqkv[:, 2 * C:],
                                                        start=True, stop=True)
                            last.then_inc(qkv_ready, 1)
                    pe.wait_ge(sums_done, 14 * b + 14)
                    pe.wait_ge(vt_done, 14 * b + 14)
                    pe.wait_ge(v_done, 7 * b + 7)
                    nc.tensor.matmul(ps[0:NWIN, 0, 0:NWIN], qsum[:], ksum[:], start=True, stop=True).then_inc(logit_ready, 1)
                    scores(b, 0, 0, (0, 1, 2, 3))
                    with pe.Fori(0, NW - 1) as g:
                        window_row(b, g, False)
                    window_row(b, NW - 1, True)
                    pe.wait_ge(lepe_done, 63 * b + 63)
                    pe.wait_ge(ot_evac, NWIN * b + NWIN + FREE)
                    for k in range(NW):
                        if k >= 2:
                            pe.wait_ge(x2_ready, 7 * b + k - 1)
                        nc.tensor.matmul(ps[:, 4 + k % 2, 0:ROW], wo[:], by_image(image(oT, k)), start=True, stop=False)
                        nc.tensor.matmul(ps[:, 4 + k % 2, 0:ROW], wo[:], image(xn, k), start=False, stop=True).then_inc(proj_ready, 1)
                    layer_norm(b, 1)
                    pe.wait_ge(normed, 14 * b + 14 + FREE)
                    for t in range(2 * NT):
                        nt, half = t // 2, t % 2
                        if t >= 4:
                            if t % 2 == 0:
                                pe.wait_ge(ut_evac0, 4 * b + t // 2 - 1)
                            else:
                                pe.wait_ge(ut_evac1, 4 * b + t // 2 - 1)
                        for r in range(4):
                            t0 = R * N1T * nt + 4 * half + r
                            src = xn[:, t0:t0 + R * (N1T - 1) + 1:R]
                            last = nc.tensor.transpose(ps[0:N1T, 4 + t % 4, r * C:(r + 1) * C], src, ident[:])
                        last.then_inc(tr_ready, 1)
                    pe.wait_ge(ut_evac0, 4 * b + 4)
                    pe.wait_ge(ut_evac1, 4 * b + 4)
                    for s in range(2 * NFT):
                        ft, c = s // 2, s % 2
                        for half in range(2):
                            q = 2 * s + half
                            if q >= 4:
                                if half == 0:
                                    pe.wait_ge(u_evac0, 8 * b + s - 1 + FREE)
                                else:
                                    pe.wait_ge(u_evac1, 8 * b + s - 1 + FREE)
                            for nt in range(NT):
                                last = nc.tensor.matmul(ps[0:FT, q % 4, :], dft[:, nt, c, ft * FT:(ft + 1) * FT],
                                                        utok[:, nt, 4 * half:4 * half + 4, :], start=(nt == 0), stop=(nt == NT - 1))
                            last.then_inc(dft_ready, 1)

            @block.scalar
            def _(act):
                act.wait_ge(consts_loaded, 16 * 13)
                act.wait_ge(ready0, 3)
                nc.scalar.mul(bqs[:], bq[:], SCALE).then_inc(ready0, 1)
                act.wait_ge(ready0, 4)
                act.sem_inc(exp_done, 4)
                for s in (u_evac1, t_evac1, ot_evac):
                    act.sem_inc(s, FREE)

                def layer_norm(b, which):
                    for k in range(NW + 1):
                        if k < NW:
                            n = 14 * b + 7 * which + k
                            act.wait_ge(centered, n + 1)
                            if k >= 2:
                                act.wait_ge(var_ready, n - 1)
                            nc.scalar.activation(sq[:, k % 2, :], xc[:, k % 2, :], ACT.Square).then_inc(squared, 1)
                        if k >= 1:
                            m, j = 14 * b + 7 * which + k - 1, k - 1
                            act.wait_ge(var_ready, m + 1)
                            if j >= 2:
                                act.wait_ge(recip_done, m - 1)
                            nc.scalar.activation(std[:, j % 2, :], ps[:, 2 + j % 2, 0:ROW], ACT.Sqrt,
                                                 bias=epsc[:, which:which + 1]).then_inc(std_ready, 1)

                def exps(b, w, i, hps):
                    u, gw = BUF[i], NWIN * b + w
                    for hp in hps:
                        act.wait_ge(max_done, 4 * gw + hp + 1)
                        nc.scalar.activation(prob[:, u, hp, :], ps[:, hp, 0:TOPK * WT], ACT.Exp,
                                             bias=nmax[:, u, hp:hp + 1], accum_out=rsum[:, u, hp:hp + 1]).then_inc(exp_done, 1)

                def out_copy(b, w):
                    gw = NWIN * b + w
                    act.wait_ge(ot_ready, gw + 1 + FREE)
                    nc.scalar.activation(oT[:, bass.ds(w * WT, WT)], ps[:, 7, 0:WT], ACT.Copy).then_inc(ot_evac, 1)

                def window_row(b, g, final):
                    for i in range(NW):
                        w = g * NW + i
                        gw = NWIN * b + w
                        more = not (final and i == NW - 1)
                        if more:
                            exps(b, w + 1, (i + 1) % NW, (0, 1))
                        act.wait_ge(t_ready, 2 * gw + 2)
                        act.wait_ge(pv_done, gw + 2)
                        nc.scalar.activation(probT[:, 1, :, :, :].rearrange("p a b c -> p (a b c)"), ps[:, 5, :], ACT.Copy).then_inc(t_evac1, 1)
                        if more:
                            exps(b, w + 1, (i + 1) % NW, (2, 3))
                        if i > 0:
                            out_copy(b, w - 1)
                        if i == NW - 1:
                            out_copy(b, w)

                with act.Fori(0, NIMG) as b:
                    layer_norm(b, 0)
                    for k in range(NW):
                        p = 4 * (k % 2)
                        act.wait_ge(qkv_ready, 35 * b + 5 * k + 1)
                        nc.scalar.activation(qT[:, k * ROW:(k + 1) * ROW], ps[:, p, 0:ROW], ACT.Identity,
                                             bias=bqs[:], scale=SCALE).then_inc(q_done, 1)
                        act.wait_ge(qkv_ready, 35 * b + 5 * k + 3)
                        nc.scalar.activation(vpad[:, 1 + k * WS:1 + (k + 1) * WS, 1:1 + HW],
                                             ps[:, p + 2, 0:ROW].rearrange("p (r c) -> p r c", r=WS), ACT.Identity,
                                             bias=bv[:]).then_inc(v_done, 1)
                    exps(b, 0, 0, (0, 1, 2, 3))
                    with act.Fori(0, NW - 1) as g:
                        window_row(b, g, False)
                    window_row(b, NW - 1, True)
                    layer_norm(b, 1)
                    for t in range(1, 2 * NT, 2):
                        act.wait_ge(tr_ready, 8 * b + t + 1)
                        nc.scalar.activation(utok[:, t // 2, 4:8, :].rearrange("p a b -> p (a b)"), ps[0:N1T, 4 + t % 4, :], ACT.Copy).then_inc(ut_evac1, 1)
                    for s in range(2 * NFT):
                        act.wait_ge(dft_ready, 16 * b + 2 * s + 2)
                        act.wait_ge(u_stored[s % 2], 16 * (4 * b + s // 2) + 16 * FREE)
                        nc.scalar.activation(ustage[:, s % 2, 512:1024], ps[0:FT, (2 * s + 1) % 4, :], ACT.Copy).then_inc(u_evac1, 1)

            @block.vector
            def _(dve):
                for s in (normed, u_evac0, t_evac0, o_evac):
                    dve.sem_inc(s, FREE)
                dve.wait_ge(consts_loaded, 16 * 13)
                dve.wait_ge(ready0, 4)

                def layer_norm(b, which):
                    for k in range(NW + 1):
                        if k < NW:
                            n = 14 * b + 7 * which + k
                            dve.wait_ge(mean_ready, n + 1)
                            if k >= 2:
                                dve.wait_ge(normed, n - 1 + FREE)
                            nc.vector.tensor_tensor(xc[:, k % 2, :], image(xs, k), ps[:, k % 2, 0:ROW], ALU.subtract).then_inc(centered, 1)
                        if k >= 1:
                            m, j = 14 * b + 7 * which + k - 1, k - 1
                            dve.wait_ge(std_ready, m + 1)
                            nc.vector.reciprocal(rstd[:, j % 2, :], std[:, j % 2, :]).then_inc(recip_done, 1)
                            dve.wait_ge(recip_done, m + 1)
                            dst = image(xn, j) if which else by_image(image(xn, j))
                            centre, scale = xc[:, j % 2, :], rstd[:, j % 2, :]
                            if not which:
                                centre, scale = (v.rearrange("p (y n x) -> p y n x", y=WS, n=NW) for v in (centre, scale))
                            nc.vector.tensor_tensor(dst, centre, scale, ALU.mult).then_inc(normed, 1)

                def maxima(b, w, i, hps):
                    u, gw = BUF[i], NWIN * b + w
                    for hp in hps:
                        dve.wait_ge(s_ready, 4 * gw + hp + 1)
                        nc.vector.tensor_reduce(nmax[:, u, hp:hp + 1], ps[:, hp, 0:TOPK * WT], AX.X, ALU.max,
                                                negate=True).then_inc(max_done, 1)

                def positional(b, g, taps):
                    acc = xn[:, bass.ds(g * ROW, ROW)].rearrange("p (r c) -> p r c", r=WS)
                    for tap in taps:
                        src = vpad[:, bass.ds(g * WS + tap // 3, WS), tap % 3:tap % 3 + HW]
                        n = 63 * b + 9 * g + tap
                        if tap == 0:
                            nc.vector.tensor_scalar(acc, src, lw[:, 0:1], lb[:], ALU.mult, ALU.add).then_inc(lepe_done, 1)
                        else:
                            dve.wait_ge(lepe_done, n)
                            nc.vector.scalar_tensor_tensor(acc, src, lw[:, tap:tap + 1], acc, ALU.mult, ALU.add).then_inc(lepe_done, 1)

                def window_row(b, g, final):
                    for i in range(NW):
                        w = g * NW + i
                        u, gw = BUF[i], NWIN * b + w
                        more = not (final and i == NW - 1)
                        if more:
                            maxima(b, w + 1, (i + 1) % NW, (0, 1))
                        dve.wait_ge(t_ready, 2 * gw + 1)
                        dve.wait_ge(pv_done, gw + 2)
                        nc.vector.tensor_copy(probT[:, 0, :, :, :].rearrange("p a b c -> p (a b c)"), ps[:, 4, :]).then_inc(t_evac0, 1)
                        if more:
                            maxima(b, w + 1, (i + 1) % NW, (2, 3))
                        dve.wait_ge(exp_done, 4 * gw + 4 + 4)
                        nc.vector.reciprocal(rinv[:, u, :], rsum[:, u, :]).then_inc(rinv_done, 1)
                        positional(b, g, ([0, 1], [2], [3], [4], [5], [6], [7, 8])[i])
                        dve.wait_ge(pv_done, gw + 3)
                        dve.wait_ge(rinv_done, gw + 1)
                        dve.wait_ge(ot_ready, gw + FREE)
                        for h in range(2):
                            rows = slice(h * WT, (h + 1) * WT)
                            last = nc.vector.tensor_tensor(
                                otok[:].rearrange("p (a h d) -> p a h d", a=NHP, h=2)[:, :, h, :],
                                ps[rows, 6, 0:C].rearrange("p (a h d) -> p a h d", a=NHP, h=2)[:, :, h, :],
                                rinv[rows, u, :].unsqueeze(2).to_broadcast([WT, NHP, HD]), ALU.mult)
                        last.then_inc(o_evac, 1)

                with dve.Fori(0, NIMG) as b:
                    layer_norm(b, 0)
                    for k in range(NW):
                        p = 4 * (k % 2)
                        dve.wait_ge(qkv_ready, 35 * b + 5 * k + 2)
                        kk = kT[:, k * ROW:(k + 1) * ROW]
                        nc.vector.tensor_scalar(kk, ps[:, p + 1, 0:ROW], bk[:], None, ALU.add).then_inc(k_done, 1)
                        for part, (first, n, bank) in enumerate(((0, 4, p + 3), (4, 3, p))):
                            dve.wait_ge(qkv_ready, 35 * b + 5 * k + 4 + part)
                            nc.vector.tensor_tensor(vtok[:, k * NW + first:k * NW + first + n, :],
                                                    ps[0:WT, bank, 0:n * C].rearrange("p (w c) -> p w c", w=n),
                                                    bvrow[0:WT, :].unsqueeze(1).to_broadcast([WT, n, C]), ALU.add).then_inc(vt_done, 1)
                        dve.wait_ge(k_done, 7 * b + k + 1)
                        nc.vector.tensor_reduce(ksum[:, k * NW:(k + 1) * NW], kk.rearrange("p (w t) -> p w t", w=NW), AX.X, ALU.add).then_inc(sums_done, 1)
                        dve.wait_ge(q_done, 7 * b + k + 1)
                        nc.vector.tensor_reduce(qsum[:, k * NW:(k + 1) * NW], qT[:, k * ROW:(k + 1) * ROW].rearrange("p (w t) -> p w t", w=NW),
                                                AX.X, ALU.add).then_inc(sums_done, 1)
                    dve.wait_ge(logit_ready, b + 1)
                    dve.wait_ge(route_stored, 16 * b + 16 * FREE)
                    nc.vector.tensor_copy(logit[:], ps[0:NWIN, 0, 0:NWIN]).then_inc(topk_step, 1)
                    dve.wait_ge(topk_step, 3 * b + 1)
                    alone(dve)
                    nc.vector.max(top[:], logit[:]).then_inc(topk_step, 1)
                    dve.wait_ge(topk_step, 3 * b + 2)
                    alone(dve)
                    nc.vector.max_index(topi[:], top[:], logit[:]).then_inc(topk_step, 1)
                    maxima(b, 0, 0, (0, 1, 2, 3))
                    dve.wait_ge(v_done, 7 * b + 7)
                    alone(dve)
                    with dve.Fori(0, NW - 1) as g:
                        window_row(b, g, False)
                    window_row(b, NW - 1, True)
                    for k in range(NW):
                        dve.wait_ge(proj_ready, 7 * b + k + 1)
                        nc.vector.scalar_tensor_tensor(image(xs, k), ps[:, 4 + k % 2, 0:ROW], bo[:], image(xs, k),
                                                       ALU.add, ALU.add).then_inc(x2_ready, 1)
                    layer_norm(b, 1)
                    for t in range(0, 2 * NT, 2):
                        dve.wait_ge(tr_ready, 8 * b + t + 1)
                        nc.vector.tensor_copy(utok[:, t // 2, 0:4, :].rearrange("p a b -> p (a b)"), ps[0:N1T, 4 + t % 4, :]).then_inc(ut_evac0, 1)
                    for s in range(2 * NFT):
                        dve.wait_ge(dft_ready, 16 * b + 2 * s + 1)
                        dve.wait_ge(u_stored[s % 2], 16 * (4 * b + s // 2) + 16 * FREE)
                        nc.vector.tensor_copy(ustage[:, s % 2, 0:512], ps[0:FT, (2 * s) % 4, :]).then_inc(u_evac0, 1)


def filter_and_product(nc, phi_d, sigma_d, mu_d, mp_d, mm_d, logw_d, gumbel_d, cst, prefix, spec_d, prod_d):
    with ExitStack() as ctx:
        def sb(name, shape, dt=F32):
            return ctx.enter_context(nc.sbuf_tensor(name, shape, dt))

        def sem(name):
            return ctx.enter_context(nc.semaphore(name))

        NB = NIMG
        Q = 2 * NB * R
        ms = sb("ms", [KP, 2, C, C], BF16)
        vs = sb("vs", [KP, NCH, 2, 4, 2, FC], BF16)
        ps = ctx.enter_context(nc.psum_tensor("psb", [C, 8, 512], F32))

        with ExitStack() as prep:
            def sbp(name, shape, dt=F32):
                return prep.enter_context(nc.sbuf_tensor(name, shape, dt))

            def semp(name):
                return prep.enter_context(nc.semaphore(name))

            MC, NMC = 2048, C * C // 2048
            UN = MC // 512
            lg = sbp("lg", [C, 2, 4])
            soft = sbp("soft", [C, 8, 4])
            col = sbp("col", [C, 8])
            sig = sbp("sig", [C, 1])
            own = sbp("own", [C, 8])
            part = sbp("part", [KP, 4])
            sel = sbp("selm", [C, 2, KP])
            selu = sbp("selu", [12, KP])
            phi = sbp("phi", [N1T, NT * R, 16])
            delta = sbp("deltas", [N1T, NT * R, 3])
            phir = sbp("phir", [N1T, NT * R, COPIES, KF])
            dft = sbp("dftb", [N1T, NT, 2, NF])
            mat = sbp("mat", [C, 2, MC])
            matu = sbp("matu", [12, 2, MC])
            hi = sbp("hi", [KP, 2, 512], BF16)
            rest = sbp("rest", [KP, 2, 512])
            mid = sbp("mid", [KP, 2, 512], BF16)
            loaded, sm, sel_ready, phi_ready, ssig = map(semp, ("b_loaded", "b_small", "b_sel", "b_phi", "b_sig"))
            smx, sma = semp("b_smx"), semp("b_sma")
            mat_loaded = [semp("mat_loaded0"), semp("mat_loaded1")]
            unit_ready, hi_done, rest_done, mid_done, split_done = map(
                semp, ("unit_ready", "hi_done", "rest_done", "mid_done", "split_done"))
            NV = 2 * R
            NUNIT = NV + 2 * UN * NMC

            with nc.Block() as block:
                @block.sync
                def _(sp):
                    loads = [(lg[:, 0, :], logw_d.partition_broadcast(C)), (lg[:, 1, :], gumbel_d.partition_broadcast(C)),
                             (own[:], cst["own_variant"]), (part[:], cst["part"]),
                             (sel[:].rearrange("p a b -> p (a b)"), cst["sel"]), (selu[:], cst["sel_u"]),
                             (delta[:].rearrange("p a b -> p (a b)"), cst["delta"]),
                             (dft[:].rearrange("p a b c -> p (a b c)"), cst["dft"])]
                    loads += [(sig[16 * i:16 * i + 16, :], sigma_d.unsqueeze(1)) for i in range(8)]
                    loads += [(phi[:, nt * R:(nt + 1) * R, :].rearrange("p a b -> p (a b)"),
                               phi_d[nt * N1T * R:(nt + 1) * N1T * R, :].rearrange("(n r) k -> n (r k)", r=R)) for nt in range(NT)]
                    assert len(loads) == 20
                    for dst, src in loads:
                        sp.dma_start(dst, src).then_inc(loaded, 16)
                    for m in range(NMC):
                        if m >= 2:
                            sp.wait_ge(unit_ready, NV + 2 * UN * (m - 1))
                        cols = slice(m * MC, (m + 1) * MC)
                        for dst, src in ((mat[0:64, m % 2, :], mp_d[:, cols]), (mat[64:128, m % 2, :], mm_d[:, cols]),
                                         (matu[:, m % 2, :], mu_d[:, cols])):
                            sp.dma_start(dst, src).then_inc(mat_loaded[m % 2], 16)

                @block.gpsimd
                def _(pool):
                    pool.wait_ge(loaded, 16 * 20)
                    for cpy in range(COPIES):
                        nc.gpsimd.tensor_copy(phir[:, :, cpy, 0:16], phi[:]).then_inc(phi_ready, 1)
                        nc.gpsimd.tensor_copy(phir[:, :, cpy, 16:KF], delta[:]).then_inc(phi_ready, 1)

                @block.tensor
                def _(pe):
                    pe.wait_ge(phi_ready, 2 * COPIES)
                    for u in range(NV):
                        s, c = u // 2, u % 2
                        if u >= 2:
                            pe.wait_ge(hi_done, u - 1)
                            pe.wait_ge(rest_done, u - 1)
                        for nt in range(NT):
                            last = nc.tensor.matmul(ps[0:KP, u % 2, 0:NF], phir[:, nt * R + s, :, :].rearrange("p a b -> p (a b)"),
                                                    dft[:, nt, c, :], start=(nt == 0), stop=(nt == NT - 1))
                        last.then_inc(unit_ready, 1)
                    pe.wait_ge(sel_ready, 2)
                    for u in range(NV, NUNIT):
                        m, rem = (u - NV) // (2 * UN), (u - NV) % (2 * UN)
                        odd, cols = rem // UN, slice((rem % UN) * 512, (rem % UN + 1) * 512)
                        if rem == 0:
                            pe.wait_ge(mat_loaded[m % 2], 48 * (m // 2 + 1))
                        pe.wait_ge(hi_done, u - 1)
                        pe.wait_ge(rest_done, u - 1)
                        nc.tensor.matmul(ps[0:KP, u % 2, :], sel[:, odd, :], mat[:, m % 2, cols], start=True, stop=False)
                        nc.tensor.matmul(ps[0:KP, u % 2, :], selu[:], matu[:, m % 2, cols], start=False, stop=True).then_inc(unit_ready, 1)

                def width(u):
                    return NF if u < NV else 512

                @block.scalar
                def _(act):
                    act.wait_ge(loaded, 16 * 20)
                    nc.scalar.activation(col[:, 0:1], sig[:], ACT.Sqrt).then_inc(ssig, 1)
                    act.wait_ge(ssig, 1)
                    nc.scalar.activation(col[:, 1:2], col[:, 0:1], ACT.Sqrt).then_inc(ssig, 1)
                    act.wait_ge(smx, 1)
                    nc.scalar.activation(soft[:, 1, :], soft[:, 0, :], ACT.Exp, bias=col[:, 2:3], accum_out=col[:, 3:4]).then_inc(sma, 1)
                    for u in range(NUNIT + 1):
                        if u < NUNIT:
                            act.wait_ge(unit_ready, u + 1)
                            if u >= 2:
                                act.wait_ge(rest_done, u - 1)
                            nc.scalar.activation(hi[:, u % 2, 0:width(u)], ps[0:KP, u % 2, 0:width(u)], ACT.Copy).then_inc(hi_done, 1)
                        if u >= 1:
                            v = u - 1
                            act.wait_ge(rest_done, v + 1)
                            if v >= 2:
                                act.wait_ge(split_done, v - 1)
                            nc.scalar.activation(mid[:, v % 2, 0:width(v)], rest[:, v % 2, 0:width(v)], ACT.Copy).then_inc(mid_done, 1)

                @block.vector
                def _(dve):
                    steps = [0]

                    def then(ins):
                        steps[0] += 1
                        ins.then_inc(sm, 1)
                        dve.wait_ge(sm, steps[0])

                    dve.wait_ge(loaded, 16 * 20)
                    v = nc.vector
                    then(v.tensor_tensor(soft[:, 0, :], lg[:, 0, :], lg[:, 1, :], ALU.add))
                    v.tensor_reduce(col[:, 2:3], soft[:, 0, :], AX.X, ALU.max, negate=True).then_inc(smx, 1)
                    dve.wait_ge(sma, 1)
                    then(v.reciprocal(col[:, 4:5], col[:, 3:4]))
                    then(v.tensor_scalar(soft[:, 2, :], soft[:, 1, :], col[:, 4:5], None, ALU.mult))
                    then(v.tensor_reduce(col[:, 5:6], soft[:, 2, :], AX.X, ALU.max))
                    then(v.tensor_scalar(soft[:, 3, :], soft[:, 2, :], col[:, 5:6], None, ALU.is_ge))
                    then(v.tensor_scalar(soft[:, 4, :], soft[:, 3, :], -1.0, 1.0, ALU.mult, ALU.add))
                    for i in range(1, 4):
                        then(v.tensor_tensor(soft[:, 3, i:i + 1], soft[:, 3, i:i + 1], soft[:, 4, i - 1:i], ALU.mult))
                        then(v.tensor_tensor(soft[:, 4, i:i + 1], soft[:, 4, i:i + 1], soft[:, 4, i - 1:i], ALU.mult))
                    then(v.tensor_copy(prefix[:, 0:1], soft[:, 3, 0:1]))
                    for i in range(1, 4):
                        then(v.tensor_tensor(prefix[:, i:i + 1], prefix[:, i - 1:i], soft[:, 3, i:i + 1], ALU.add))
                    then(v.tensor_tensor(soft[:, 5, :], soft[:, 3, :], soft[:, 2, :], ALU.subtract))
                    then(v.tensor_tensor(soft[:, 6, :], soft[:, 5, :], soft[:, 2, :], ALU.add))
                    for i in range(2):
                        then(v.tensor_tensor(soft[:, 7, :], soft[:, 6, :], own[:, 4 * i:4 * i + 4], ALU.mult))
                        then(v.tensor_reduce(col[:, 6 + i:7 + i], soft[:, 7, :], AX.X, ALU.add))
                    dve.wait_ge(ssig, 2)
                    then(v.tensor_tensor(col[:, 6:7], col[:, 6:7], col[:, 1:2], ALU.mult))
                    v.tensor_scalar(sel[:], sel[:], col[:, 6:7], None, ALU.mult).then_inc(sel_ready, 1)
                    v.tensor_scalar(selu[:], selu[:], col[0:12, 7:8], None, ALU.mult).then_inc(sel_ready, 1)
                    for u in range(NUNIT + 1):
                        if u < NUNIT:
                            w, lv = width(u), (0 if u < NV else 2)
                            dve.wait_ge(hi_done, u + 1)
                            if u >= 2:
                                dve.wait_ge(split_done, u - 1)
                            v.scalar_tensor_tensor(rest[:, u % 2, 0:w], hi[:, u % 2, 0:w], part[:, lv:lv + 1],
                                                   ps[0:KP, u % 2, 0:w], ALU.mult, ALU.add).then_inc(rest_done, 1)
                        if u >= 1:
                            q = u - 1
                            w, lv = width(q), (0 if q < NV else 2)
                            dve.wait_ge(mid_done, q + 1)
                            dve.wait_ge(rest_done, q + 1)
                            if q < NV:
                                s, c = q // 2, q % 2
                                dst = vs[:, :, s % 2, s // 2, c, :]
                                a, b = (z[:, q % 2, 0:w].rearrange("p (h f) -> p h f", f=FC) for z in (mid, rest))
                            else:
                                m, rem = (q - NV) // (2 * UN), (q - NV) % (2 * UN)
                                d0 = (m * UN + rem % UN) * 4
                                dst = ms[:, rem // UN, :, d0:d0 + 4].rearrange("p e d -> p d e")
                                a, b = (z[:, q % 2, 0:w].rearrange("p (d e) -> p d e", e=C) for z in (mid, rest))
                            v.scalar_tensor_tensor(dst, a, part[:, lv + 1:lv + 2], b, ALU.mult, ALU.add).then_inc(split_done, 1)

        gf = sb("gf", [C, FC, 16, C])
        ux = sb("ux", [C, FC, 3, NB, RX])
        tw = sb("tw", [C, 2, FC, 2 * NB, R - 1])
        vcur = sb("vcur", [KP, 2, 64], BF16)
        tcur = sb("tcur", [C, 2, FC])
        xin = sb("xin", [Q, FC, C])
        ye = sb("ye", [C, FC, Q])
        yst = sb("yst", [Q, FC, C])
        ident = sb("identb", [C, C])
        twist = sb("twist", [C, 2, NF])
        cl, x_in, xtr_ready, ux_plain, twist_step, vcur_ready = map(
            sem, ("bc_loaded", "x_in", "xtr_ready", "ux_plain", "twist_step", "vcur_ready"))
        g_ready, g_evac0, g_evac1, y_ready, ye_evac, ytr_ready, yst_evac, y_stored = map(
            sem, ("g_ready", "g_evac0", "g_evac1", "y_ready", "ye_evac", "ytr_ready", "yst_evac", "y_stored"))

        with nc.Block() as block:
            @block.sync
            def _(sp):
                sp.sem_inc(y_stored, 16 * FREE)
                sp.dma_start(ident[:], cst["ident"]).then_inc(cl, 16)
                sp.dma_start(twist[:].rearrange("p a b -> p (a b)"), cst["twist"]).then_inc(cl, 16)
                with sp.Fori(0, NCH) as ch:
                    sp.wait_ge(xtr_ready, 2 * ch + FREE)
                    sp.dma_start(xin[:], spec_d[bass.ds(ch * FC, FC)].rearrange("f c b n -> f (c b n)").rearrange("f (q d) -> q f d", d=C)).then_inc(x_in, 16)
                    sp.wait_ge(yst_evac, 2 * ch + 2 + FREE)
                    sp.dma_start(prod_d[bass.ds(ch * FC, FC)].rearrange("f q e -> q f e"), yst[:]).then_inc(y_stored, 16)
                sp.wait_ge(y_stored, 16 * NCH + 16 * FREE)

            @block.gpsimd
            def _(pool):
                pool.sem_inc(twist_step, FREE)
                pool.wait_ge(cl, 32)

                def kb(v):
                    return v.rearrange("p f k b r -> p f (k b) r")

                with pool.Fori(0, NCH) as ch:
                    pool.wait_ge(ux_plain, 4 * ch + 4)
                    pool.wait_ge(vcur_ready, 2 * ch + 2)
                    cs, sn = (tcur[:, z, :].unsqueeze(2).unsqueeze(3) for z in range(2))
                    dims = [C, FC, 2 * NB, R - 1]
                    half = [C, FC, NB, R - 1]
                    nc.gpsimd.tensor_tensor(tw[:, 0], kb(ux[:, :, 0:2, :, R:RX]), cs.to_broadcast(dims), ALU.mult).then_inc(twist_step, 1)
                    nc.gpsimd.tensor_tensor(tw[:, 1], kb(ux[:, :, 1:3, :, R:RX]), sn.to_broadcast(dims), ALU.mult).then_inc(twist_step, 1)
                    pool.wait_ge(twist_step, 6 * ch + 2 + FREE)
                    nc.gpsimd.tensor_tensor(kb(ux[:, :, 0:2, :, 0:R - 1]), tw[:, 0], tw[:, 1], ALU.add).then_inc(twist_step, 1)
                    pool.wait_ge(twist_step, 6 * ch + 3 + FREE)
                    nc.gpsimd.tensor_tensor(tw[:, 0, :, 0:NB, :], ux[:, :, 2, :, R:RX], cs.to_broadcast(half), ALU.mult).then_inc(twist_step, 1)
                    nc.gpsimd.tensor_tensor(tw[:, 1, :, 0:NB, :], ux[:, :, 1, :, R:RX], sn.to_broadcast(half), ALU.mult).then_inc(twist_step, 1)
                    pool.wait_ge(twist_step, 6 * ch + 5 + FREE)
                    nc.gpsimd.tensor_tensor(ux[:, :, 2, :, 0:R - 1], tw[:, 0, :, 0:NB, :], tw[:, 1, :, 0:NB, :], ALU.subtract).then_inc(twist_step, 1)

            @block.tensor
            def _(pe):
                for s in (xtr_ready, y_ready, ytr_ready):
                    pe.sem_inc(s, FREE)
                pe.wait_ge(cl, 32)
                with pe.Fori(0, NCH) as ch:
                    pe.wait_ge(x_in, 16 * ch + 16)
                    pe.wait_ge(yst_evac, 2 * ch + FREE)
                    for half in range(2):
                        for f in range(4):
                            last = nc.tensor.transpose(ps[:, half, f * Q:(f + 1) * Q], xin[:, 4 * half + f, :], ident[0:Q, 0:Q])
                        last.then_inc(xtr_ready, 1)
                    pe.wait_ge(vcur_ready, 2 * ch + 1)
                    for blk in range(32):
                        if blk < 4:
                            if blk % 2 == 0:
                                pe.wait_ge(g_evac0, 16 * ch + FREE)
                            else:
                                pe.wait_ge(g_evac1, 16 * ch + FREE)
                        elif blk % 2 == 0:
                            pe.wait_ge(g_evac0, 16 * ch + blk // 2 - 1 + FREE)
                        else:
                            pe.wait_ge(g_evac1, 16 * ch + blk // 2 - 1 + FREE)
                        for e in range(4):
                            for odd in range(2):
                                o = (2 * e + odd) * 64
                                last = nc.tensor.matmul(ps[:, 2 + blk % 4, o:o + 64], ms[:, odd, 4 * blk + e, :], vcur[:, odd, :],
                                                        start=True, stop=True)
                        last.then_inc(g_ready, 1)
                    pe.wait_ge(g_evac0, 16 * ch + 16 + FREE)
                    pe.wait_ge(g_evac1, 16 * ch + 16 + FREE)
                    pe.wait_ge(twist_step, 6 * ch + 6 + FREE)
                    for half in range(2):
                        pe.wait_ge(ye_evac, 2 * ch + half + FREE)
                        for f in range(4):
                            fi = 4 * half + f
                            for m in range(16):
                                odd, sp_, c = m // 8, (m % 8) // 2, m % 2
                                s = 2 * sp_ + odd
                                parts = slice(1, 3) if c == 0 else slice(0, 2)
                                last = nc.tensor.matmul(ps[:, 6 + half, f * Q:(f + 1) * Q], gf[:, fi, m, :],
                                                        ux[:, fi, parts, :, R - 1 - s:RX - s].rearrange("p k b r -> p (k b) r"),
                                                        start=(m == 0), stop=(m == 15))
                        last.then_inc(y_ready, 1)
                    for half in range(2):
                        pe.wait_ge(ye_evac, 2 * ch + half + 1 + FREE)
                        for f in range(4):
                            last = nc.tensor.transpose(ps[0:Q, half, f * C:(f + 1) * C], ye[:, 4 * half + f, :], ident[:])
                        last.then_inc(ytr_ready, 1)

            def spread(blk):
                return (gf[:, :, :, 4 * blk:4 * blk + 4].rearrange("p f m e -> p e m f"),
                        ps[:, 2 + blk % 4, :].rearrange("p (e m f) -> p e m f", e=4, f=FC))

            @block.scalar
            def _(act):
                for s in (g_evac1, ye_evac):
                    act.sem_inc(s, FREE)
                with act.Fori(0, NCH) as ch:
                    for half in range(2):
                        fs = slice(4 * half, 4 * half + 4)
                        act.wait_ge(xtr_ready, 2 * ch + half + 1 + FREE)
                        act.wait_ge(y_ready, 2 * ch + FREE)
                        nc.scalar.activation(ux[:, fs, 1:3, :, R - 1:RX].rearrange("p f k b r -> p f (k b) r"),
                                             ps[:, half, 0:4 * Q].rearrange("p (f q r) -> p f q r", f=4, r=R), ACT.Copy).then_inc(ux_plain, 1)
                        nc.scalar.activation(ux[:, fs, 0, :, R - 1:RX],
                                             ps[:, half, 0:4 * Q].rearrange("p (f c b r) -> p f c b r", f=4, c=2, b=NB)[:, :, 1],
                                             ACT.Copy, scale=-1.0).then_inc(ux_plain, 1)
                    for blk in range(1, 32, 2):
                        act.wait_ge(g_ready, 32 * ch + blk + 1)
                        dst, src = spread(blk)
                        nc.scalar.activation(dst, src, ACT.Copy).then_inc(g_evac1, 1)
                    for half in range(2):
                        act.wait_ge(y_ready, 2 * ch + half + 1 + FREE)
                        act.wait_ge(ytr_ready, 2 * ch + FREE)
                        nc.scalar.activation(ye[:, 4 * half:4 * half + 4, :].rearrange("p f q -> p (f q)"), ps[:, 6 + half, 0:4 * Q], ACT.Copy).then_inc(ye_evac, 1)

            @block.vector
            def _(dve):
                for s in (g_evac0, yst_evac):
                    dve.sem_inc(s, FREE)
                dve.wait_ge(cl, 32)
                with dve.Fori(0, NCH) as ch:
                    dve.wait_ge(y_ready, 2 * ch + FREE)
                    nc.vector.tensor_copy(vcur[:].unsqueeze(1), vs[:, bass.ds(ch, 1)].rearrange("p a o s c f -> p a o (s c f)")).then_inc(vcur_ready, 1)
                    dve.wait_ge(twist_step, 6 * ch + FREE)
                    nc.vector.tensor_copy(tcur[:], twist[:, :, bass.ds(ch * FC, FC)]).then_inc(vcur_ready, 1)
                    for blk in range(0, 32, 2):
                        dve.wait_ge(g_ready, 32 * ch + blk + 1)
                        dst, src = spread(blk)
                        nc.vector.tensor_copy(dst, src).then_inc(g_evac0, 1)
                    dve.wait_ge(y_stored, 16 * ch + 16 * FREE)
                    for half in range(2):
                        dve.wait_ge(ytr_ready, 2 * ch + half + 1 + FREE)
                        nc.vector.tensor_copy(yst[:, 4 * half:4 * half + 4, :].rearrange("p f e -> p (f e)"), ps[0:Q, half, :]).then_inc(yst_evac, 1)


def inverse_and_store(nc, cst, prefix, prod_d, x2_d, out_d):
    with ExitStack() as ctx:
        def sb(name, shape, dt=F32):
            return ctx.enter_context(nc.sbuf_tensor(name, shape, dt))

        def sem(name):
            return ctx.enter_context(nc.semaphore(name))

        idft = sb("idft", [FT, NFT, 2, N1])
        yin = sb("yin", [FT, 2, NFT, 2, R * C])
        x2 = sb("x2", [C, 2, T])
        ps = ctx.enter_context(nc.psum_tensor("psc", [C, 8, 512], F32))
        cl, masked, z_ready, x3_done = map(sem, ("cc_loaded", "masked", "z_ready", "x3_done"))
        y_in, x2_in, stored = ([sem(f"{n}{z}") for z in range(2)] for n in ("y_in", "x2_in", "stored"))
        REACH = [(0, N1 // 8, 3), (N1 // 8, N1 // 4, 2), (N1 // 4, N1 // 2, 1), (N1 // 2, N1, 0)]
        with nc.Block() as block:
            @block.sync
            def _(sp):
                for z in range(2):
                    sp.sem_inc(stored[z], 16 * FREE)
                sp.dma_start(idft[:].rearrange("p a b c -> p (a b c)"), cst["idft"]).then_inc(cl, 16)

                def load(b, z):
                    for ft in range(NFT):
                        sp.dma_start(yin[:, z, ft], prod_d[ft * FT:(ft + 1) * FT].rearrange("f (c b r) e -> f c b (r e)", c=2, r=R)[:, :, bass.ds(b, 1), :]
                                     .rearrange("f c b n -> f (c b) n")).then_inc(y_in[z], 16)
                    sp.dma_start(x2[:, z], x2_d[bass.ds(b, 1)].rearrange("a c t -> (a c) t")).then_inc(x2_in[z], 16)

                with sp.Fori(0, NIMG // 2) as p:
                    for z in range(2):
                        sp.wait_ge(stored[z], 16 * p + 16 * FREE)
                        load(2 * p + z, z)
                    for z in range(2):
                        sp.wait_ge(x3_done, 8 * (2 * p + z) + 16)
                        sp.dma_start(out_d[bass.ds(2 * p + z, 1)].rearrange("a c t -> (a c) t"), x2[:, z]).then_inc(stored[z], 16)
                for z in range(2):
                    sp.wait_ge(stored[z], 16 * (NIMG // 2) + 16 * FREE)

            @block.tensor
            def _(pe):
                pe.wait_ge(masked, 4)
                with pe.Fori(0, NIMG // 2) as p:
                    for z in range(2):
                        pe.wait_ge(y_in[z], 16 * NFT * (p + 1))
                        for r in range(R):
                            pe.wait_ge(x3_done, 8 * (2 * p + z) + r + 1)
                            for q in range(2 * NFT):
                                ft, c = q // 2, q % 2
                                last = nc.tensor.matmul(ps[:, r, 0:N1], yin[:, z, ft, c, r * C:(r + 1) * C], idft[:, ft, c, :],
                                                        start=(q == 0), stop=(q == 2 * NFT - 1))
                            last.then_inc(z_ready, 1)

            @block.vector
            def _(dve):
                dve.sem_inc(x3_done, 8)
                dve.wait_ge(cl, 16)
                for a, b, i in REACH:
                    nc.vector.tensor_scalar(idft[:, :, :, a:b], idft[:, :, :, a:b], prefix[0:FT, i:i + 1], None, ALU.mult).then_inc(masked, 1)
                with dve.Fori(0, NIMG // 2) as p:
                    for z in range(2):
                        dve.wait_ge(x2_in[z], 16 * (p + 1))
                        for r in range(R):
                            dve.wait_ge(z_ready, 8 * (2 * p + z) + r + 1)
                            v = x2[:, z].rearrange("p (n r) -> p n r", r=R)[:, :, r]
                            nc.vector.tensor_tensor(v, v, ps[:, r, 0:N1], ALU.add).then_inc(x3_done, 1)


def program(nc, x, w_qkv, b_qkv, lepe_w, lepe_b, w_o, b_o, sigma, phi, m_u, m_plus, m_minus, log_weights, gumbel, cst, out):
    x2_d = nc.dram_tensor("x2_scratch", (NIMG, C, T), F32, kind="Internal").ap()
    spec_d = nc.dram_tensor("spectrum_scratch", (NF, 2, NIMG, R * C), F32, kind="Internal").ap()
    prod_d = nc.dram_tensor("product_scratch", (NF, 2 * NIMG * R, C), F32, kind="Internal").ap()
    route_d = nc.dram_tensor("route_scratch", (NIMG, NWIN * TOPK), U32, kind="Internal").ap()
    attention_and_dft(nc, x, w_qkv, b_qkv, lepe_w, lepe_b, w_o, b_o, cst, x2_d, spec_d, route_d)
    with nc.sbuf_tensor("prefix", [C, 4], F32) as prefix:
        filter_and_product(nc, phi, sigma, m_u, m_plus, m_minus, log_weights, gumbel, cst, prefix, spec_d, prod_d)
        inverse_and_store(nc, cst, prefix, prod_d, x2_d, out)


_INS = [("x", (NIMG, C, T)), ("L0_conv_W_qkv", (C, 3 * C)), ("L0_conv_b_qkv", (3 * C,)), ("L0_conv_lepe_w", (C, 9)),
        ("L0_conv_lepe_b", (C,)), ("L0_conv_W_o", (C, C)), ("L0_conv_b_o", (C,)), ("L0_ffn_sigma", (16,)),
        ("L0_ffn_phi", (4096, 16)), ("L0_ffn_M_u", (12, C * C)), ("L0_ffn_M_phi_plus", (64, C * C)),
        ("L0_ffn_M_phi_minus", (64, C * C)), ("L0_ffn_log_weights", (4,)), ("L0_ffn_gumbel", (4,))]


def kernel(**inputs):
    import numpy as _np
    import concourse.bacc as _bacc
    from concourse.bass_utils import run_bass_kernel_spmd as _run

    nc = _bacc.Bacc("TRN2", target_bir_lowering=False, num_devices=1)
    arrays, args, cst = {}, [], {}
    for name, shape in _INS:
        arrays[f"in_{name}_dram"] = _np.ascontiguousarray(inputs[name]).reshape(shape)
        args.append(nc.dram_tensor(f"in_{name}_dram", shape, F32, kind="ExternalInput").ap())
    for name, table in constants().items():
        arrays[f"const_{name}_dram"] = table
        cst[name] = nc.dram_tensor(f"const_{name}_dram", table.shape, F32, kind="ExternalInput").ap()
    out = nc.dram_tensor("out_0_dram", (NIMG, C, T), F32, kind="ExternalOutput").ap()
    program(nc, *args, cst, out)
    done = _run(nc, [arrays], core_ids=[0])
    return done.results[0]["out_0_dram"].reshape(NIMG, C, HW, HW)
```

```python
from contextlib import ExitStack

import concourse.bass as bass
import numpy as np
from concourse import mybir

F32 = mybir.dt.float32
BF16 = mybir.dt.bfloat16
U32 = mybir.dt.uint32
ALU = mybir.AluOpType
ACT = mybir.ActivationFunctionType
AX = mybir.AxisListType

NIMG, C, HW = 8, 128, 56
T = HW * HW
NW = 7
WS = HW // NW
NWIN, WT = NW * NW, WS * WS
ROW = NW * WT
QT = ROW // 4
TOPK, HEADS, HD = 4, 8, 16
NHP = HEADS // 2
SCALE = float(C) ** -0.5
EPS_C, EPS_T = 1e-6, 1e-5

R = 8
N1 = T // R
NF2 = 2 * N1
NT, N1T = 4, N1 // 4
FT, NFT = 100, 4
NF = FT * NFT
FC = 8
NCH = NF // FC
KF, COPIES = 19, 6
KP = KF * COPIES
RX = 2 * R - 1

FREE = 1
BUF = [0, 1, 0, 1, 0, 1, 2]


def constants():
    c = {}
    c["ident"] = np.eye(C, dtype=np.float32)
    c["mean_mat"] = np.full((C, C), 1.0 / C, np.float32)
    c["head_parity"] = np.stack([(np.arange(C) // HD) % 2 == h for h in range(2)]
                                + [np.arange(C) // HD == h for h in range(HEADS)], 1).astype(np.float32)
    n, f = np.arange(N1), np.arange(NF)
    live = (f <= NF2 // 2)
    ang = 2 * np.pi * ((n[:, None] * f[None]) % NF2) / NF2
    fwd = np.stack([np.cos(ang), -np.sin(ang)], 1) * live
    c["dft"] = fwd.reshape(NT, N1T, 2, NF).transpose(1, 0, 2, 3).reshape(N1T, NT * 2 * NF).astype(np.float32)
    amp = np.where((f == 0) | (f == NF2 // 2), 1.0, 2.0) * live / NF2
    inv = np.stack([np.cos(ang.T), -np.sin(ang.T)], 1) * amp[:, None, None]
    c["idft"] = inv.reshape(NFT, FT, 2, N1).transpose(1, 0, 2, 3).reshape(FT, NFT * 2 * N1).astype(np.float32)
    th = 2 * np.pi * f / NF2
    c["twist"] = np.broadcast_to(np.stack([np.cos(th), np.sin(th)]).astype(np.float32)[None], (C, 2, NF)).reshape(C, 2 * NF).copy()
    delta = np.zeros((N1T, NT, R, 3), np.float32)
    for j in range(3):
        delta[0, 0, j, j] = 1.0
    c["delta"] = delta.reshape(N1T, NT * R * 3)
    lvl_v, lvl_m = [0, 0, 0, 1, 1, 2], [0, 1, 2, 0, 1, 0]
    part = np.zeros((KP, 4), np.float32)
    for cpy in range(COPIES):
        rows = slice(cpy * KF, (cpy + 1) * KF)
        part[rows, 0] = -1.0 if lvl_v[cpy] >= 1 else 0.0
        part[rows, 1] = -1.0 if lvl_v[cpy] == 2 else 0.0
        part[rows, 2] = -1.0 if lvl_m[cpy] >= 1 else 0.0
        part[rows, 3] = -1.0 if lvl_m[cpy] == 2 else 0.0
    c["part"] = part
    sel = np.zeros((128, 2, COPIES, KF), np.float32)
    for s in range(2):
        for i in range(4):
            for k in range(16):
                sel[s * 64 + i * 16 + k, 0, :, k] = 1.0
                sel[s * 64 + i * 16 + k, 1, :, k] = 1.0 if s == 0 else -1.0
    c["sel"] = sel.reshape(128, 2 * KP)
    selu = np.zeros((12, COPIES, KF), np.float32)
    for i in range(4):
        for j in range(3):
            selu[i * 3 + j, :, 16 + j] = 1.0
    c["sel_u"] = selu.reshape(12, KP)
    own = np.zeros((128, 8), np.float32)
    for p in range(128):
        own[p, (p // 16) % 4] = 1.0
    for p in range(12):
        own[p, 4 + p // 3] = 1.0
    c["own_variant"] = own
    return c


def attention_and_dft(nc, x_d, wqkv_d, bqkv_d, lepe_w_d, lepe_b_d, wo_d, bo_d, cst, x2_d, spec_d, route_d):
    with ExitStack() as ctx:
        def sb(name, shape, dt=F32):
            return ctx.enter_context(nc.sbuf_tensor(name, shape, dt))

        def sem(name):
            return ctx.enter_context(nc.semaphore(name))

        xs = sb("xs", [C, T])
        xn = sb("xn", [C, T])
        xc = sb("xc", [C, 3, ROW])
        sq = sb("sq", [C, 2, ROW])
        std = sb("std", [QT, 2, 4])
        rstd = sb("rstd", [QT, 2, 4])
        epsc = sb("epsc", [C, 2])
        qT = sb("qT", [C, T])
        kT = sb("kT", [C, T])
        vpad = sb("vpad", [C, HW + 2, HW + 2])
        vtok = sb("vtok", [WT, NWIN, C])
        oT = sb("oT", [C, T])
        utok = sb("utok", [N1T, NT, R, C])
        wqkv = sb("wqkv", [C, 3 * C])
        wo = sb("wo", [C, C])
        bq, bk, bv, bo, lb = (sb(n, [C, 1]) for n in ("bq", "bk", "bv", "bo", "lb"))
        bqs = sb("bqs", [C, 1])
        bvrow = sb("bvrow", [C, C])
        lw = sb("lw", [C, 9])
        ident = sb("ident", [C, C])
        mean_mat = sb("mean_mat", [C, C])
        hpar = sb("hpar", [C, 2 + HEADS])
        dft = sb("dft", [N1T, NT, 2, NF])
        qsum = sb("qsum", [C, NWIN])
        ksum = sb("ksum", [C, NWIN])
        logit = sb("logit", [NWIN, NWIN])
        top = sb("top", [NWIN, 8])
        topi = sb("topi", [NWIN, 8], U32)
        route = sb("route", [1, NWIN * TOPK], U32)
        ksel = sb("ksel", [C, NW, TOPK * WT])
        vsel = sb("vsel", [C, NW, 2, C])
        qz = sb("qz", [C, NW, HEADS, WT])
        nmax = sb("nmax", [C, 3, NHP])
        rsum = sb("rsum", [C, 3, NHP])
        rinv = sb("rinv", [C, 3, NHP])
        prob = sb("prob", [C, 3, NHP, TOPK * WT])
        probT = sb("probT", [C, 3, 2, 2, 2, C])
        oeven = sb("oeven", [C, WT])
        ustage = sb("ustage", [FT, 2, R * C])
        ps = ctx.enter_context(nc.psum_tensor("ps", [C, 8, 512], F32))

        consts_loaded, x_loaded, ready0, x2_stored = map(sem, ("consts_loaded", "x_loaded", "ready0", "x2_stored"))
        mean_ready, centered, squared, var_ready, std_ready, inverted, spread_ready, normed = map(
            sem, ("mean_ready", "centered", "squared", "var_ready", "std_ready", "inverted", "spread_ready", "normed"))
        qkv_ready, q_done, k_done, v_done, vt_done, sums_done = map(
            sem, ("qkv_ready", "q_done", "k_done", "v_done", "vt_done", "sums_done"))
        logit_ready, topk_step, route_stored, route_loaded = map(
            sem, ("logit_ready", "topk_step", "route_stored", "route_loaded"))
        gathered, s_ready, max_done, exp_done, t_ready, t_evac0, t_evac1 = map(
            sem, ("gathered", "s_ready", "max_done", "exp_done", "t_ready", "t_evac0", "t_evac1"))
        pv_done, rinv_done, norm_done, even_done, o_evac, lepe_done = map(
            sem, ("pv_done", "rinv_done", "norm_done", "even_done", "o_evac", "lepe_done"))
        proj_ready, x2_ready, tr_ready, ut_evac0, ut_evac1 = map(
            sem, ("proj_ready", "x2_ready", "tr_ready", "ut_evac0", "ut_evac1"))
        dft_ready, u_evac0, u_evac1 = map(sem, ("dft_ready", "u_evac0", "u_evac1"))
        passed = sem("passed")
        v_gathered = [sem(f"v_gathered{u}") for u in range(NW)]
        u_stored = [sem("u_stored0"), sem("u_stored1")]

        NCONST = 17

        def load_route(w, engine):
            return nc.values_load_multi_w_load_instructions(
                route[0:1, bass.ds(w * TOPK, TOPK)], engines=[engine], min_val=0, max_val=NWIN - 1)[1]

        def image(v, k):
            return v[:, k * ROW:(k + 1) * ROW]

        def by_window(v):
            return v.rearrange("p (y n x) -> p n y x", y=WS, n=NW)

        def by_image(v):
            return v.rearrange("p (n y x) -> p y n x", y=WS, n=NW)

        def alone(eng):
            eng.sem_inc(passed, 1)

        with nc.Block() as block:
            @block.sync
            def _(sp):
                for s in (x2_stored, route_stored, *u_stored):
                    sp.sem_inc(s, 16 * FREE)
                loads = [
                    (wqkv[:], wqkv_d), (wo[:], wo_d),
                    (bq[:], bqkv_d[0:C].unsqueeze(1)), (bk[:], bqkv_d[C:2 * C].unsqueeze(1)),
                    (bv[:], bqkv_d[2 * C:3 * C].unsqueeze(1)), (bo[:], bo_d.unsqueeze(1)),
                    (lb[:], lepe_b_d.unsqueeze(1)), (lw[:], lepe_w_d),
                    (bvrow[:], bqkv_d[2 * C:3 * C].partition_broadcast(C)),
                    (ident[:], cst["ident"]), (mean_mat[:], cst["mean_mat"]), (hpar[:], cst["head_parity"]),
                    (dft[:].rearrange("p a b c -> p (a b c)"), cst["dft"]),
                ]
                for dst, src in loads:
                    sp.dma_start(dst, src).then_inc(consts_loaded, 16)
                assert len(loads) == 13

                def gather_values(b, w, i):
                    routed = load_route(w, mybir.EngineType.SP)
                    sp.wait_ge(pv_done, NWIN * b + w + 1)
                    for j, n in enumerate(routed):
                        sp.dma_start(vsel[(j % 2) * WT:(j % 2 + 1) * WT, i, j // 2, :],
                                     vtok[:, bass.ds(n, 1), :].rearrange("p a c -> p (a c)")).then_inc(v_gathered[i], 16)

                with sp.Fori(0, NIMG) as b:
                    sp.wait_ge(normed, 14 * b + FREE)
                    alone(sp)
                    sp.wait_ge(x2_stored, 16 * b + 16 * FREE)
                    sp.dma_start(xs[:], x_d[bass.ds(b, 1)].rearrange("a c t -> (a c) t")).then_inc(x_loaded, 16)
                    sp.wait_ge(topk_step, 3 * b + 3)
                    sp.dma_start(route_d[bass.ds(b, 1)].rearrange("a (w j) -> (a w) j", j=TOPK), topi[:, 0:TOPK]).then_inc(route_stored, 16)
                    sp.wait_ge(route_stored, 16 * b + 16 + 16 * FREE)
                    sp.dma_start(route[:], route_d[bass.ds(b, 1)]).then_inc(route_loaded, 16)
                    sp.wait_ge(route_loaded, 16 * b + 16)
                    alone(sp)
                    sp.wait_ge(vt_done, 14 * b + 14)
                    alone(sp)
                    with sp.Fori(0, NW) as g:
                        for i in range(NW):
                            gather_values(b, g * NW + i, i)
                    sp.wait_ge(x2_ready, 7 * b + 7)
                    sp.dma_start(x2_d[bass.ds(b, 1)].rearrange("a c t -> (a c) t"), xs[:]).then_inc(x2_stored, 16)
                    for s in range(2 * NFT):
                        ft, c = s // 2, s % 2
                        sp.wait_ge(u_evac0, 8 * b + s + 1 + FREE)
                        sp.wait_ge(u_evac1, 8 * b + s + 1 + FREE)
                        sp.dma_start(spec_d[ft * FT:(ft + 1) * FT, c, bass.ds(b, 1), :].rearrange("f a n -> f (a n)"),
                                     ustage[:, s % 2, :]).then_inc(u_stored[s % 2], 16)
                sp.wait_ge(x2_stored, 16 * NIMG + 16 * FREE)
                for s in range(2):
                    sp.wait_ge(u_stored[s], 16 * NFT * NIMG + 16 * FREE)

            @block.gpsimd
            def _(pool):
                nc.gpsimd.memset(vpad[:], 0.0).then_inc(ready0, 1)
                nc.gpsimd.memset(epsc[:, 0:1], EPS_C).then_inc(ready0, 1)
                nc.gpsimd.memset(epsc[:, 1:2], EPS_T).then_inc(ready0, 1)
                pool.wait_ge(consts_loaded, 16 * 13)

                def gather(b, w, i):
                    u = i
                    gw = NWIN * b + w
                    routed = load_route(w, mybir.EngineType.Pool)
                    pool.wait_ge(pv_done, gw + 1)
                    nc.gpsimd.tensor_tensor(qz[:, u], qT[:, bass.ds(w * WT, WT)].unsqueeze(1).to_broadcast([C, HEADS, WT]),
                                            hpar[:, 2:].unsqueeze(2).to_broadcast([C, HEADS, WT]), ALU.mult)
                    for j, n in enumerate(routed):
                        last = nc.gpsimd.tensor_copy(ksel[:, u, j * WT:(j + 1) * WT], kT[:, bass.ds(n * WT, WT)])
                    last.then_inc(gathered, 1)

                with pool.Fori(0, NIMG) as b:
                    pool.wait_ge(route_loaded, 16 * b + 16)
                    pool.wait_ge(q_done, 7 * b + 7)
                    pool.wait_ge(sums_done, 14 * b + 14)
                    alone(pool)
                    with pool.Fori(0, NW) as g:
                        for i in range(NW):
                            gather(b, g * NW + i, i)

            @block.tensor
            def _(pe):
                pe.sem_inc(pv_done, NW)
                pe.wait_ge(consts_loaded, 16 * 13)

                def layer_norm(b, which):
                    for k in range(NW + 2):
                        n = 14 * b + 7 * which + k
                        if k < NW:
                            if which:
                                pe.wait_ge(x2_ready, 7 * b + k + 1)
                            if k >= 2:
                                pe.wait_ge(centered, n - 1)
                            nc.tensor.matmul(ps[:, k % 2, 0:ROW], mean_mat[:], image(xs, k),
                                             start=True, stop=True).then_inc(mean_ready, 1)
                        if 1 <= k <= NW:
                            pe.wait_ge(squared, n)
                            if k >= 3:
                                pe.wait_ge(std_ready, n - 2)
                            for j in range(4):
                                last = nc.tensor.matmul(ps[0:QT, 2 + (k - 1) % 2, j:j + 1], sq[:, (k - 1) % 2, j * QT:(j + 1) * QT],
                                                        mean_mat[:, 0:1], start=True, stop=True)
                            last.then_inc(var_ready, 1)
                        if k >= 2:
                            pe.wait_ge(inverted, n - 1)
                            if k >= 4:
                                pe.wait_ge(normed, n - 3 + FREE)
                            for j in range(4):
                                last = nc.tensor.matmul(ps[:, 6 + k % 2, j * QT:(j + 1) * QT],
                                                        rstd[:, k % 2, j:j + 1].to_broadcast([QT, C]), ident[0:QT, 0:QT],
                                                        start=True, stop=True)
                            last.then_inc(spread_ready, 1)

                def scores(b, w, i, hps):
                    u, gw = i, NWIN * b + w
                    pe.wait_ge(gathered, gw + 1)
                    for hp in hps:
                        pe.wait_ge(exp_done, 4 * gw + hp - 3 + 4)
                        nc.tensor.matmul(ps[:, hp, 0:TOPK * WT], qz[:, u, 2 * hp:2 * hp + 2, :], ksel[:, u, :],
                                         start=True, stop=True).then_inc(s_ready, 1)

                def transposes(b, w, i, a):
                    u, gw = BUF[i], NWIN * b + w
                    pe.wait_ge(norm_done, 4 * gw + 2 * a + 2)
                    if a == 0:
                        pe.wait_ge(t_evac0, gw + FREE)
                    else:
                        pe.wait_ge(t_evac1, gw + FREE)
                    for h in range(2):
                        for kt in range(2):
                            last = nc.tensor.transpose(ps[:, 4 + a, (2 * h + kt) * C:(2 * h + kt + 1) * C],
                                                       prob[:, u, 2 * a + h, kt * C:(kt + 1) * C], ident[:])
                    last.then_inc(t_ready, 1)

                def values(b, g, i, a):
                    gw = NWIN * b + NW * g + i
                    if a == 0:
                        pe.wait_ge(v_gathered[i], 16 * TOPK * (NW * b + g + 1))
                        pe.wait_ge(o_evac, gw + FREE)
                        pe.wait_ge(t_evac0, gw + 1 + FREE)
                    else:
                        pe.wait_ge(t_evac1, gw + 1 + FREE)
                    for h in range(2):
                        hp = 2 * a + h
                        for kt in range(2):
                            last = nc.tensor.matmul(ps[32 * hp:32 * hp + 32, 6, 0:C], vsel[:, i, kt, 32 * hp:32 * hp + 32],
                                                    probT[:, BUF[i], a, h, kt, :], start=(kt == 0), stop=(kt == 1))
                    if a == 1:
                        last.then_inc(pv_done, 1)

                def window_row(b, g, first, final):
                    for i in range(NW):
                        w = g * NW + i
                        more = not (final and i == NW - 1)
                        before = not (first and i == 0)
                        pg, pi = (g, i - 1) if i else (g - 1, NW - 1)
                        if more:
                            scores(b, w + 1, (i + 1) % NW, (0, 1))
                        transposes(b, w, i, 0)
                        if before:
                            values(b, pg, pi, 0)
                        if more:
                            scores(b, w + 1, (i + 1) % NW, (2, 3))
                        transposes(b, w, i, 1)
                        if before:
                            values(b, pg, pi, 1)

                with pe.Fori(0, NIMG) as b:
                    pe.wait_ge(x_loaded, 16 * b + 16)
                    pe.wait_ge(u_evac0, 8 * b + FREE)
                    pe.wait_ge(u_evac1, 8 * b + FREE)
                    layer_norm(b, 0)
                    for k in range(NW):
                        p = 4 * (k % 2)
                        xk = xn[:, k * ROW:(k + 1) * ROW]
                        if k == 0:
                            pe.wait_ge(normed, 14 * b + 7 + FREE)
                        if k >= 2:
                            pe.wait_ge(vt_done, 14 * b + 2 * k - 2)
                            pe.wait_ge(k_done, 7 * b + k - 1)
                            pe.wait_ge(v_done, 7 * b + k - 1)
                        nc.tensor.matmul(ps[:, p, 0:ROW], wqkv[:, 0:C], xk, start=True, stop=True).then_inc(qkv_ready, 1)
                        nc.tensor.matmul(ps[:, p + 1, 0:ROW], wqkv[:, C:2 * C], xk, start=True, stop=True).then_inc(qkv_ready, 1)
                        nc.tensor.matmul(ps[:, p + 2, 0:ROW], wqkv[:, 2 * C:], by_image(xk), start=True, stop=True).then_inc(qkv_ready, 1)
                        for part, (first, n, bank) in enumerate(((0, 4, p + 3), (4, 3, p))):
                            if part == 1:
                                pe.wait_ge(q_done, 7 * b + k + 1)
                            for i in range(n):
                                win = xk[:, (first + i) * WT:(first + i + 1) * WT]
                                last = nc.tensor.matmul(ps[0:WT, bank, i * C:(i + 1) * C], win, wqkv[:, 2 * C:],
                                                        start=True, stop=True)
                            last.then_inc(qkv_ready, 1)
                    pe.wait_ge(sums_done, 14 * b + 14)
                    pe.wait_ge(vt_done, 14 * b + 14)
                    pe.wait_ge(v_done, 7 * b + 7)
                    nc.tensor.matmul(ps[0:NWIN, 0, 0:NWIN], qsum[:], ksum[:], start=True, stop=True).then_inc(logit_ready, 1)
                    scores(b, 0, 0, (0, 1, 2, 3))
                    window_row(b, 0, True, False)
                    with pe.Fori(1, NW - 1) as g:
                        window_row(b, g, False, False)
                    window_row(b, NW - 1, False, True)
                    values(b, NW - 1, NW - 1, 0)
                    values(b, NW - 1, NW - 1, 1)
                    pe.wait_ge(lepe_done, 63 * b + 63)
                    pe.wait_ge(o_evac, NWIN * b + NWIN + FREE)
                    for k in range(NW):
                        if k >= 2:
                            pe.wait_ge(x2_ready, 7 * b + k - 1)
                        nc.tensor.matmul(ps[:, 4 + k % 2, 0:ROW], wo[:], by_image(image(oT, k)), start=True, stop=False)
                        nc.tensor.matmul(ps[:, 4 + k % 2, 0:ROW], wo[:], image(xn, k), start=False, stop=True).then_inc(proj_ready, 1)
                    layer_norm(b, 1)
                    pe.wait_ge(normed, 14 * b + 14 + FREE)
                    for t in range(2 * NT):
                        nt, half = t // 2, t % 2
                        if t >= 4:
                            if t % 2 == 0:
                                pe.wait_ge(ut_evac0, 4 * b + t // 2 - 1)
                            else:
                                pe.wait_ge(ut_evac1, 4 * b + t // 2 - 1)
                        for r in range(4):
                            t0 = R * N1T * nt + 4 * half + r
                            src = xn[:, t0:t0 + R * (N1T - 1) + 1:R]
                            last = nc.tensor.transpose(ps[0:N1T, 4 + t % 4, r * C:(r + 1) * C], src, ident[:])
                        last.then_inc(tr_ready, 1)
                    pe.wait_ge(ut_evac0, 4 * b + 4)
                    pe.wait_ge(ut_evac1, 4 * b + 4)
                    for s in range(2 * NFT):
                        ft, c = s // 2, s % 2
                        for half in range(2):
                            q = 2 * s + half
                            if q >= 4:
                                if half == 0:
                                    pe.wait_ge(u_evac0, 8 * b + s - 1 + FREE)
                                else:
                                    pe.wait_ge(u_evac1, 8 * b + s - 1 + FREE)
                            for nt in range(NT):
                                last = nc.tensor.matmul(ps[0:FT, q % 4, :], dft[:, nt, c, ft * FT:(ft + 1) * FT],
                                                        utok[:, nt, 4 * half:4 * half + 4, :], start=(nt == 0), stop=(nt == NT - 1))
                            last.then_inc(dft_ready, 1)

            @block.scalar
            def _(act):
                act.wait_ge(consts_loaded, 16 * 13)
                act.wait_ge(ready0, 3)
                nc.scalar.mul(bqs[:], bq[:], SCALE).then_inc(ready0, 1)
                act.wait_ge(ready0, 4)
                act.sem_inc(exp_done, 4)
                for s in (u_evac1, t_evac0, t_evac1):
                    act.sem_inc(s, FREE)

                def layer_norm(b, which):
                    for k in range(NW + 1):
                        if k < NW:
                            n = 14 * b + 7 * which + k
                            act.wait_ge(centered, n + 1)
                            if k >= 2:
                                act.wait_ge(var_ready, n - 1)
                            nc.scalar.activation(sq[:, k % 2, :], xc[:, k % 3, :], ACT.Square).then_inc(squared, 1)
                        if k >= 1:
                            m, j = 14 * b + 7 * which + k - 1, k - 1
                            act.wait_ge(var_ready, m + 1)
                            if j >= 2:
                                act.wait_ge(inverted, m - 1)
                            nc.scalar.activation(std[:, j % 2, :], ps[0:QT, 2 + j % 2, 0:4], ACT.Sqrt,
                                                 bias=epsc[0:QT, which:which + 1]).then_inc(std_ready, 1)

                def exps(b, w, i, hps):
                    u, gw = BUF[i], NWIN * b + w
                    for hp in hps:
                        act.wait_ge(max_done, 4 * gw + hp + 1)
                        nc.scalar.activation(prob[:, u, hp, :], ps[:, hp, 0:TOPK * WT], ACT.Exp,
                                             bias=nmax[:, u, hp:hp + 1], accum_out=rsum[:, u, hp:hp + 1]).then_inc(exp_done, 1)

                def even_heads(b, w):
                    gw = NWIN * b + w
                    act.wait_ge(pv_done, gw + 1 + NW)
                    act.wait_ge(o_evac, gw + FREE)
                    nc.scalar.activation(oeven[:], ps[:, 6, 0:WT], ACT.Copy, scale=hpar[:, 0:1]).then_inc(even_done, 1)

                def window_row(b, g, first, final):
                    for i in range(NW):
                        w = g * NW + i
                        gw = NWIN * b + w
                        more = not (final and i == NW - 1)
                        if more:
                            exps(b, w + 1, (i + 1) % NW, (0, 1))
                        act.wait_ge(t_ready, 2 * gw + 1)
                        act.wait_ge(pv_done, gw - 1 + NW)
                        nc.scalar.activation(probT[:, BUF[i], 0].rearrange("p a b c -> p (a b c)"), ps[:, 4, :], ACT.Copy).then_inc(t_evac0, 1)
                        if more:
                            exps(b, w + 1, (i + 1) % NW, (2, 3))
                        act.wait_ge(t_ready, 2 * gw + 2)
                        nc.scalar.activation(probT[:, BUF[i], 1].rearrange("p a b c -> p (a b c)"), ps[:, 5, :], ACT.Copy).then_inc(t_evac1, 1)
                        if not (first and i == 0):
                            even_heads(b, w - 1)

                with act.Fori(0, NIMG) as b:
                    layer_norm(b, 0)
                    for k in range(NW):
                        p = 4 * (k % 2)
                        act.wait_ge(qkv_ready, 35 * b + 5 * k + 1)
                        nc.scalar.activation(qT[:, k * ROW:(k + 1) * ROW], ps[:, p, 0:ROW], ACT.Identity,
                                             bias=bqs[:], scale=SCALE).then_inc(q_done, 1)
                        act.wait_ge(qkv_ready, 35 * b + 5 * k + 3)
                        nc.scalar.activation(vpad[:, 1 + k * WS:1 + (k + 1) * WS, 1:1 + HW],
                                             ps[:, p + 2, 0:ROW].rearrange("p (r c) -> p r c", r=WS), ACT.Identity,
                                             bias=bv[:]).then_inc(v_done, 1)
                    exps(b, 0, 0, (0, 1, 2, 3))
                    window_row(b, 0, True, False)
                    with act.Fori(1, NW - 1) as g:
                        window_row(b, g, False, False)
                    window_row(b, NW - 1, False, True)
                    even_heads(b, NWIN - 1)
                    layer_norm(b, 1)
                    for t in range(1, 2 * NT, 2):
                        act.wait_ge(tr_ready, 8 * b + t + 1)
                        nc.scalar.activation(utok[:, t // 2, 4:8, :].rearrange("p a b -> p (a b)"), ps[0:N1T, 4 + t % 4, :], ACT.Copy).then_inc(ut_evac1, 1)
                    for s in range(2 * NFT):
                        act.wait_ge(dft_ready, 16 * b + 2 * s + 2)
                        act.wait_ge(u_stored[s % 2], 16 * (4 * b + s // 2) + 16 * FREE)
                        nc.scalar.activation(ustage[:, s % 2, 512:1024], ps[0:FT, (2 * s + 1) % 4, :], ACT.Copy).then_inc(u_evac1, 1)

            @block.vector
            def _(dve):
                for s in (normed, u_evac0, o_evac):
                    dve.sem_inc(s, FREE)
                dve.wait_ge(consts_loaded, 16 * 13)
                dve.wait_ge(ready0, 4)

                def layer_norm(b, which):
                    for k in range(NW + 2):
                        n = 14 * b + 7 * which + k
                        if k < NW:
                            dve.wait_ge(mean_ready, n + 1)
                            if k >= 3:
                                dve.wait_ge(normed, n - 2 + FREE)
                            nc.vector.tensor_tensor(xc[:, k % 3, :], image(xs, k), ps[:, k % 2, 0:ROW], ALU.subtract).then_inc(centered, 1)
                        if 1 <= k <= NW:
                            dve.wait_ge(std_ready, n)
                            if k >= 3:
                                dve.wait_ge(spread_ready, n - 2)
                            nc.vector.reciprocal(rstd[:, (k - 1) % 2, :], std[:, (k - 1) % 2, :]).then_inc(inverted, 1)
                        if k >= 2:
                            dve.wait_ge(spread_ready, n - 1)
                            dst = image(xn, k - 2) if which else by_image(image(xn, k - 2))
                            centre, scale = xc[:, (k - 2) % 3, :], ps[:, 6 + k % 2, 0:ROW]
                            if not which:
                                centre, scale = (v.rearrange("p (y n x) -> p y n x", y=WS, n=NW) for v in (centre, scale))
                            nc.vector.tensor_tensor(dst, centre, scale, ALU.mult).then_inc(normed, 1)

                def maxima(b, w, i, hps):
                    u, gw = BUF[i], NWIN * b + w
                    for hp in hps:
                        dve.wait_ge(s_ready, 4 * gw + hp + 1)
                        nc.vector.tensor_reduce(nmax[:, u, hp:hp + 1], ps[:, hp, 0:TOPK * WT], AX.X, ALU.max,
                                                negate=True).then_inc(max_done, 1)

                def positional(b, g, taps):
                    acc = xn[:, bass.ds(g * ROW, ROW)].rearrange("p (r c) -> p r c", r=WS)
                    for tap in taps:
                        src = vpad[:, bass.ds(g * WS + tap // 3, WS), tap % 3:tap % 3 + HW]
                        n = 63 * b + 9 * g + tap
                        if tap == 0:
                            nc.vector.tensor_scalar(acc, src, lw[:, 0:1], lb[:], ALU.mult, ALU.add).then_inc(lepe_done, 1)
                        else:
                            dve.wait_ge(lepe_done, n)
                            nc.vector.scalar_tensor_tensor(acc, src, lw[:, tap:tap + 1], acc, ALU.mult, ALU.add).then_inc(lepe_done, 1)

                def normalise(b, w, i, hps):
                    u, gw = BUF[i], NWIN * b + w
                    first, n = hps[0], len(hps)
                    dve.wait_ge(exp_done, 4 * gw + first + n + 4)
                    nc.vector.reciprocal(rinv[:, u, first:first + n], rsum[:, u, first:first + n]).then_inc(rinv_done, n)
                    dve.wait_ge(rinv_done, 4 * gw + first + n)
                    for hp in hps:
                        nc.vector.tensor_scalar(prob[:, u, hp, :], prob[:, u, hp, :], rinv[:, u, hp:hp + 1], None,
                                                ALU.mult).then_inc(norm_done, 1)

                def odd_heads(b, w):
                    gw = NWIN * b + w
                    dve.wait_ge(even_done, gw + 1)
                    nc.vector.scalar_tensor_tensor(oT[:, bass.ds(w * WT, WT)], ps[:, 6, WT:2 * WT], hpar[:, 1:2], oeven[:],
                                                   ALU.mult, ALU.add).then_inc(o_evac, 1)

                def window_row(b, g, first, final):
                    for i in range(NW):
                        w = g * NW + i
                        gw = NWIN * b + w
                        more = not (final and i == NW - 1)
                        if more:
                            maxima(b, w + 1, (i + 1) % NW, (0, 1))
                        if more:
                            normalise(b, w + 1, (i + 1) % NW, (0, 1))
                            maxima(b, w + 1, (i + 1) % NW, (2, 3))
                        positional(b, g, ([0, 1], [2], [3], [4], [5], [6], [7, 8])[i])
                        if more:
                            normalise(b, w + 1, (i + 1) % NW, (2, 3))
                        if not (first and i == 0):
                            odd_heads(b, w - 1)

                with dve.Fori(0, NIMG) as b:
                    layer_norm(b, 0)
                    for k in range(NW):
                        p = 4 * (k % 2)
                        dve.wait_ge(qkv_ready, 35 * b + 5 * k + 2)
                        kk = kT[:, k * ROW:(k + 1) * ROW]
                        nc.vector.tensor_scalar(kk, ps[:, p + 1, 0:ROW], bk[:], None, ALU.add).then_inc(k_done, 1)
                        for part, (first, n, bank) in enumerate(((0, 4, p + 3), (4, 3, p))):
                            dve.wait_ge(qkv_ready, 35 * b + 5 * k + 4 + part)
                            nc.vector.tensor_tensor(vtok[:, k * NW + first:k * NW + first + n, :],
                                                    ps[0:WT, bank, 0:n * C].rearrange("p (w c) -> p w c", w=n),
                                                    bvrow[0:WT, :].unsqueeze(1).to_broadcast([WT, n, C]), ALU.add).then_inc(vt_done, 1)
                        dve.wait_ge(k_done, 7 * b + k + 1)
                        nc.vector.tensor_reduce(ksum[:, k * NW:(k + 1) * NW], kk.rearrange("p (w t) -> p w t", w=NW), AX.X, ALU.add).then_inc(sums_done, 1)
                        dve.wait_ge(q_done, 7 * b + k + 1)
                        nc.vector.tensor_reduce(qsum[:, k * NW:(k + 1) * NW], qT[:, k * ROW:(k + 1) * ROW].rearrange("p (w t) -> p w t", w=NW),
                                                AX.X, ALU.add).then_inc(sums_done, 1)
                    dve.wait_ge(logit_ready, b + 1)
                    dve.wait_ge(route_stored, 16 * b + 16 * FREE)
                    nc.vector.tensor_copy(logit[:], ps[0:NWIN, 0, 0:NWIN]).then_inc(topk_step, 1)
                    dve.wait_ge(topk_step, 3 * b + 1)
                    alone(dve)
                    nc.vector.max(top[:], logit[:]).then_inc(topk_step, 1)
                    dve.wait_ge(topk_step, 3 * b + 2)
                    alone(dve)
                    nc.vector.max_index(topi[:], top[:], logit[:]).then_inc(topk_step, 1)
                    maxima(b, 0, 0, (0, 1, 2, 3))
                    normalise(b, 0, 0, (0, 1, 2, 3))
                    dve.wait_ge(v_done, 7 * b + 7)
                    alone(dve)
                    window_row(b, 0, True, False)
                    with dve.Fori(1, NW - 1) as g:
                        window_row(b, g, False, False)
                    window_row(b, NW - 1, False, True)
                    odd_heads(b, NWIN - 1)
                    for k in range(NW):
                        dve.wait_ge(proj_ready, 7 * b + k + 1)
                        nc.vector.scalar_tensor_tensor(image(xs, k), ps[:, 4 + k % 2, 0:ROW], bo[:], image(xs, k),
                                                       ALU.add, ALU.add).then_inc(x2_ready, 1)
                    layer_norm(b, 1)
                    for t in range(0, 2 * NT, 2):
                        dve.wait_ge(tr_ready, 8 * b + t + 1)
                        nc.vector.tensor_copy(utok[:, t // 2, 0:4, :].rearrange("p a b -> p (a b)"), ps[0:N1T, 4 + t % 4, :]).then_inc(ut_evac0, 1)
                    for s in range(2 * NFT):
                        dve.wait_ge(dft_ready, 16 * b + 2 * s + 1)
                        dve.wait_ge(u_stored[s % 2], 16 * (4 * b + s // 2) + 16 * FREE)
                        nc.vector.tensor_copy(ustage[:, s % 2, 0:512], ps[0:FT, (2 * s) % 4, :]).then_inc(u_evac0, 1)


def filter_and_product(nc, phi_d, sigma_d, mu_d, mp_d, mm_d, logw_d, gumbel_d, cst, prefix, spec_d, prod_d):
    with ExitStack() as ctx:
        def sb(name, shape, dt=F32):
            return ctx.enter_context(nc.sbuf_tensor(name, shape, dt))

        def sem(name):
            return ctx.enter_context(nc.semaphore(name))

        NB = NIMG
        Q = 2 * NB * R
        ms = sb("ms", [KP, 2, C, C], BF16)
        vs = sb("vs", [KP, NCH, 2, 4, 2, FC], BF16)
        ps = ctx.enter_context(nc.psum_tensor("psb", [C, 8, 512], F32))

        with ExitStack() as prep:
            def sbp(name, shape, dt=F32):
                return prep.enter_context(nc.sbuf_tensor(name, shape, dt))

            def semp(name):
                return prep.enter_context(nc.semaphore(name))

            MC, NMC = 2048, C * C // 2048
            UN = MC // 512
            lg = sbp("lg", [C, 2, 4])
            soft = sbp("soft", [C, 8, 4])
            col = sbp("col", [C, 8])
            sig = sbp("sig", [C, 1])
            own = sbp("own", [C, 8])
            part = sbp("part", [KP, 4])
            sel = sbp("selm", [C, 2, KP])
            selu = sbp("selu", [12, KP])
            phi = sbp("phi", [N1T, NT * R, 16])
            delta = sbp("deltas", [N1T, NT * R, 3])
            phir = sbp("phir", [N1T, NT * R, COPIES, KF])
            dft = sbp("dftb", [N1T, NT, 2, NF])
            mat = sbp("mat", [C, 2, MC])
            matu = sbp("matu", [12, 2, MC])
            hi = sbp("hi", [KP, 2, 512], BF16)
            rest = sbp("rest", [KP, 2, 512])
            mid = sbp("mid", [KP, 2, 512], BF16)
            loaded, sm, sel_ready, phi_ready, ssig = map(semp, ("b_loaded", "b_small", "b_sel", "b_phi", "b_sig"))
            smx, sma = semp("b_smx"), semp("b_sma")
            mat_loaded = [semp("mat_loaded0"), semp("mat_loaded1")]
            unit_ready, hi_done, rest_done, mid_done, split_done = map(
                semp, ("unit_ready", "hi_done", "rest_done", "mid_done", "split_done"))
            NV = 2 * R
            NUNIT = NV + 2 * UN * NMC

            with nc.Block() as block:
                @block.sync
                def _(sp):
                    loads = [(lg[:, 0, :], logw_d.partition_broadcast(C)), (lg[:, 1, :], gumbel_d.partition_broadcast(C)),
                             (own[:], cst["own_variant"]), (part[:], cst["part"]),
                             (sel[:].rearrange("p a b -> p (a b)"), cst["sel"]), (selu[:], cst["sel_u"]),
                             (delta[:].rearrange("p a b -> p (a b)"), cst["delta"]),
                             (dft[:].rearrange("p a b c -> p (a b c)"), cst["dft"])]
                    loads += [(sig[16 * i:16 * i + 16, :], sigma_d.unsqueeze(1)) for i in range(8)]
                    loads += [(phi[:, nt * R:(nt + 1) * R, :].rearrange("p a b -> p (a b)"),
                               phi_d[nt * N1T * R:(nt + 1) * N1T * R, :].rearrange("(n r) k -> n (r k)", r=R)) for nt in range(NT)]
                    assert len(loads) == 20
                    for dst, src in loads:
                        sp.dma_start(dst, src).then_inc(loaded, 16)
                    for m in range(NMC):
                        if m >= 2:
                            sp.wait_ge(unit_ready, NV + 2 * UN * (m - 1))
                        cols = slice(m * MC, (m + 1) * MC)
                        for dst, src in ((mat[0:64, m % 2, :], mp_d[:, cols]), (mat[64:128, m % 2, :], mm_d[:, cols]),
                                         (matu[:, m % 2, :], mu_d[:, cols])):
                            sp.dma_start(dst, src).then_inc(mat_loaded[m % 2], 16)

                @block.gpsimd
                def _(pool):
                    pool.wait_ge(loaded, 16 * 20)
                    for cpy in range(COPIES):
                        nc.gpsimd.tensor_copy(phir[:, :, cpy, 0:16], phi[:]).then_inc(phi_ready, 1)
                        nc.gpsimd.tensor_copy(phir[:, :, cpy, 16:KF], delta[:]).then_inc(phi_ready, 1)

                @block.tensor
                def _(pe):
                    pe.wait_ge(phi_ready, 2 * COPIES)
                    for u in range(NV):
                        s, c = u // 2, u % 2
                        if u >= 2:
                            pe.wait_ge(hi_done, u - 1)
                            pe.wait_ge(rest_done, u - 1)
                        for nt in range(NT):
                            last = nc.tensor.matmul(ps[0:KP, u % 2, 0:NF], phir[:, nt * R + s, :, :].rearrange("p a b -> p (a b)"),
                                                    dft[:, nt, c, :], start=(nt == 0), stop=(nt == NT - 1))
                        last.then_inc(unit_ready, 1)
                    pe.wait_ge(sel_ready, 2)
                    for u in range(NV, NUNIT):
                        m, rem = (u - NV) // (2 * UN), (u - NV) % (2 * UN)
                        odd, cols = rem // UN, slice((rem % UN) * 512, (rem % UN + 1) * 512)
                        if rem == 0:
                            pe.wait_ge(mat_loaded[m % 2], 48 * (m // 2 + 1))
                        pe.wait_ge(hi_done, u - 1)
                        pe.wait_ge(rest_done, u - 1)
                        nc.tensor.matmul(ps[0:KP, u % 2, :], sel[:, odd, :], mat[:, m % 2, cols], start=True, stop=False)
                        nc.tensor.matmul(ps[0:KP, u % 2, :], selu[:], matu[:, m % 2, cols], start=False, stop=True).then_inc(unit_ready, 1)

                def width(u):
                    return NF if u < NV else 512

                @block.scalar
                def _(act):
                    act.wait_ge(loaded, 16 * 20)
                    nc.scalar.activation(col[:, 0:1], sig[:], ACT.Sqrt).then_inc(ssig, 1)
                    act.wait_ge(ssig, 1)
                    nc.scalar.activation(col[:, 1:2], col[:, 0:1], ACT.Sqrt).then_inc(ssig, 1)
                    act.wait_ge(smx, 1)
                    nc.scalar.activation(soft[:, 1, :], soft[:, 0, :], ACT.Exp, bias=col[:, 2:3], accum_out=col[:, 3:4]).then_inc(sma, 1)
                    for u in range(NUNIT + 1):
                        if u < NUNIT:
                            act.wait_ge(unit_ready, u + 1)
                            if u >= 2:
                                act.wait_ge(rest_done, u - 1)
                            nc.scalar.activation(hi[:, u % 2, 0:width(u)], ps[0:KP, u % 2, 0:width(u)], ACT.Copy).then_inc(hi_done, 1)
                        if u >= 1:
                            v = u - 1
                            act.wait_ge(rest_done, v + 1)
                            if v >= 2:
                                act.wait_ge(split_done, v - 1)
                            nc.scalar.activation(mid[:, v % 2, 0:width(v)], rest[:, v % 2, 0:width(v)], ACT.Copy).then_inc(mid_done, 1)

                @block.vector
                def _(dve):
                    steps = [0]

                    def then(ins):
                        steps[0] += 1
                        ins.then_inc(sm, 1)
                        dve.wait_ge(sm, steps[0])

                    dve.wait_ge(loaded, 16 * 20)
                    v = nc.vector
                    then(v.tensor_tensor(soft[:, 0, :], lg[:, 0, :], lg[:, 1, :], ALU.add))
                    v.tensor_reduce(col[:, 2:3], soft[:, 0, :], AX.X, ALU.max, negate=True).then_inc(smx, 1)
                    dve.wait_ge(sma, 1)
                    then(v.reciprocal(col[:, 4:5], col[:, 3:4]))
                    then(v.tensor_scalar(soft[:, 2, :], soft[:, 1, :], col[:, 4:5], None, ALU.mult))
                    then(v.tensor_reduce(col[:, 5:6], soft[:, 2, :], AX.X, ALU.max))
                    then(v.tensor_scalar(soft[:, 3, :], soft[:, 2, :], col[:, 5:6], None, ALU.is_ge))
                    then(v.tensor_scalar(soft[:, 4, :], soft[:, 3, :], -1.0, 1.0, ALU.mult, ALU.add))
                    for i in range(1, 4):
                        then(v.tensor_tensor(soft[:, 3, i:i + 1], soft[:, 3, i:i + 1], soft[:, 4, i - 1:i], ALU.mult))
                        then(v.tensor_tensor(soft[:, 4, i:i + 1], soft[:, 4, i:i + 1], soft[:, 4, i - 1:i], ALU.mult))
                    then(v.tensor_copy(prefix[:, 0:1], soft[:, 3, 0:1]))
                    for i in range(1, 4):
                        then(v.tensor_tensor(prefix[:, i:i + 1], prefix[:, i - 1:i], soft[:, 3, i:i + 1], ALU.add))
                    then(v.tensor_tensor(soft[:, 5, :], soft[:, 3, :], soft[:, 2, :], ALU.subtract))
                    then(v.tensor_tensor(soft[:, 6, :], soft[:, 5, :], soft[:, 2, :], ALU.add))
                    for i in range(2):
                        then(v.tensor_tensor(soft[:, 7, :], soft[:, 6, :], own[:, 4 * i:4 * i + 4], ALU.mult))
                        then(v.tensor_reduce(col[:, 6 + i:7 + i], soft[:, 7, :], AX.X, ALU.add))
                    dve.wait_ge(ssig, 2)
                    then(v.tensor_tensor(col[:, 6:7], col[:, 6:7], col[:, 1:2], ALU.mult))
                    v.tensor_scalar(sel[:], sel[:], col[:, 6:7], None, ALU.mult).then_inc(sel_ready, 1)
                    v.tensor_scalar(selu[:], selu[:], col[0:12, 7:8], None, ALU.mult).then_inc(sel_ready, 1)
                    for u in range(NUNIT + 1):
                        if u < NUNIT:
                            w, lv = width(u), (0 if u < NV else 2)
                            dve.wait_ge(hi_done, u + 1)
                            if u >= 2:
                                dve.wait_ge(split_done, u - 1)
                            v.scalar_tensor_tensor(rest[:, u % 2, 0:w], hi[:, u % 2, 0:w], part[:, lv:lv + 1],
                                                   ps[0:KP, u % 2, 0:w], ALU.mult, ALU.add).then_inc(rest_done, 1)
                        if u >= 1:
                            q = u - 1
                            w, lv = width(q), (0 if q < NV else 2)
                            dve.wait_ge(mid_done, q + 1)
                            dve.wait_ge(rest_done, q + 1)
                            if q < NV:
                                s, c = q // 2, q % 2
                                dst = vs[:, :, s % 2, s // 2, c, :]
                                a, b = (z[:, q % 2, 0:w].rearrange("p (h f) -> p h f", f=FC) for z in (mid, rest))
                            else:
                                m, rem = (q - NV) // (2 * UN), (q - NV) % (2 * UN)
                                d0 = (m * UN + rem % UN) * 4
                                dst = ms[:, rem // UN, :, d0:d0 + 4].rearrange("p e d -> p d e")
                                a, b = (z[:, q % 2, 0:w].rearrange("p (d e) -> p d e", e=C) for z in (mid, rest))
                            v.scalar_tensor_tensor(dst, a, part[:, lv + 1:lv + 2], b, ALU.mult, ALU.add).then_inc(split_done, 1)

        gf = sb("gf", [C, FC, 16, C])
        ux = sb("ux", [C, FC, 3, NB, RX])
        tw = sb("tw", [C, 2, FC, 2 * NB, R - 1])
        vcur = sb("vcur", [KP, 2, 64], BF16)
        tcur = sb("tcur", [C, 2, FC])
        xin = sb("xin", [Q, FC, C])
        ye = sb("ye", [C, FC, Q])
        yst = sb("yst", [Q, FC, C])
        ident = sb("identb", [C, C])
        twist = sb("twist", [C, 2, NF])
        cl, x_in, xtr_ready, ux_plain, twist_step, vcur_ready = map(
            sem, ("bc_loaded", "x_in", "xtr_ready", "ux_plain", "twist_step", "vcur_ready"))
        g_ready, g_evac0, g_evac1, y_ready, ye_evac, ytr_ready, yst_evac, y_stored = map(
            sem, ("g_ready", "g_evac0", "g_evac1", "y_ready", "ye_evac", "ytr_ready", "yst_evac", "y_stored"))

        with nc.Block() as block:
            @block.sync
            def _(sp):
                sp.sem_inc(y_stored, 16 * FREE)
                sp.dma_start(ident[:], cst["ident"]).then_inc(cl, 16)
                sp.dma_start(twist[:].rearrange("p a b -> p (a b)"), cst["twist"]).then_inc(cl, 16)
                with sp.Fori(0, NCH) as ch:
                    sp.wait_ge(xtr_ready, 2 * ch + FREE)
                    sp.dma_start(xin[:], spec_d[bass.ds(ch * FC, FC)].rearrange("f c b n -> f (c b n)").rearrange("f (q d) -> q f d", d=C)).then_inc(x_in, 16)
                    sp.wait_ge(yst_evac, 2 * ch + 2 + FREE)
                    sp.dma_start(prod_d[bass.ds(ch * FC, FC)].rearrange("f q e -> q f e"), yst[:]).then_inc(y_stored, 16)
                sp.wait_ge(y_stored, 16 * NCH + 16 * FREE)

            @block.gpsimd
            def _(pool):
                pool.sem_inc(twist_step, FREE)
                pool.wait_ge(cl, 32)

                def kb(v):
                    return v.rearrange("p f k b r -> p f (k b) r")

                with pool.Fori(0, NCH) as ch:
                    pool.wait_ge(ux_plain, 4 * ch + 4)
                    pool.wait_ge(vcur_ready, 2 * ch + 2)
                    cs, sn = (tcur[:, z, :].unsqueeze(2).unsqueeze(3) for z in range(2))
                    dims = [C, FC, 2 * NB, R - 1]
                    half = [C, FC, NB, R - 1]
                    nc.gpsimd.tensor_tensor(tw[:, 0], kb(ux[:, :, 0:2, :, R:RX]), cs.to_broadcast(dims), ALU.mult).then_inc(twist_step, 1)
                    nc.gpsimd.tensor_tensor(tw[:, 1], kb(ux[:, :, 1:3, :, R:RX]), sn.to_broadcast(dims), ALU.mult).then_inc(twist_step, 1)
                    pool.wait_ge(twist_step, 6 * ch + 2 + FREE)
                    nc.gpsimd.tensor_tensor(kb(ux[:, :, 0:2, :, 0:R - 1]), tw[:, 0], tw[:, 1], ALU.add).then_inc(twist_step, 1)
                    pool.wait_ge(twist_step, 6 * ch + 3 + FREE)
                    nc.gpsimd.tensor_tensor(tw[:, 0, :, 0:NB, :], ux[:, :, 2, :, R:RX], cs.to_broadcast(half), ALU.mult).then_inc(twist_step, 1)
                    nc.gpsimd.tensor_tensor(tw[:, 1, :, 0:NB, :], ux[:, :, 1, :, R:RX], sn.to_broadcast(half), ALU.mult).then_inc(twist_step, 1)
                    pool.wait_ge(twist_step, 6 * ch + 5 + FREE)
                    nc.gpsimd.tensor_tensor(ux[:, :, 2, :, 0:R - 1], tw[:, 0, :, 0:NB, :], tw[:, 1, :, 0:NB, :], ALU.subtract).then_inc(twist_step, 1)

            @block.tensor
            def _(pe):
                for s in (xtr_ready, y_ready, ytr_ready):
                    pe.sem_inc(s, FREE)
                pe.wait_ge(cl, 32)
                with pe.Fori(0, NCH) as ch:
                    pe.wait_ge(x_in, 16 * ch + 16)
                    pe.wait_ge(yst_evac, 2 * ch + FREE)
                    for half in range(2):
                        for f in range(4):
                            last = nc.tensor.transpose(ps[:, half, f * Q:(f + 1) * Q], xin[:, 4 * half + f, :], ident[0:Q, 0:Q])
                        last.then_inc(xtr_ready, 1)
                    pe.wait_ge(vcur_ready, 2 * ch + 1)
                    for blk in range(32):
                        if blk < 4:
                            if blk % 2 == 0:
                                pe.wait_ge(g_evac0, 16 * ch + FREE)
                            else:
                                pe.wait_ge(g_evac1, 16 * ch + FREE)
                        elif blk % 2 == 0:
                            pe.wait_ge(g_evac0, 16 * ch + blk // 2 - 1 + FREE)
                        else:
                            pe.wait_ge(g_evac1, 16 * ch + blk // 2 - 1 + FREE)
                        for e in range(4):
                            for odd in range(2):
                                o = (2 * e + odd) * 64
                                last = nc.tensor.matmul(ps[:, 2 + blk % 4, o:o + 64], ms[:, odd, 4 * blk + e, :], vcur[:, odd, :],
                                                        start=True, stop=True)
                        last.then_inc(g_ready, 1)
                    pe.wait_ge(g_evac0, 16 * ch + 16 + FREE)
                    pe.wait_ge(g_evac1, 16 * ch + 16 + FREE)
                    pe.wait_ge(twist_step, 6 * ch + 6 + FREE)
                    for half in range(2):
                        pe.wait_ge(ye_evac, 2 * ch + half + FREE)
                        for f in range(4):
                            fi = 4 * half + f
                            for m in range(16):
                                odd, sp_, c = m // 8, (m % 8) // 2, m % 2
                                s = 2 * sp_ + odd
                                parts = slice(1, 3) if c == 0 else slice(0, 2)
                                last = nc.tensor.matmul(ps[:, 6 + half, f * Q:(f + 1) * Q], gf[:, fi, m, :],
                                                        ux[:, fi, parts, :, R - 1 - s:RX - s].rearrange("p k b r -> p (k b) r"),
                                                        start=(m == 0), stop=(m == 15))
                        last.then_inc(y_ready, 1)
                    for half in range(2):
                        pe.wait_ge(ye_evac, 2 * ch + half + 1 + FREE)
                        for f in range(4):
                            last = nc.tensor.transpose(ps[0:Q, half, f * C:(f + 1) * C], ye[:, 4 * half + f, :], ident[:])
                        last.then_inc(ytr_ready, 1)

            def spread(blk):
                return (gf[:, :, :, 4 * blk:4 * blk + 4].rearrange("p f m e -> p e m f"),
                        ps[:, 2 + blk % 4, :].rearrange("p (e m f) -> p e m f", e=4, f=FC))

            @block.scalar
            def _(act):
                for s in (g_evac1, ye_evac):
                    act.sem_inc(s, FREE)
                with act.Fori(0, NCH) as ch:
                    for half in range(2):
                        fs = slice(4 * half, 4 * half + 4)
                        act.wait_ge(xtr_ready, 2 * ch + half + 1 + FREE)
                        act.wait_ge(y_ready, 2 * ch + FREE)
                        nc.scalar.activation(ux[:, fs, 1:3, :, R - 1:RX].rearrange("p f k b r -> p f (k b) r"),
                                             ps[:, half, 0:4 * Q].rearrange("p (f q r) -> p f q r", f=4, r=R), ACT.Copy).then_inc(ux_plain, 1)
                        nc.scalar.activation(ux[:, fs, 0, :, R - 1:RX],
                                             ps[:, half, 0:4 * Q].rearrange("p (f c b r) -> p f c b r", f=4, c=2, b=NB)[:, :, 1],
                                             ACT.Copy, scale=-1.0).then_inc(ux_plain, 1)
                    for blk in range(1, 32, 2):
                        act.wait_ge(g_ready, 32 * ch + blk + 1)
                        dst, src = spread(blk)
                        nc.scalar.activation(dst, src, ACT.Copy).then_inc(g_evac1, 1)
                    for half in range(2):
                        act.wait_ge(y_ready, 2 * ch + half + 1 + FREE)
                        act.wait_ge(ytr_ready, 2 * ch + FREE)
                        nc.scalar.activation(ye[:, 4 * half:4 * half + 4, :].rearrange("p f q -> p (f q)"), ps[:, 6 + half, 0:4 * Q], ACT.Copy).then_inc(ye_evac, 1)

            @block.vector
            def _(dve):
                for s in (g_evac0, yst_evac):
                    dve.sem_inc(s, FREE)
                dve.wait_ge(cl, 32)
                with dve.Fori(0, NCH) as ch:
                    dve.wait_ge(y_ready, 2 * ch + FREE)
                    nc.vector.tensor_copy(vcur[:].unsqueeze(1), vs[:, bass.ds(ch, 1)].rearrange("p a o s c f -> p a o (s c f)")).then_inc(vcur_ready, 1)
                    dve.wait_ge(twist_step, 6 * ch + FREE)
                    nc.vector.tensor_copy(tcur[:], twist[:, :, bass.ds(ch * FC, FC)]).then_inc(vcur_ready, 1)
                    for blk in range(0, 32, 2):
                        dve.wait_ge(g_ready, 32 * ch + blk + 1)
                        dst, src = spread(blk)
                        nc.vector.tensor_copy(dst, src).then_inc(g_evac0, 1)
                    dve.wait_ge(y_stored, 16 * ch + 16 * FREE)
                    for half in range(2):
                        dve.wait_ge(ytr_ready, 2 * ch + half + 1 + FREE)
                        nc.vector.tensor_copy(yst[:, 4 * half:4 * half + 4, :].rearrange("p f e -> p (f e)"), ps[0:Q, half, :]).then_inc(yst_evac, 1)


def inverse_and_store(nc, cst, prefix, prod_d, x2_d, out_d):
    with ExitStack() as ctx:
        def sb(name, shape, dt=F32):
            return ctx.enter_context(nc.sbuf_tensor(name, shape, dt))

        def sem(name):
            return ctx.enter_context(nc.semaphore(name))

        idft = sb("idft", [FT, NFT, 2, N1])
        yin = sb("yin", [FT, 2, NFT, 2, R * C])
        x2 = sb("x2", [C, 2, T])
        ps = ctx.enter_context(nc.psum_tensor("psc", [C, 8, 512], F32))
        cl, masked, z_ready, x3_done = map(sem, ("cc_loaded", "masked", "z_ready", "x3_done"))
        y_in, x2_in, stored = ([sem(f"{n}{z}") for z in range(2)] for n in ("y_in", "x2_in", "stored"))
        REACH = [(0, N1 // 8, 3), (N1 // 8, N1 // 4, 2), (N1 // 4, N1 // 2, 1), (N1 // 2, N1, 0)]
        with nc.Block() as block:
            @block.sync
            def _(sp):
                sp.dma_start(idft[:].rearrange("p a b c -> p (a b c)"), cst["idft"]).then_inc(cl, 16)
                with sp.Fori(0, NIMG // 2) as p:
                    for z in range(2):
                        b = 2 * p + z
                        sp.wait_ge(z_ready, 8 * b + 8)
                        for ft in range(NFT):
                            sp.dma_start(yin[:, z, ft], prod_d[ft * FT:(ft + 1) * FT].rearrange("f (c b r) e -> f c b (r e)", c=2, r=R)[:, :, bass.ds(b, 1), :]
                                         .rearrange("f c b n -> f (c b) n")).then_inc(y_in[z], 16)
                        sp.wait_ge(stored[z], 16 * p + 16 * FREE)
                        sp.dma_start(x2[:, z], x2_d[bass.ds(b, 1)].rearrange("a c t -> (a c) t")).then_inc(x2_in[z], 16)

            @block.scalar
            def _(act):
                for z in range(2):
                    act.sem_inc(stored[z], 16 * FREE)
                with act.Fori(0, NIMG // 2) as p:
                    for z in range(2):
                        act.wait_ge(x3_done, 8 * (2 * p + z) + 16)
                        act.dma_start(out_d[bass.ds(2 * p + z, 1)].rearrange("a c t -> (a c) t"), x2[:, z]).then_inc(stored[z], 16)
                for z in range(2):
                    act.wait_ge(stored[z], 16 * (NIMG // 2) + 16 * FREE)

            @block.tensor
            def _(pe):
                pe.sem_inc(z_ready, 16)
                pe.wait_ge(masked, 4)
                with pe.Fori(0, NIMG // 2) as p:
                    for z in range(2):
                        pe.wait_ge(y_in[z], 16 * NFT * (p + 1))
                        for r in range(R):
                            pe.wait_ge(x3_done, 8 * (2 * p + z) + r + 1)
                            for q in range(2 * NFT):
                                ft, c = q // 2, q % 2
                                last = nc.tensor.matmul(ps[:, r, 0:N1], yin[:, z, ft, c, r * C:(r + 1) * C], idft[:, ft, c, :],
                                                        start=(q == 0), stop=(q == 2 * NFT - 1))
                            last.then_inc(z_ready, 1)

            @block.vector
            def _(dve):
                dve.sem_inc(x3_done, 8)
                dve.wait_ge(cl, 16)
                for a, b, i in REACH:
                    nc.vector.tensor_scalar(idft[:, :, :, a:b], idft[:, :, :, a:b], prefix[0:FT, i:i + 1], None, ALU.mult).then_inc(masked, 1)
                with dve.Fori(0, NIMG // 2) as p:
                    for z in range(2):
                        dve.wait_ge(x2_in[z], 16 * (p + 1))
                        for r in range(R):
                            dve.wait_ge(z_ready, 8 * (2 * p + z) + r + 1 + 16)
                            v = x2[:, z].rearrange("p (n r) -> p n r", r=R)[:, :, r]
                            nc.vector.tensor_tensor(v, v, ps[:, r, 0:N1], ALU.add).then_inc(x3_done, 1)


def program(nc, x, w_qkv, b_qkv, lepe_w, lepe_b, w_o, b_o, sigma, phi, m_u, m_plus, m_minus, log_weights, gumbel, cst, out):
    x2_d = nc.dram_tensor("x2_scratch", (NIMG, C, T), F32, kind="Internal").ap()
    spec_d = nc.dram_tensor("spectrum_scratch", (NF, 2, NIMG, R * C), F32, kind="Internal").ap()
    prod_d = nc.dram_tensor("product_scratch", (NF, 2 * NIMG * R, C), F32, kind="Internal").ap()
    route_d = nc.dram_tensor("route_scratch", (NIMG, NWIN * TOPK), U32, kind="Internal").ap()
    attention_and_dft(nc, x, w_qkv, b_qkv, lepe_w, lepe_b, w_o, b_o, cst, x2_d, spec_d, route_d)
    with nc.sbuf_tensor("prefix", [C, 4], F32) as prefix:
        filter_and_product(nc, phi, sigma, m_u, m_plus, m_minus, log_weights, gumbel, cst, prefix, spec_d, prod_d)
        inverse_and_store(nc, cst, prefix, prod_d, x2_d, out)


_INS = [("x", (NIMG, C, T)), ("L0_conv_W_qkv", (C, 3 * C)), ("L0_conv_b_qkv", (3 * C,)), ("L0_conv_lepe_w", (C, 9)),
        ("L0_conv_lepe_b", (C,)), ("L0_conv_W_o", (C, C)), ("L0_conv_b_o", (C,)), ("L0_ffn_sigma", (16,)),
        ("L0_ffn_phi", (4096, 16)), ("L0_ffn_M_u", (12, C * C)), ("L0_ffn_M_phi_plus", (64, C * C)),
        ("L0_ffn_M_phi_minus", (64, C * C)), ("L0_ffn_log_weights", (4,)), ("L0_ffn_gumbel", (4,))]


def kernel(**inputs):
    import numpy as _np
    import concourse.bacc as _bacc
    from concourse.bass_utils import run_bass_kernel_spmd as _run

    nc = _bacc.Bacc("TRN2", target_bir_lowering=False, num_devices=1)
    arrays, args, cst = {}, [], {}
    for name, shape in _INS:
        arrays[f"in_{name}_dram"] = _np.ascontiguousarray(inputs[name]).reshape(shape)
        args.append(nc.dram_tensor(f"in_{name}_dram", shape, F32, kind="ExternalInput").ap())
    for name, table in constants().items():
        arrays[f"const_{name}_dram"] = table
        cst[name] = nc.dram_tensor(f"const_{name}_dram", table.shape, F32, kind="ExternalInput").ap()
    out = nc.dram_tensor("out_0_dram", (NIMG, C, T), F32, kind="ExternalOutput").ap()
    program(nc, *args, cst, out)
    done = _run(nc, [arrays], core_ids=[0])
    return done.results[0]["out_0_dram"].reshape(NIMG, C, HW, HW)
```

```python
from contextlib import ExitStack

import concourse.bass as bass
import numpy as np
from concourse import mybir

F32 = mybir.dt.float32
BF16 = mybir.dt.bfloat16
U32 = mybir.dt.uint32
ALU = mybir.AluOpType
ACT = mybir.ActivationFunctionType
AX = mybir.AxisListType

NIMG, C, HW = 8, 128, 56
T = HW * HW
NW = 7
WS = HW // NW
NWIN, WT = NW * NW, WS * WS
ROW = NW * WT
QT = ROW // 4
TOPK, HEADS, HD = 4, 8, 16
NHP = HEADS // 2
SCALE = float(C) ** -0.5
EPS_C, EPS_T = 1e-6, 1e-5

R = 8
N1 = T // R
NF2 = 2 * N1
NT, N1T = 4, N1 // 4
NRE = NF2 // 2 + 1
NF = 400
FT = 112
NFT = NF2 // FT
FC = 8
NCH = NF // FC
KF, COPIES = 19, 6
KP = KF * COPIES
RX = 2 * R - 1

FREE = 1
BUF = [0, 1, 0, 1, 0, 1, 2]


def packed(t):
    lo, hi, out = FT * t, FT * (t + 1), []
    if lo < NRE:
        out.append((0, min(hi, NRE) - lo, 0, lo))
    if hi > NRE:
        out.append((max(NRE - lo, 0), FT, 1, max(lo, NRE) - NRE + 1))
    return out


NPACK = sum(len(packed(t)) for t in range(NFT))


def constants():
    c = {}
    c["ident"] = np.eye(C, dtype=np.float32)
    c["mean_mat"] = np.full((C, C), 1.0 / C, np.float32)
    c["quarter_mean"] = np.broadcast_to(np.eye(4, dtype=np.float32) / C, (C, 4, 4)).reshape(C, 16).copy()
    c["quarter_spread"] = np.repeat(np.eye(4, dtype=np.float32), C, axis=1)
    c["head_parity"] = np.stack([(np.arange(C) // HD) % 2 == h for h in range(2)]
                                + [np.arange(C) // HD == h for h in range(HEADS)], 1).astype(np.float32)
    n, f = np.arange(N1), np.arange(NF)
    live = (f <= NF2 // 2)
    ang = 2 * np.pi * ((n[:, None] * f[None]) % NF2) / NF2
    fwd = np.stack([np.cos(ang), -np.sin(ang)], 1) * live
    c["dft"] = fwd.reshape(NT, N1T, 2, NF).transpose(1, 0, 2, 3).reshape(N1T, NT * 2 * NF).astype(np.float32)
    amp = np.where((f == 0) | (f == NF2 // 2), 1.0, 2.0) * live / NF2
    pack = np.concatenate([fwd[:, 0, :NRE], fwd[:, 1, 1:NRE - 1]], 1)
    c["dft_packed"] = pack.reshape(NT, N1T, NF2).transpose(1, 0, 2).reshape(N1T, NT * NF2).astype(np.float32)
    inv = np.stack([np.cos(ang.T), -np.sin(ang.T)], 1) * amp[:, None, None]
    inv = np.concatenate([inv[:NRE, 0], inv[1:NRE - 1, 1]], 0)
    c["idft"] = inv.reshape(NFT, FT, N1).transpose(1, 0, 2).reshape(FT, NFT * N1).astype(np.float32)
    c["zeros"] = np.zeros((8, NIMG * R * C), np.float32)
    th = 2 * np.pi * f / NF2
    c["twist"] = np.broadcast_to(np.stack([np.cos(th), np.sin(th)]).astype(np.float32)[None], (C, 2, NF)).reshape(C, 2 * NF).copy()
    delta = np.zeros((N1T, NT, R, 3), np.float32)
    for j in range(3):
        delta[0, 0, j, j] = 1.0
    c["delta"] = delta.reshape(N1T, NT * R * 3)
    lvl_v, lvl_m = [0, 0, 0, 1, 1, 2], [0, 1, 2, 0, 1, 0]
    part = np.zeros((KP, 4), np.float32)
    for cpy in range(COPIES):
        rows = slice(cpy * KF, (cpy + 1) * KF)
        part[rows, 0] = -1.0 if lvl_v[cpy] >= 1 else 0.0
        part[rows, 1] = -1.0 if lvl_v[cpy] == 2 else 0.0
        part[rows, 2] = -1.0 if lvl_m[cpy] >= 1 else 0.0
        part[rows, 3] = -1.0 if lvl_m[cpy] == 2 else 0.0
    c["part"] = part
    sel = np.zeros((128, 2, COPIES, KF), np.float32)
    for s in range(2):
        for i in range(4):
            for k in range(16):
                sel[s * 64 + i * 16 + k, 0, :, k] = 1.0
                sel[s * 64 + i * 16 + k, 1, :, k] = 1.0 if s == 0 else -1.0
    c["sel"] = sel.reshape(128, 2 * KP)
    selu = np.zeros((12, COPIES, KF), np.float32)
    for i in range(4):
        for j in range(3):
            selu[i * 3 + j, :, 16 + j] = 1.0
    c["sel_u"] = selu.reshape(12, KP)
    own = np.zeros((128, 8), np.float32)
    for p in range(128):
        own[p, (p // 16) % 4] = 1.0
    for p in range(12):
        own[p, 4 + p // 3] = 1.0
    c["own_variant"] = own
    return c


def attention_and_dft(nc, x_d, wqkv_d, bqkv_d, lepe_w_d, lepe_b_d, wo_d, bo_d, cst, x2_d, spec_d, route_d):
    with ExitStack() as ctx:
        def sb(name, shape, dt=F32):
            return ctx.enter_context(nc.sbuf_tensor(name, shape, dt))

        def sem(name):
            return ctx.enter_context(nc.semaphore(name))

        xs = sb("xs", [C, T])
        xn = sb("xn", [C, T])
        xc = sb("xc", [C, 3, ROW])
        sq = sb("sq", [C, 2, ROW])
        std = sb("std", [4, 2, QT])
        rstd = sb("rstd", [4, 2, QT])
        epsc = sb("epsc", [C, 2])
        qmean = sb("qmean", [C, 4, 4])
        qspread = sb("qspread", [4, 4, C])
        qT = sb("qT", [C, T])
        kT = sb("kT", [C, T])
        vpad = sb("vpad", [C, HW + 2, HW + 2])
        vtok = sb("vtok", [WT, NWIN, C])
        oT = sb("oT", [C, T])
        utok = sb("utok", [N1T, NT, R, C])
        wqkv = sb("wqkv", [C, 3 * C])
        wo = sb("wo", [C, C])
        bq, bk, bv, bo, lb = (sb(n, [C, 1]) for n in ("bq", "bk", "bv", "bo", "lb"))
        bqs = sb("bqs", [C, 1])
        bvrow = sb("bvrow", [C, C])
        lw = sb("lw", [C, 9])
        ident = sb("ident", [C, C])
        mean_mat = sb("mean_mat", [C, C])
        hpar = sb("hpar", [C, 2 + HEADS])
        dft = sb("dft", [N1T, NT, NF2])
        qsum = sb("qsum", [C, NWIN])
        ksum = sb("ksum", [C, NWIN])
        logit = sb("logit", [NWIN, NWIN])
        top = sb("top", [NWIN, 8])
        topi = sb("topi", [NWIN, 8], U32)
        route = sb("route", [1, NWIN * TOPK], U32)
        ksel = sb("ksel", [C, NW, TOPK * WT])
        vsel = sb("vsel", [C, NW, 2, C])
        qz = sb("qz", [C, NW, HEADS, WT])
        nmax = sb("nmax", [C, 3, NHP])
        rsum = sb("rsum", [C, 3, NHP])
        rinv = sb("rinv", [C, 3, NHP])
        prob = sb("prob", [C, 3, NHP, TOPK * WT])
        probT = sb("probT", [C, 3, 2, 2, 2, C])
        oeven = sb("oeven", [C, 3, WT])
        ustage = sb("ustage", [FT, 2, R * C])
        ps = ctx.enter_context(nc.psum_tensor("ps", [C, 8, 512], F32))

        consts_loaded, x_loaded, ready0, x2_stored = map(sem, ("consts_loaded", "x_loaded", "ready0", "x2_stored"))
        mean_ready, centered, squared, var_ready, std_ready, inverted, spread_ready, normed = map(
            sem, ("mean_ready", "centered", "squared", "var_ready", "std_ready", "inverted", "spread_ready", "normed"))
        qk_ready, vv_ready, q_done, k_done, v_done, vt_done, sums_done = map(
            sem, ("qk_ready", "vv_ready", "q_done", "k_done", "v_done", "vt_done", "sums_done"))
        logit_ready, topk_step, route_stored, route_loaded = map(
            sem, ("logit_ready", "topk_step", "route_stored", "route_loaded"))
        gathered, s_ready, max_done, exp_done, t_ready, t_evac0, t_evac1, norm_last = map(
            sem, ("gathered", "s_ready", "max_done", "exp_done", "t_ready", "t_evac0", "t_evac1", "norm_last"))
        pv_done, rinv_done, norm_done, even_done, o_evac, lepe_done = map(
            sem, ("pv_done", "rinv_done", "norm_done", "even_done", "o_evac", "lepe_done"))
        proj_ready, x2_ready, tr_ready, ut_evac0, ut_evac1 = map(
            sem, ("proj_ready", "x2_ready", "tr_ready", "ut_evac0", "ut_evac1"))
        dft_ready, u_evac0, u_evac1, spec_zeroed = map(sem, ("dft_ready", "u_evac0", "u_evac1", "spec_zeroed"))
        passed = sem("passed")
        v_gathered = [sem(f"v_gathered{u}") for u in range(NW)]
        u_stored = [sem("u_stored0"), sem("u_stored1")]

        def load_route(w, engine):
            return nc.values_load_multi_w_load_instructions(
                route[0:1, bass.ds(w * TOPK, TOPK)], engines=[engine], min_val=0, max_val=NWIN - 1,
                skip_runtime_bounds_check_because="max_index counts the columns of logit, of which there are NWIN")[1]

        def image(v, k):
            return v[:, k * ROW:(k + 1) * ROW]

        def by_window(v):
            return v.rearrange("p (y n x) -> p n y x", y=WS, n=NW)

        def by_image(v):
            return v.rearrange("p (n y x) -> p y n x", y=WS, n=NW)

        def outputs(i):
            return ps[:, 6 + i % 2, 0:C]

        NGROUP, LAG = 2 * NFT, 4

        def u_free(s, b):
            mine = [len(packed(t)) for t in range(s % 2, NFT, 2)]
            return 16 * (sum(mine) * b + sum(mine[:s // 2]) + FREE)

        def alone(eng):
            eng.sem_inc(passed, 1)

        with nc.Block() as block:
            @block.sync
            def _(sp):
                for s in (x2_stored, route_stored, *u_stored):
                    sp.sem_inc(s, 16 * FREE)
                def load_image(b):
                    sp.wait_ge(normed, 14 * b + FREE)
                    alone(sp)
                    sp.wait_ge(x2_stored, 16 * b + 16 * FREE)
                    sp.dma_start(xs[:], x_d[bass.ds(b, 1)].rearrange("a c t -> (a c) t")).then_inc(x_loaded, 16)

                load_image(0)
                loads = [
                    (wqkv[:], wqkv_d), (wo[:], wo_d),
                    (bq[:], bqkv_d[0:C].unsqueeze(1)), (bk[:], bqkv_d[C:2 * C].unsqueeze(1)),
                    (bv[:], bqkv_d[2 * C:3 * C].unsqueeze(1)), (bo[:], bo_d.unsqueeze(1)),
                    (lb[:], lepe_b_d.unsqueeze(1)), (lw[:], lepe_w_d),
                    (bvrow[:], bqkv_d[2 * C:3 * C].partition_broadcast(C)),
                    (qmean[:].rearrange("p a b -> p (a b)"), cst["quarter_mean"]),
                    (qspread[:].rearrange("p a b -> p (a b)"), cst["quarter_spread"]), (ident[:], cst["ident"]), (mean_mat[:], cst["mean_mat"]), (hpar[:], cst["head_parity"]),
                    (dft[:].rearrange("p a b -> p (a b)"), cst["dft_packed"]),
                ]
                for dst, src in loads:
                    sp.dma_start(dst, src).then_inc(consts_loaded, 16)
                assert len(loads) == 15

                for f0, f1, c in ((0, 1, 1), (NRE - 1, NF, 1), (NRE, NF, 0)):
                    sp.dma_start(spec_d[f0:f1, c].rearrange("f b n -> f (b n)"), cst["zeros"][0:f1 - f0]).then_inc(spec_zeroed, 16)

                def gather_values(b, w, i):
                    routed = load_route(w, mybir.EngineType.SP)
                    sp.wait_ge(pv_done, NWIN * b + w + 1)
                    for j, n in enumerate(routed):
                        sp.dma_start(vsel[(j % 2) * WT:(j % 2 + 1) * WT, i, j // 2, :],
                                     vtok[:, bass.ds(n, 1), :].rearrange("p a c -> p (a c)")).then_inc(v_gathered[i], 16)

                def whole_image(b, final):
                    sp.wait_ge(topk_step, 3 * b + 3)
                    sp.dma_start(route_d[bass.ds(b, 1)].rearrange("a (w j) -> (a w) j", j=TOPK), topi[:, 0:TOPK]).then_inc(route_stored, 16)
                    sp.wait_ge(route_stored, 16 * b + 16 + 16 * FREE)
                    sp.dma_start(route[:], route_d[bass.ds(b, 1)]).then_inc(route_loaded, 16)
                    sp.wait_ge(route_loaded, 16 * b + 16)
                    alone(sp)
                    sp.wait_ge(vt_done, 14 * b + 14)
                    alone(sp)
                    with sp.Fori(0, NW) as g:
                        for i in range(NW):
                            gather_values(b, g * NW + i, i)
                    sp.wait_ge(x2_ready, 7 * b + 7)
                    sp.dma_start(x2_d[bass.ds(b, 1)].rearrange("a c t -> (a c) t"), xs[:]).then_inc(x2_stored, 16)
                    if not final:
                        load_image(b + 1)
                    for s in range(NFT):
                        sp.wait_ge(u_evac0, NFT * b + s + 1 + FREE)
                        sp.wait_ge(u_evac1, NFT * b + s + 1 + FREE)
                        for r0, r1, c, f0 in packed(s):
                            sp.dma_start(spec_d[f0:f0 + r1 - r0, c, bass.ds(b, 1), :].rearrange("f a n -> f (a n)"),
                                         ustage[r0:r1, s % 2, :]).then_inc(u_stored[s % 2], 16)

                with sp.Fori(0, NIMG - 1) as b:
                    whole_image(b, False)
                whole_image(NIMG - 1, True)
                sp.wait_ge(x2_stored, 16 * NIMG + 16 * FREE)
                for s in range(2):
                    sp.wait_ge(u_stored[s], u_free(s, NIMG))
                sp.wait_ge(spec_zeroed, 48)

            @block.gpsimd
            def _(pool):
                nc.gpsimd.memset(vpad[:], 0.0).then_inc(ready0, 1)
                nc.gpsimd.memset(epsc[:, 0:1], EPS_C).then_inc(ready0, 1)
                nc.gpsimd.memset(epsc[:, 1:2], EPS_T).then_inc(ready0, 1)
                pool.wait_ge(consts_loaded, 16 * 15)

                def gather(b, w, i):
                    u = i
                    gw = NWIN * b + w
                    routed = load_route(w, mybir.EngineType.Pool)
                    pool.wait_ge(pv_done, gw + 1)
                    nc.gpsimd.tensor_tensor(qz[:, u], qT[:, bass.ds(w * WT, WT)].unsqueeze(1).to_broadcast([C, HEADS, WT]),
                                            hpar[:, 2:].unsqueeze(2).to_broadcast([C, HEADS, WT]), ALU.mult)
                    for j, n in enumerate(routed):
                        last = nc.gpsimd.tensor_copy(ksel[:, u, j * WT:(j + 1) * WT], kT[:, bass.ds(n * WT, WT)])
                    last.then_inc(gathered, 1)

                def normalise_last(b, w, i):
                    u, gw = BUF[i], NWIN * b + w
                    pool.wait_ge(rinv_done, 4 * gw + 4)
                    nc.gpsimd.tensor_tensor(prob[:, u, NHP - 1, :], prob[:, u, NHP - 1, :],
                                            rinv[:, u, NHP - 1:NHP].to_broadcast([C, TOPK * WT]), ALU.mult).then_inc(norm_last, 1)

                def whole_image(b):
                    pool.wait_ge(route_loaded, 16 * b + 16)
                    pool.wait_ge(q_done, 7 * b + 7)
                    pool.wait_ge(sums_done, 14 * b + 14)
                    alone(pool)
                    for i in range(NW):
                        if i >= 5:
                            normalise_last(b, i - 5, i - 5)
                        gather(b, i, i)
                    with pool.Fori(1, NW) as g:
                        for i in range(NW):
                            normalise_last(b, g * NW + i - 5, (i - 5) % NW)
                            gather(b, g * NW + i, i)
                    for i in range(NW - 5, NW):
                        normalise_last(b, NWIN - NW + i, i)

                with pool.Fori(0, NIMG) as b:
                    whole_image(b)

            @block.tensor
            def _(pe):
                pe.sem_inc(pv_done, NW)
                pe.wait_ge(consts_loaded, 16 * 15)
                pe.wait_ge(ready0, 4)

                def norm_step(b, which, k):
                    n = 14 * b + 7 * which + k
                    if k < NW:
                        if which:
                            pe.wait_ge(x2_ready, 7 * b + k + 1)
                        if k >= 1:
                            pe.wait_ge(centered, n)
                        nc.tensor.matmul(ps[:, 4, 0:ROW], mean_mat[:], image(xs, k),
                                         start=True, stop=True).then_inc(mean_ready, 1)
                    if 1 <= k <= NW:
                        pe.wait_ge(squared, n)
                        if k >= 2:
                            pe.wait_ge(std_ready, n - 1)
                        for j in range(4):
                            last = nc.tensor.matmul(ps[0:4, 5, 0:QT], qmean[:, j, :], sq[:, (k - 1) % 2, j * QT:(j + 1) * QT],
                                                    start=(j == 0), stop=(j == 3))
                        last.then_inc(var_ready, 1)
                    if k >= 2:
                        pe.wait_ge(inverted, n - 1)
                        if k >= 4:
                            pe.wait_ge(normed, n - 3 + FREE)
                        for j in range(4):
                            last = nc.tensor.matmul(ps[:, 6 + k % 2, j * QT:(j + 1) * QT], qspread[:, j, :], rstd[:, k % 2, :],
                                                    start=True, stop=True)
                        last.then_inc(spread_ready, 1)

                def scores(b, w, i, hps):
                    u, gw = i, NWIN * b + w
                    pe.wait_ge(gathered, gw + 1)
                    for hp in hps:
                        pe.wait_ge(exp_done, 4 * gw + hp - 3 + 4)
                        nc.tensor.matmul(ps[:, hp, 0:TOPK * WT], qz[:, u, 2 * hp:2 * hp + 2, :], ksel[:, u, :],
                                         start=True, stop=True).then_inc(s_ready, 1)

                def transposes(b, w, i, a):
                    u, gw = BUF[i], NWIN * b + w
                    pe.wait_ge(norm_done, 3 * gw + a + 2)
                    if a == 1:
                        pe.wait_ge(norm_last, gw + 1)
                    if a == 0:
                        pe.wait_ge(t_evac0, gw + FREE)
                    else:
                        pe.wait_ge(t_evac1, gw + FREE)
                    for h in range(2):
                        for kt in range(2):
                            last = nc.tensor.transpose(ps[:, 4 + a, (2 * h + kt) * C:(2 * h + kt + 1) * C],
                                                       prob[:, u, 2 * a + h, kt * C:(kt + 1) * C], ident[:])
                    last.then_inc(t_ready, 1)

                def values(b, g, i, a):
                    gw = NWIN * b + NW * g + i
                    if a == 0:
                        pe.wait_ge(v_gathered[i], 16 * TOPK * (NW * b + g + 1))
                        pe.wait_ge(o_evac, gw + 2 if i == 0 else gw + 1)
                        pe.wait_ge(t_evac0, gw + 1 + FREE)
                    else:
                        pe.wait_ge(t_evac1, gw + 1 + FREE)
                    for h in range(2):
                        hp = 2 * a + h
                        for kt in range(2):
                            last = nc.tensor.matmul(outputs(i)[32 * hp:32 * hp + 32, :], vsel[:, i, kt, 32 * hp:32 * hp + 32],
                                                    probT[:, BUF[i], a, h, kt, :], start=(kt == 0), stop=(kt == 1))
                    if a == 1:
                        last.then_inc(pv_done, 1)

                def window_row(b, g, first, final):
                    for i in range(NW):
                        w = g * NW + i
                        more = not (final and i == NW - 1)
                        before = not (first and i == 0)
                        pg, pi = (g, i - 1) if i else (g - 1, NW - 1)
                        if more:
                            scores(b, w + 1, (i + 1) % NW, (0, 1, 2, 3))
                        for a in range(2):
                            transposes(b, w, i, a)
                            if before:
                                values(b, pg, pi, a)

                def project(b, k):
                    if k >= 2:
                        pe.wait_ge(x2_ready, 7 * b + k - 1)
                    nc.tensor.matmul(ps[:, k % 2, 0:ROW], wo[:], by_image(image(oT, k)), start=True, stop=False)
                    nc.tensor.matmul(ps[:, k % 2, 0:ROW], wo[:], image(xn, k), start=False, stop=True).then_inc(proj_ready, 1)

                def whole_image(b, final):
                    pe.wait_ge(normed, 14 * b + 7 + FREE)
                    pe.wait_ge(u_evac0, NFT * b + FREE)
                    pe.wait_ge(u_evac1, NFT * b + FREE)
                    for k in range(NW):
                        xk = image(xn, k)
                        p = 2 * (k % 2)
                        if k >= 2:
                            pe.wait_ge(q_done, 7 * b + k - 1)
                            pe.wait_ge(k_done, 7 * b + k - 1)
                        nc.tensor.matmul(ps[:, p, 0:ROW], wqkv[:, 0:C], xk, start=True, stop=True).then_inc(qk_ready, 1)
                        nc.tensor.matmul(ps[:, p + 1, 0:ROW], wqkv[:, C:2 * C], xk, start=True, stop=True).then_inc(qk_ready, 1)
                    pe.wait_ge(sums_done, 14 * b + 14)
                    nc.tensor.matmul(ps[0:NWIN, 4, 0:NWIN], qsum[:], ksum[:], start=True, stop=True).then_inc(logit_ready, 1)
                    for k in range(NW):
                        xk = image(xn, k)
                        p = 5 if k % 2 == 0 else 0
                        if k >= 2:
                            pe.wait_ge(v_done, 7 * b + k - 1)
                            pe.wait_ge(vt_done, 14 * b + 2 * k - 2)
                        nc.tensor.matmul(ps[:, p, 0:ROW], wqkv[:, 2 * C:], by_image(xk), start=True, stop=True).then_inc(vv_ready, 1)
                        for i in range(0, NW, 2):
                            win = xk[:, i * WT:min(i + 2, NW) * WT]
                            last = nc.tensor.matmul(ps[0:win.shape[1], p + 1, i // 2 * C:(i // 2 + 1) * C], win, wqkv[:, 2 * C:],
                                                    start=True, stop=True)
                        last.then_inc(vv_ready, 1)
                    pe.wait_ge(vt_done, 14 * b + 14)
                    pe.wait_ge(v_done, 7 * b + 7)
                    scores(b, 0, 0, (0, 1, 2, 3))
                    window_row(b, 0, True, False)
                    with pe.Fori(1, NW - 1) as g:
                        window_row(b, g, False, False)
                    window_row(b, NW - 1, False, True)
                    values(b, NW - 1, NW - 1, 0)
                    values(b, NW - 1, NW - 1, 1)
                    pe.wait_ge(lepe_done, 63 * b + 63)
                    pe.wait_ge(o_evac, NWIN * b + NWIN + 2)
                    project(b, 0)
                    for k in range(NW + 2):
                        if k + 1 < NW:
                            project(b, k + 1)
                        norm_step(b, 1, k)
                    pe.wait_ge(normed, 14 * b + 14 + FREE)
                    for t in range(2 * NT):
                        nt, half = t // 2, t % 2
                        if t >= 4:
                            if t % 2 == 0:
                                pe.wait_ge(ut_evac0, 4 * b + t // 2 - 1)
                            else:
                                pe.wait_ge(ut_evac1, 4 * b + t // 2 - 1)
                        for r in range(4):
                            t0 = R * N1T * nt + 4 * half + r
                            src = xn[:, t0:t0 + R * (N1T - 1) + 1:R]
                            last = nc.tensor.transpose(ps[0:N1T, 4 + t % 4, r * C:(r + 1) * C], src, ident[:])
                        last.then_inc(tr_ready, 1)
                    pe.wait_ge(ut_evac0, 4 * b + 4)
                    pe.wait_ge(ut_evac1, 4 * b + 4)
                    for q in range(NGROUP):
                        s, half = q // 2, q % 2
                        if q >= 4:
                            if half == 0:
                                pe.wait_ge(u_evac0, NFT * b + s - 1 + FREE)
                            else:
                                pe.wait_ge(u_evac1, NFT * b + s - 1 + FREE)
                        for nt in range(NT):
                            last = nc.tensor.matmul(ps[0:FT, q % 4, :], dft[:, nt, s * FT:(s + 1) * FT],
                                                    utok[:, nt, 4 * half:4 * half + 4, :], start=(nt == 0), stop=(nt == NT - 1))
                        last.then_inc(dft_ready, 1)
                        if not final and LAG <= q < LAG + NW + 2:
                            if q == LAG:
                                pe.wait_ge(x_loaded, 16 * b + 32)
                            norm_step(b + 1, 0, q - LAG)

                pe.wait_ge(x_loaded, 16)
                for k in range(NW + 2):
                    norm_step(0, 0, k)
                with pe.Fori(0, NIMG - 1) as b:
                    whole_image(b, False)
                whole_image(NIMG - 1, True)

            @block.scalar
            def _(act):
                act.wait_ge(consts_loaded, 16 * 15)
                act.wait_ge(ready0, 3)
                nc.scalar.mul(bqs[:], bq[:], SCALE).then_inc(ready0, 1)
                act.wait_ge(ready0, 4)
                act.sem_inc(exp_done, 4)
                for s in (u_evac1, t_evac0, t_evac1):
                    act.sem_inc(s, FREE)

                def norm_step(b, which, k):
                    if k < NW:
                        n = 14 * b + 7 * which + k
                        act.wait_ge(centered, n + 1)
                        if k >= 2:
                            act.wait_ge(var_ready, n - 1)
                        nc.scalar.activation(sq[:, k % 2, :], xc[:, k % 3, :], ACT.Square).then_inc(squared, 1)
                    if 1 <= k <= NW:
                        m, j = 14 * b + 7 * which + k - 1, k - 1
                        act.wait_ge(var_ready, m + 1)
                        if j >= 2:
                            act.wait_ge(inverted, m - 1)
                        nc.scalar.activation(std[:, j % 2, :], ps[0:4, 5, 0:QT], ACT.Sqrt,
                                             bias=epsc[0:4, which:which + 1]).then_inc(std_ready, 1)

                def exps(b, w, i, hps):
                    u, gw = BUF[i], NWIN * b + w
                    for hp in hps:
                        act.wait_ge(max_done, 4 * gw + hp + 1)
                        nc.scalar.activation(prob[:, u, hp, :], ps[:, hp, 0:TOPK * WT], ACT.Exp,
                                             bias=nmax[:, u, hp:hp + 1], accum_out=rsum[:, u, hp:hp + 1]).then_inc(exp_done, 1)

                def even_heads(b, w, i):
                    gw = NWIN * b + w
                    act.wait_ge(pv_done, gw + 1 + NW)
                    act.wait_ge(o_evac, gw + 1)
                    nc.scalar.activation(oeven[:, BUF[i]], outputs(i)[:, 0:WT], ACT.Copy, scale=hpar[:, 0:1]).then_inc(even_done, 1)

                def window_row(b, g, first, final):
                    for i in range(NW):
                        w = g * NW + i
                        gw = NWIN * b + w
                        more = not (final and i == NW - 1)
                        if more:
                            exps(b, w + 1, (i + 1) % NW, (0, 1))
                        act.wait_ge(t_ready, 2 * gw + 1)
                        act.wait_ge(pv_done, gw - 1 + NW)
                        nc.scalar.activation(probT[:, BUF[i], 0].rearrange("p a b c -> p (a b c)"), ps[:, 4, :], ACT.Copy).then_inc(t_evac0, 1)
                        if more:
                            exps(b, w + 1, (i + 1) % NW, (2, 3))
                        act.wait_ge(t_ready, 2 * gw + 2)
                        nc.scalar.activation(probT[:, BUF[i], 1].rearrange("p a b c -> p (a b c)"), ps[:, 5, :], ACT.Copy).then_inc(t_evac1, 1)
                        if not (first and i == 0):
                            even_heads(b, w - 1, (i - 1) % NW)

                def whole_image(b, final):
                    for k in range(NW):
                        act.wait_ge(qk_ready, 14 * b + 2 * k + 1)
                        nc.scalar.activation(qT[:, k * ROW:(k + 1) * ROW], ps[:, 2 * (k % 2), 0:ROW], ACT.Identity,
                                             bias=bqs[:], scale=SCALE).then_inc(q_done, 1)
                    for k in range(NW):
                        act.wait_ge(vv_ready, 14 * b + 2 * k + 1)
                        nc.scalar.activation(vpad[:, 1 + k * WS:1 + (k + 1) * WS, 1:1 + HW],
                                             ps[:, 5 if k % 2 == 0 else 0, 0:ROW].rearrange("p (r c) -> p r c", r=WS), ACT.Identity,
                                             bias=bv[:]).then_inc(v_done, 1)
                    exps(b, 0, 0, (0, 1, 2, 3))
                    window_row(b, 0, True, False)
                    with act.Fori(1, NW - 1) as g:
                        window_row(b, g, False, False)
                    window_row(b, NW - 1, False, True)
                    even_heads(b, NWIN - 1, NW - 1)
                    for k in range(NW + 1):
                        norm_step(b, 1, k)
                    for t in range(1, 2 * NT, 2):
                        act.wait_ge(tr_ready, 8 * b + t + 1)
                        nc.scalar.activation(utok[:, t // 2, 4:8, :].rearrange("p a b -> p (a b)"), ps[0:N1T, 4 + t % 4, :], ACT.Copy).then_inc(ut_evac1, 1)
                    for q in range(NGROUP):
                        if q % 2 == 1:
                            s = q // 2
                            act.wait_ge(dft_ready, NGROUP * b + q + 1)
                            act.wait_ge(u_stored[s % 2], u_free(s, b))
                            nc.scalar.activation(ustage[:, s % 2, 512:1024], ps[0:FT, q % 4, :], ACT.Copy).then_inc(u_evac1, 1)
                        if not final and LAG <= q <= LAG + NW:
                            norm_step(b + 1, 0, q - LAG)

                for k in range(NW + 1):
                    norm_step(0, 0, k)
                with act.Fori(0, NIMG - 1) as b:
                    whole_image(b, False)
                whole_image(NIMG - 1, True)

            @block.vector
            def _(dve):
                for s in (normed, u_evac0):
                    dve.sem_inc(s, FREE)
                dve.sem_inc(o_evac, 2)
                dve.wait_ge(consts_loaded, 16 * 15)
                dve.wait_ge(ready0, 4)

                def norm_step(b, which, k):
                    n = 14 * b + 7 * which + k
                    if k < NW:
                        dve.wait_ge(mean_ready, n + 1)
                        if k >= 3:
                            dve.wait_ge(normed, n - 2 + FREE)
                        nc.vector.tensor_tensor(xc[:, k % 3, :], image(xs, k), ps[:, 4, 0:ROW], ALU.subtract).then_inc(centered, 1)
                    if k >= 2:
                        dve.wait_ge(spread_ready, n - 1)
                        dst = image(xn, k - 2) if which else by_image(image(xn, k - 2))
                        centre, scale = xc[:, (k - 2) % 3, :], ps[:, 6 + k % 2, 0:ROW]
                        if not which:
                            centre, scale = (v.rearrange("p (y n x) -> p y n x", y=WS, n=NW) for v in (centre, scale))
                        nc.vector.tensor_tensor(dst, centre, scale, ALU.mult).then_inc(normed, 1)
                    if 1 <= k <= NW:
                        dve.wait_ge(std_ready, n)
                        if k >= 3:
                            dve.wait_ge(spread_ready, n - 2)
                        nc.vector.reciprocal(rstd[:, (k - 1) % 2, :], std[:, (k - 1) % 2, :]).then_inc(inverted, 1)

                def maxima(b, w, i, hps):
                    u, gw = BUF[i], NWIN * b + w
                    for hp in hps:
                        dve.wait_ge(s_ready, 4 * gw + hp + 1)
                        nc.vector.tensor_reduce(nmax[:, u, hp:hp + 1], ps[:, hp, 0:TOPK * WT], AX.X, ALU.max,
                                                negate=True).then_inc(max_done, 1)

                def positional(b, g, taps):
                    acc = xn[:, bass.ds(g * ROW, ROW)].rearrange("p (r c) -> p r c", r=WS)
                    for tap in taps:
                        src = vpad[:, bass.ds(g * WS + tap // 3, WS), tap % 3:tap % 3 + HW]
                        n = 63 * b + 9 * g + tap
                        if tap == 0:
                            nc.vector.tensor_scalar(acc, src, lw[:, 0:1], lb[:], ALU.mult, ALU.add).then_inc(lepe_done, 1)
                        else:
                            dve.wait_ge(lepe_done, n)
                            nc.vector.scalar_tensor_tensor(acc, src, lw[:, tap:tap + 1], acc, ALU.mult, ALU.add).then_inc(lepe_done, 1)

                def normalise(b, w, i, hps):
                    u, gw = BUF[i], NWIN * b + w
                    first, n = hps[0], len(hps)
                    dve.wait_ge(exp_done, 4 * gw + first + n + 4)
                    nc.vector.reciprocal(rinv[:, u, first:first + n], rsum[:, u, first:first + n]).then_inc(rinv_done, n)
                    dve.wait_ge(rinv_done, 4 * gw + first + n)
                    for hp in hps:
                        if hp == NHP - 1:
                            continue
                        nc.vector.tensor_scalar(prob[:, u, hp, :], prob[:, u, hp, :], rinv[:, u, hp:hp + 1], None,
                                                ALU.mult).then_inc(norm_done, 1)

                def odd_heads(b, w, i):
                    gw = NWIN * b + w
                    dve.wait_ge(even_done, gw + 1)
                    nc.vector.scalar_tensor_tensor(oT[:, bass.ds(w * WT, WT)], outputs(i)[:, WT:2 * WT], hpar[:, 1:2], oeven[:, BUF[i]],
                                                   ALU.mult, ALU.add).then_inc(o_evac, 1)

                def window_row(b, g, first, final):
                    for i in range(NW):
                        w = g * NW + i
                        gw = NWIN * b + w
                        more = not (final and i == NW - 1)
                        if more:
                            maxima(b, w + 1, (i + 1) % NW, (0, 1))
                        normalise(b, w, i, (2, 3))
                        if not (first and i < 2):
                            odd_heads(b, w - 2, (i - 2) % NW)
                        if more:
                            maxima(b, w + 1, (i + 1) % NW, (2, 3))
                        positional(b, g, ([0, 1], [2], [3], [4], [5], [6], [7, 8])[i])
                        if more:
                            normalise(b, w + 1, (i + 1) % NW, (0, 1))

                def residual(b, k):
                    dve.wait_ge(proj_ready, 7 * b + k + 1)
                    nc.vector.scalar_tensor_tensor(image(xs, k), ps[:, k % 2, 0:ROW], bo[:], image(xs, k),
                                                   ALU.add, ALU.add).then_inc(x2_ready, 1)

                def whole_image(b, final):
                    for k in range(NW):
                        dve.wait_ge(qk_ready, 14 * b + 2 * k + 2)
                        kk = image(kT, k)
                        nc.vector.tensor_scalar(kk, ps[:, 2 * (k % 2) + 1, 0:ROW], bk[:], None, ALU.add).then_inc(k_done, 1)
                        dve.wait_ge(q_done, 7 * b + k + 1)
                        nc.vector.tensor_reduce(qsum[:, k * NW:(k + 1) * NW], image(qT, k).rearrange("p (w t) -> p w t", w=NW),
                                                AX.X, ALU.add).then_inc(sums_done, 1)
                        dve.wait_ge(k_done, 7 * b + k + 1)
                        nc.vector.tensor_reduce(ksum[:, k * NW:(k + 1) * NW], kk.rearrange("p (w t) -> p w t", w=NW), AX.X, ALU.add).then_inc(sums_done, 1)
                    dve.wait_ge(logit_ready, b + 1)
                    dve.wait_ge(route_stored, 16 * b + 16 * FREE)
                    nc.vector.tensor_copy(logit[:], ps[0:NWIN, 4, 0:NWIN]).then_inc(topk_step, 1)
                    dve.wait_ge(topk_step, 3 * b + 1)
                    alone(dve)
                    nc.vector.max(top[:], logit[:]).then_inc(topk_step, 1)
                    dve.wait_ge(topk_step, 3 * b + 2)
                    alone(dve)
                    nc.vector.max_index(topi[:], top[:], logit[:]).then_inc(topk_step, 1)
                    for k in range(NW):
                        dve.wait_ge(vv_ready, 14 * b + 2 * k + 2)
                        for odd in range(2):
                            n, half = (NW + 1 - odd) // 2, slice(odd * WT, (odd + 1) * WT)
                            nc.vector.tensor_tensor(vtok[:, k * NW + odd:k * NW + odd + 2 * n - 1:2, :],
                                                    ps[half, 6 if k % 2 == 0 else 1, 0:n * C].rearrange("p (w c) -> p w c", w=n),
                                                    bvrow[half, :].unsqueeze(1).to_broadcast([WT, n, C]), ALU.add).then_inc(vt_done, 1)
                    maxima(b, 0, 0, (0, 1, 2, 3))
                    normalise(b, 0, 0, (0, 1))
                    dve.wait_ge(v_done, 7 * b + 7)
                    alone(dve)
                    window_row(b, 0, True, False)
                    with dve.Fori(1, NW - 1) as g:
                        window_row(b, g, False, False)
                    window_row(b, NW - 1, False, True)
                    odd_heads(b, NWIN - 2, NW - 2)
                    odd_heads(b, NWIN - 1, NW - 1)
                    residual(b, 0)
                    for k in range(NW + 2):
                        if k + 1 < NW:
                            residual(b, k + 1)
                        norm_step(b, 1, k)
                    for t in range(0, 2 * NT, 2):
                        dve.wait_ge(tr_ready, 8 * b + t + 1)
                        nc.vector.tensor_copy(utok[:, t // 2, 0:4, :].rearrange("p a b -> p (a b)"), ps[0:N1T, 4 + t % 4, :]).then_inc(ut_evac0, 1)
                    for q in range(NGROUP):
                        if q % 2 == 0:
                            s = q // 2
                            dve.wait_ge(dft_ready, NGROUP * b + q + 1)
                            dve.wait_ge(u_stored[s % 2], u_free(s, b))
                            nc.vector.tensor_copy(ustage[:, s % 2, 0:512], ps[0:FT, q % 4, :]).then_inc(u_evac0, 1)
                        if not final and LAG <= q < LAG + NW + 2:
                            norm_step(b + 1, 0, q - LAG)

                for k in range(NW + 2):
                    norm_step(0, 0, k)
                with dve.Fori(0, NIMG - 1) as b:
                    whole_image(b, False)
                whole_image(NIMG - 1, True)


def filter_and_product(nc, phi_d, sigma_d, mu_d, mp_d, mm_d, logw_d, gumbel_d, cst, prefix, spec_d, prod_d):
    with ExitStack() as ctx:
        def sb(name, shape, dt=F32):
            return ctx.enter_context(nc.sbuf_tensor(name, shape, dt))

        def sem(name):
            return ctx.enter_context(nc.semaphore(name))

        NB = NIMG
        Q = 2 * NB * R
        ms = sb("ms", [KP, 2, C, C], BF16)
        vs = sb("vs", [KP, NCH, 2, 4, 2, FC], BF16)
        ps = ctx.enter_context(nc.psum_tensor("psb", [C, 8, 512], F32))

        with ExitStack() as prep:
            def sbp(name, shape, dt=F32):
                return prep.enter_context(nc.sbuf_tensor(name, shape, dt))

            def semp(name):
                return prep.enter_context(nc.semaphore(name))

            MC, NMC = 2048, C * C // 2048
            UN = MC // 512
            lg = sbp("lg", [C, 2, 4])
            soft = sbp("soft", [C, 8, 4])
            col = sbp("col", [C, 8])
            sig = sbp("sig", [C, 1])
            own = sbp("own", [C, 8])
            part = sbp("part", [KP, 4])
            sel = sbp("selm", [C, 2, KP])
            selu = sbp("selu", [12, KP])
            phi = sbp("phi", [N1T, NT * R, 16])
            delta = sbp("deltas", [N1T, NT * R, 3])
            phir = sbp("phir", [N1T, NT * R, COPIES, KF])
            dft = sbp("dftb", [N1T, NT, 2, NF])
            mat = sbp("mat", [C, 2, MC])
            matu = sbp("matu", [12, 2, MC])
            hi = sbp("hi", [KP, 2, 512], BF16)
            rest = sbp("rest", [KP, 2, 512])
            mid = sbp("mid", [KP, 2, 512], BF16)
            loaded, sm, sel_ready, phi_ready, ssig = map(semp, ("b_loaded", "b_small", "b_sel", "b_phi", "b_sig"))
            smx, sma, filters_loaded = semp("b_smx"), semp("b_sma"), semp("b_filters")
            mat_loaded = [semp("mat_loaded0"), semp("mat_loaded1")]
            unit_ready, hi_done, rest_done, mid_done, split_done = map(
                semp, ("unit_ready", "hi_done", "rest_done", "mid_done", "split_done"))
            NV = 2 * R
            NUNIT = NV + 2 * UN * NMC

            with nc.Block() as block:
                @block.sync
                def _(sp):
                    filters = [(phi[:, nt * R:(nt + 1) * R, :].rearrange("p a b -> p (a b)"),
                                phi_d[nt * N1T * R:(nt + 1) * N1T * R, :].rearrange("(n r) k -> n (r k)", r=R)) for nt in range(NT)]
                    filters += [(delta[:].rearrange("p a b -> p (a b)"), cst["delta"]),
                                (dft[:].rearrange("p a b c -> p (a b c)"), cst["dft"])]
                    assert len(filters) == 6
                    for dst, src in filters:
                        sp.dma_start(dst, src).then_inc(filters_loaded, 16)
                    loads = [(part[:], cst["part"]),
                             (lg[:, 0, :], logw_d.partition_broadcast(C)), (lg[:, 1, :], gumbel_d.partition_broadcast(C)),
                             (own[:], cst["own_variant"]),
                             (sel[:].rearrange("p a b -> p (a b)"), cst["sel"]), (selu[:], cst["sel_u"])]
                    loads += [(sig[16 * i:16 * i + 16, :], sigma_d.unsqueeze(1)) for i in range(8)]
                    assert len(loads) == 14
                    for dst, src in loads:
                        sp.dma_start(dst, src).then_inc(loaded, 16)
                    for m in range(NMC):
                        if m >= 2:
                            sp.wait_ge(unit_ready, NV + 2 * UN * (m - 1))
                        cols = slice(m * MC, (m + 1) * MC)
                        for dst, src in ((mat[0:64, m % 2, :], mp_d[:, cols]), (mat[64:128, m % 2, :], mm_d[:, cols]),
                                         (matu[:, m % 2, :], mu_d[:, cols])):
                            sp.dma_start(dst, src).then_inc(mat_loaded[m % 2], 16)

                @block.gpsimd
                def _(pool):
                    pool.wait_ge(filters_loaded, 16 * 6)
                    for cpy in range(COPIES):
                        nc.gpsimd.tensor_copy(phir[:, :, cpy, 0:16], phi[:]).then_inc(phi_ready, 1)
                        nc.gpsimd.tensor_copy(phir[:, :, cpy, 16:KF], delta[:]).then_inc(phi_ready, 1)

                @block.tensor
                def _(pe):
                    pe.wait_ge(phi_ready, 2 * COPIES)
                    for u in range(NV):
                        s, c = u // 2, u % 2
                        if u >= 2:
                            pe.wait_ge(hi_done, u - 1)
                            pe.wait_ge(rest_done, u - 1)
                        for nt in range(NT):
                            last = nc.tensor.matmul(ps[0:KP, u % 2, 0:NF], phir[:, nt * R + s, :, :].rearrange("p a b -> p (a b)"),
                                                    dft[:, nt, c, :], start=(nt == 0), stop=(nt == NT - 1))
                        last.then_inc(unit_ready, 1)
                    pe.wait_ge(sel_ready, 2)
                    for u in range(NV, NUNIT):
                        m, rem = (u - NV) // (2 * UN), (u - NV) % (2 * UN)
                        odd, cols = rem // UN, slice((rem % UN) * 512, (rem % UN + 1) * 512)
                        if rem == 0:
                            pe.wait_ge(mat_loaded[m % 2], 48 * (m // 2 + 1))
                        pe.wait_ge(hi_done, u - 1)
                        pe.wait_ge(rest_done, u - 1)
                        nc.tensor.matmul(ps[0:KP, u % 2, :], sel[:, odd, :], mat[:, m % 2, cols], start=True, stop=False)
                        nc.tensor.matmul(ps[0:KP, u % 2, :], selu[:], matu[:, m % 2, cols], start=False, stop=True).then_inc(unit_ready, 1)

                def width(u):
                    return NF if u < NV else 512

                @block.scalar
                def _(act):
                    act.wait_ge(loaded, 16 * 14)
                    nc.scalar.activation(col[:, 0:1], sig[:], ACT.Sqrt).then_inc(ssig, 1)
                    act.wait_ge(ssig, 1)
                    nc.scalar.activation(col[:, 1:2], col[:, 0:1], ACT.Sqrt).then_inc(ssig, 1)
                    act.wait_ge(smx, 1)
                    nc.scalar.activation(soft[:, 1, :], soft[:, 0, :], ACT.Exp, bias=col[:, 2:3], accum_out=col[:, 3:4]).then_inc(sma, 1)
                    for u in range(NUNIT + 1):
                        if u < NUNIT:
                            act.wait_ge(unit_ready, u + 1)
                            if u >= 2:
                                act.wait_ge(rest_done, u - 1)
                            nc.scalar.activation(hi[:, u % 2, 0:width(u)], ps[0:KP, u % 2, 0:width(u)], ACT.Copy).then_inc(hi_done, 1)
                        if u >= 1:
                            v = u - 1
                            act.wait_ge(rest_done, v + 1)
                            if v >= 2:
                                act.wait_ge(split_done, v - 1)
                            nc.scalar.activation(mid[:, v % 2, 0:width(v)], rest[:, v % 2, 0:width(v)], ACT.Copy).then_inc(mid_done, 1)

                @block.vector
                def _(dve):
                    steps = [0]

                    def then(ins):
                        steps[0] += 1
                        ins.then_inc(sm, 1)
                        dve.wait_ge(sm, steps[0])

                    dve.wait_ge(loaded, 16 * 14)
                    v = nc.vector
                    then(v.tensor_tensor(soft[:, 0, :], lg[:, 0, :], lg[:, 1, :], ALU.add))
                    v.tensor_reduce(col[:, 2:3], soft[:, 0, :], AX.X, ALU.max, negate=True).then_inc(smx, 1)
                    dve.wait_ge(sma, 1)
                    then(v.reciprocal(col[:, 4:5], col[:, 3:4]))
                    then(v.tensor_scalar(soft[:, 2, :], soft[:, 1, :], col[:, 4:5], None, ALU.mult))
                    then(v.tensor_reduce(col[:, 5:6], soft[:, 2, :], AX.X, ALU.max))
                    then(v.tensor_scalar(soft[:, 3, :], soft[:, 2, :], col[:, 5:6], None, ALU.is_ge))
                    then(v.tensor_scalar(soft[:, 4, :], soft[:, 3, :], -1.0, 1.0, ALU.mult, ALU.add))
                    for i in range(1, 4):
                        then(v.tensor_tensor(soft[:, 3, i:i + 1], soft[:, 3, i:i + 1], soft[:, 4, i - 1:i], ALU.mult))
                        then(v.tensor_tensor(soft[:, 4, i:i + 1], soft[:, 4, i:i + 1], soft[:, 4, i - 1:i], ALU.mult))
                    then(v.tensor_copy(prefix[:, 0:1], soft[:, 3, 0:1]))
                    for i in range(1, 4):
                        then(v.tensor_tensor(prefix[:, i:i + 1], prefix[:, i - 1:i], soft[:, 3, i:i + 1], ALU.add))
                    then(v.tensor_tensor(soft[:, 5, :], soft[:, 3, :], soft[:, 2, :], ALU.subtract))
                    then(v.tensor_tensor(soft[:, 6, :], soft[:, 5, :], soft[:, 2, :], ALU.add))
                    for i in range(2):
                        then(v.tensor_tensor(soft[:, 7, :], soft[:, 6, :], own[:, 4 * i:4 * i + 4], ALU.mult))
                        then(v.tensor_reduce(col[:, 6 + i:7 + i], soft[:, 7, :], AX.X, ALU.add))
                    dve.wait_ge(ssig, 2)
                    then(v.tensor_tensor(col[:, 6:7], col[:, 6:7], col[:, 1:2], ALU.mult))
                    v.tensor_scalar(sel[:], sel[:], col[:, 6:7], None, ALU.mult).then_inc(sel_ready, 1)
                    v.tensor_scalar(selu[:], selu[:], col[0:12, 7:8], None, ALU.mult).then_inc(sel_ready, 1)
                    for u in range(NUNIT + 1):
                        if u < NUNIT:
                            w, lv = width(u), (0 if u < NV else 2)
                            dve.wait_ge(hi_done, u + 1)
                            if u >= 2:
                                dve.wait_ge(split_done, u - 1)
                            v.scalar_tensor_tensor(rest[:, u % 2, 0:w], hi[:, u % 2, 0:w], part[:, lv:lv + 1],
                                                   ps[0:KP, u % 2, 0:w], ALU.mult, ALU.add).then_inc(rest_done, 1)
                        if u >= 1:
                            q = u - 1
                            w, lv = width(q), (0 if q < NV else 2)
                            dve.wait_ge(mid_done, q + 1)
                            dve.wait_ge(rest_done, q + 1)
                            if q < NV:
                                s, c = q // 2, q % 2
                                dst = vs[:, :, s % 2, s // 2, c, :]
                                a, b = (z[:, q % 2, 0:w].rearrange("p (h f) -> p h f", f=FC) for z in (mid, rest))
                            else:
                                m, rem = (q - NV) // (2 * UN), (q - NV) % (2 * UN)
                                d0 = (m * UN + rem % UN) * 4
                                dst = ms[:, rem // UN, :, d0:d0 + 4].rearrange("p e d -> p d e")
                                a, b = (z[:, q % 2, 0:w].rearrange("p (d e) -> p d e", e=C) for z in (mid, rest))
                            v.scalar_tensor_tensor(dst, a, part[:, lv + 1:lv + 2], b, ALU.mult, ALU.add).then_inc(split_done, 1)

        gf = sb("gf", [C, FC, 16, C])
        ux = sb("ux", [C, FC, 3, NB, RX])
        tw = sb("tw", [C, 2, FC, 2 * NB, R - 1])
        vcur = sb("vcur", [KP, 2, 64], BF16)
        tcur = sb("tcur", [C, 2, FC])
        xin = sb("xin", [Q, FC, C])
        ye = sb("ye", [C, FC, Q])
        yst = sb("yst", [Q, FC, C])
        ident = sb("identb", [C, C])
        twist = sb("twist", [C, 2, NF])
        cl, x_in, xtr_ready, ux_plain, twist_step, vcur_ready, tcur_ready = map(
            sem, ("bc_loaded", "x_in", "xtr_ready", "ux_plain", "twist_step", "vcur_ready", "tcur_ready"))
        g_ready, g_evac0, g_evac1, y_ready, ye_evac, ytr_ready, yst_evac, y_stored = map(
            sem, ("g_ready", "g_evac0", "g_evac1", "y_ready", "ye_evac", "ytr_ready", "yst_evac", "y_stored"))
        LAST = NRE - (NCH - 1) * FC

        def halves(live):
            return [(half, min(4, live - 4 * half)) for half in range(2) if live > 4 * half]

        def plain(half):
            fs = slice(4 * half, 4 * half + 4)
            src = ps[:, half, 0:4 * Q]
            return ((ux[:, fs, 1:3, :, R - 1:RX].rearrange("p f k b r -> p f (k b) r"),
                     src.rearrange("p (f q r) -> p f q r", f=4, r=R)),
                    (ux[:, fs, 0, :, R - 1:RX], src.rearrange("p (f c b r) -> p f c b r", f=4, c=2, b=NB)[:, :, 1]))

        BY_ACT = [blk for blk in range(32) if blk % 9 % 2 == 0]
        BY_DVE = [blk for blk in range(32) if blk % 9 % 2 == 1]

        def wait_g_read(eng, ch, blk):
            mine, done = (BY_ACT, g_evac1) if blk in BY_ACT else (BY_DVE, g_evac0)
            eng.wait_ge(done, len(mine) * ch + mine.index(blk) + 1)

        def spread(blk):
            return (gf[:, :, :, 4 * blk:4 * blk + 4].rearrange("p f m e -> p e m f"),
                    ps[:, 2 + blk % 4, :].rearrange("p (e m f) -> p e m f", e=4, f=FC))

        with nc.Block() as block:
            @block.sync
            def _(sp):
                sp.sem_inc(y_stored, 16 * FREE)
                sp.dma_start(ident[:], cst["ident"]).then_inc(cl, 16)
                sp.dma_start(twist[:].rearrange("p a b -> p (a b)"), cst["twist"]).then_inc(cl, 16)

                def load(ch):
                    sp.dma_start(xin[:], spec_d[bass.ds(ch * FC, FC)].rearrange("f c b n -> f (c b n)").rearrange("f (q d) -> q f d", d=C)).then_inc(x_in, 16)

                def store(ch, live=FC):
                    sp.wait_ge(yst_evac, 2 * ch + len(halves(live)) + FREE)
                    sp.dma_start(prod_d[bass.ds(ch * FC, live)].rearrange("f q e -> q f e"), yst[:, 0:live]).then_inc(y_stored, 16)

                load(0)
                with sp.Fori(1, NCH) as ch:
                    sp.wait_ge(xtr_ready, 2 * ch)
                    load(ch)
                    store(ch - 1)
                store(NCH - 1, LAST)
                sp.wait_ge(y_stored, 16 * NCH + 16 * FREE)

            @block.gpsimd
            def _(pool):
                pool.wait_ge(cl, 32)

                def kb(v):
                    return v.rearrange("p f k b r -> p f (k b) r")

                with pool.Fori(0, NCH) as ch:
                    pool.wait_ge(ux_plain, 4 * ch + 4)
                    pool.wait_ge(tcur_ready, ch + 1)
                    cs, sn = (tcur[:, z, :].unsqueeze(2).unsqueeze(3) for z in range(2))
                    dims = [C, FC, 2 * NB, R - 1]
                    half = [C, FC, NB, R - 1]
                    nc.gpsimd.tensor_tensor(tw[:, 0], kb(ux[:, :, 0:2, :, R:RX]), cs.to_broadcast(dims), ALU.mult).then_inc(twist_step, 1)
                    nc.gpsimd.tensor_tensor(tw[:, 1], kb(ux[:, :, 1:3, :, R:RX]), sn.to_broadcast(dims), ALU.mult).then_inc(twist_step, 1)
                    pool.wait_ge(twist_step, 6 * ch + 2)
                    nc.gpsimd.tensor_tensor(kb(ux[:, :, 0:2, :, 0:R - 1]), tw[:, 0], tw[:, 1], ALU.add).then_inc(twist_step, 1)
                    pool.wait_ge(twist_step, 6 * ch + 3)
                    nc.gpsimd.tensor_tensor(tw[:, 0, :, 0:NB, :], ux[:, :, 2, :, R:RX], cs.to_broadcast(half), ALU.mult).then_inc(twist_step, 1)
                    nc.gpsimd.tensor_tensor(tw[:, 1, :, 0:NB, :], ux[:, :, 1, :, R:RX], sn.to_broadcast(half), ALU.mult).then_inc(twist_step, 1)
                    pool.wait_ge(twist_step, 6 * ch + 5)
                    nc.gpsimd.tensor_tensor(ux[:, :, 2, :, 0:R - 1], tw[:, 0, :, 0:NB, :], tw[:, 1, :, 0:NB, :], ALU.subtract).then_inc(twist_step, 1)

            @block.tensor
            def _(pe):
                pe.wait_ge(cl, 32)

                def turn_product(ch, live=FC):
                    pe.wait_ge(ye_evac, 2 * ch + len(halves(live)))
                    for half, nf in halves(live):
                        for f in range(nf):
                            last = nc.tensor.transpose(ps[0:Q, half, f * C:(f + 1) * C], ye[:, 4 * half + f, :], ident[:])
                        last.then_inc(ytr_ready, 1)

                def chunk(ch, first, live=FC):
                    pe.wait_ge(x_in, 16 * ch + 16)
                    if not first:
                        pe.wait_ge(yst_evac, 2 * (ch - 1) + FREE)
                    for half in range(2):
                        for f in range(4):
                            last = nc.tensor.transpose(ps[:, half, f * Q:(f + 1) * Q], xin[:, 4 * half + f, :], ident[0:Q, 0:Q])
                        last.then_inc(xtr_ready, 1)
                    pe.wait_ge(vcur_ready, ch + 1)
                    for blk in range(32):
                        if blk >= 4:
                            wait_g_read(pe, ch, blk - 4)
                        for e in range(4):
                            for odd in range(2):
                                o = (2 * e + odd) * 64
                                last = nc.tensor.matmul(ps[:, 2 + blk % 4, o:o + 64], ms[:, odd, 4 * blk + e, :], vcur[:, odd, :],
                                                        start=True, stop=True)
                        last.then_inc(g_ready, 1)
                    if not first:
                        pe.wait_ge(ux_plain, 4 * ch + 4)
                        turn_product(ch - 1)
                    wait_g_read(pe, ch, BY_DVE[-1])
                    wait_g_read(pe, ch, BY_ACT[-1])
                    pe.wait_ge(twist_step, 6 * ch + 6)
                    for half, nf in halves(live):
                        for f in range(nf):
                            fi = 4 * half + f
                            for m in range(16):
                                odd, sp_, c = m // 8, (m % 8) // 2, m % 2
                                s = 2 * sp_ + odd
                                parts = slice(1, 3) if c == 0 else slice(0, 2)
                                last = nc.tensor.matmul(ps[:, 6 + half, f * Q:(f + 1) * Q], gf[:, fi, m, :],
                                                        ux[:, fi, parts, :, R - 1 - s:RX - s].rearrange("p k b r -> p (k b) r"),
                                                        start=(m == 0), stop=(m == 15))
                        last.then_inc(y_ready, 1)

                chunk(0, True)
                with pe.Fori(1, NCH - 1) as ch:
                    chunk(ch, False)
                chunk(NCH - 1, False, LAST)
                pe.wait_ge(yst_evac, 2 * (NCH - 1) + FREE)
                turn_product(NCH - 1, LAST)

            @block.scalar
            def _(act):
                def chunk(ch, first, live=FC):
                    act.wait_ge(xtr_ready, 2 * ch + 1)
                    if not first:
                        act.wait_ge(y_ready, 2 * ch)
                    (dst, src), (neg, im) = plain(0)
                    nc.scalar.activation(dst, src, ACT.Copy).then_inc(ux_plain, 1)
                    nc.scalar.activation(neg, im, ACT.Copy, scale=-1.0).then_inc(ux_plain, 1)
                    for blk in BY_ACT:
                        act.wait_ge(g_ready, 32 * ch + blk + 1)
                        dst, src = spread(blk)
                        nc.scalar.activation(dst, src, ACT.Copy).then_inc(g_evac1, 1)
                    for half, nf in halves(live):
                        act.wait_ge(y_ready, 2 * ch + half + 1)
                        nc.scalar.activation(ye[:, 4 * half:4 * half + nf, :].rearrange("p f q -> p (f q)"), ps[:, 6 + half, 0:nf * Q], ACT.Copy).then_inc(ye_evac, 1)

                chunk(0, True)
                with act.Fori(1, NCH - 1) as ch:
                    chunk(ch, False)
                chunk(NCH - 1, False, LAST)

            @block.vector
            def _(dve):
                dve.sem_inc(yst_evac, FREE)
                dve.wait_ge(cl, 32)

                def stage_product(ch, live=FC):
                    dve.wait_ge(y_stored, 16 * ch + 16 * FREE)
                    for half, nf in halves(live):
                        dve.wait_ge(ytr_ready, 2 * ch + half + 1)
                        nc.vector.tensor_copy(yst[:, 4 * half:4 * half + nf, :].rearrange("p f e -> p (f e)"), ps[0:Q, half, 0:nf * C]).then_inc(yst_evac, 1)

                def chunk(ch, first, live=FC):
                    if not first:
                        dve.wait_ge(g_ready, 32 * ch)
                    nc.vector.tensor_copy(vcur[:].unsqueeze(1), vs[:, bass.ds(ch, 1)].rearrange("p a o s c f -> p a o (s c f)")).then_inc(vcur_ready, 1)
                    if not first:
                        dve.wait_ge(twist_step, 6 * ch)
                    nc.vector.tensor_copy(tcur[:], twist[:, :, bass.ds(ch * FC, FC)]).then_inc(tcur_ready, 1)
                    dve.wait_ge(xtr_ready, 2 * ch + 2)
                    if not first:
                        dve.wait_ge(y_ready, 2 * ch)
                    (dst, src), (neg, im) = plain(1)
                    nc.vector.tensor_copy(dst, src).then_inc(ux_plain, 1)
                    nc.vector.tensor_scalar(neg, im, -1.0, None, ALU.mult).then_inc(ux_plain, 1)
                    for blk in BY_DVE:
                        dve.wait_ge(g_ready, 32 * ch + blk + 1)
                        dst, src = spread(blk)
                        nc.vector.tensor_copy(dst, src).then_inc(g_evac0, 1)
                    if not first:
                        stage_product(ch - 1)

                chunk(0, True)
                with dve.Fori(1, NCH - 1) as ch:
                    chunk(ch, False)
                chunk(NCH - 1, False, LAST)
                stage_product(NCH - 1, LAST)


def inverse_and_store(nc, cst, prefix, prod_d, x2_d, out_d):
    with ExitStack() as ctx:
        def sb(name, shape, dt=F32):
            return ctx.enter_context(nc.sbuf_tensor(name, shape, dt))

        def sem(name):
            return ctx.enter_context(nc.semaphore(name))

        idft = sb("idft", [FT, NFT, N1])
        yin = sb("yin", [FT, 2, NFT, R * C])
        x2 = sb("x2", [C, 2, T])
        ps = ctx.enter_context(nc.psum_tensor("psc", [C, 8, 512], F32))
        cl, masked, z_ready, x3_done = map(sem, ("cc_loaded", "masked", "z_ready", "x3_done"))
        y_in, x2_in, stored = ([sem(f"{n}{z}") for z in range(2)] for n in ("y_in", "x2_in", "stored"))
        REACH = [(0, N1 // 8, 3), (N1 // 8, N1 // 4, 2), (N1 // 4, N1 // 2, 1), (N1 // 2, N1, 0)]
        with nc.Block() as block:
            @block.sync
            def _(sp):
                sp.dma_start(idft[:].rearrange("p a b -> p (a b)"), cst["idft"]).then_inc(cl, 16)
                with sp.Fori(0, NIMG // 2) as p:
                    for z in range(2):
                        b = 2 * p + z
                        sp.wait_ge(z_ready, 8 * b + 8)
                        for t in range(NFT):
                            for r0, r1, c, f0 in packed(t):
                                sp.dma_start(yin[r0:r1, z, t], prod_d[f0:f0 + r1 - r0].rearrange("f (c b r) e -> f c b (r e)", c=2, r=R)[:, c, bass.ds(b, 1), :]
                                             .rearrange("f b n -> f (b n)")).then_inc(y_in[z], 16)
                        sp.wait_ge(stored[z], 16 * p + 16 * FREE)
                        sp.dma_start(x2[:, z], x2_d[bass.ds(b, 1)].rearrange("a c t -> (a c) t")).then_inc(x2_in[z], 16)

            @block.scalar
            def _(act):
                for z in range(2):
                    act.sem_inc(stored[z], 16 * FREE)
                with act.Fori(0, NIMG // 2) as p:
                    for z in range(2):
                        act.wait_ge(x3_done, 8 * (2 * p + z) + 16)
                        act.dma_start(out_d[bass.ds(2 * p + z, 1)].rearrange("a c t -> (a c) t"), x2[:, z]).then_inc(stored[z], 16)
                for z in range(2):
                    act.wait_ge(stored[z], 16 * (NIMG // 2) + 16 * FREE)

            @block.tensor
            def _(pe):
                pe.sem_inc(z_ready, 16)
                pe.wait_ge(masked, 4)
                with pe.Fori(0, NIMG // 2) as p:
                    for z in range(2):
                        pe.wait_ge(y_in[z], 16 * NPACK * (p + 1))
                        for r in range(R):
                            pe.wait_ge(x3_done, 8 * (2 * p + z) + r + 1)
                            for t in range(NFT):
                                last = nc.tensor.matmul(ps[:, r, 0:N1], yin[:, z, t, r * C:(r + 1) * C], idft[:, t, :],
                                                        start=(t == 0), stop=(t == NFT - 1))
                            last.then_inc(z_ready, 1)

            @block.vector
            def _(dve):
                dve.sem_inc(x3_done, 8)
                dve.wait_ge(cl, 16)
                for a, b, i in REACH:
                    nc.vector.tensor_scalar(idft[:, :, a:b], idft[:, :, a:b], prefix[0:FT, i:i + 1], None, ALU.mult).then_inc(masked, 1)
                with dve.Fori(0, NIMG // 2) as p:
                    for z in range(2):
                        dve.wait_ge(x2_in[z], 16 * (p + 1))
                        for r in range(R):
                            dve.wait_ge(z_ready, 8 * (2 * p + z) + r + 1 + 16)
                            v = x2[:, z].rearrange("p (n r) -> p n r", r=R)[:, :, r]
                            nc.vector.tensor_tensor(v, v, ps[:, r, 0:N1], ALU.add).then_inc(x3_done, 1)


def program(nc, x, w_qkv, b_qkv, lepe_w, lepe_b, w_o, b_o, sigma, phi, m_u, m_plus, m_minus, log_weights, gumbel, cst, out):
    x2_d = nc.dram_tensor("x2_scratch", (NIMG, C, T), F32, kind="Internal").ap()
    spec_d = nc.dram_tensor("spectrum_scratch", (NF, 2, NIMG, R * C), F32, kind="Internal").ap()
    prod_d = nc.dram_tensor("product_scratch", (NF, 2 * NIMG * R, C), F32, kind="Internal").ap()
    route_d = nc.dram_tensor("route_scratch", (NIMG, NWIN * TOPK), U32, kind="Internal").ap()
    attention_and_dft(nc, x, w_qkv, b_qkv, lepe_w, lepe_b, w_o, b_o, cst, x2_d, spec_d, route_d)
    with nc.sbuf_tensor("prefix", [C, 4], F32) as prefix:
        filter_and_product(nc, phi, sigma, m_u, m_plus, m_minus, log_weights, gumbel, cst, prefix, spec_d, prod_d)
        inverse_and_store(nc, cst, prefix, prod_d, x2_d, out)


_INS = [("x", (NIMG, C, T)), ("L0_conv_W_qkv", (C, 3 * C)), ("L0_conv_b_qkv", (3 * C,)), ("L0_conv_lepe_w", (C, 9)),
        ("L0_conv_lepe_b", (C,)), ("L0_conv_W_o", (C, C)), ("L0_conv_b_o", (C,)), ("L0_ffn_sigma", (16,)),
        ("L0_ffn_phi", (4096, 16)), ("L0_ffn_M_u", (12, C * C)), ("L0_ffn_M_phi_plus", (64, C * C)),
        ("L0_ffn_M_phi_minus", (64, C * C)), ("L0_ffn_log_weights", (4,)), ("L0_ffn_gumbel", (4,))]


def kernel(**inputs):
    import numpy as _np
    import concourse.bacc as _bacc
    from concourse.bass_utils import run_bass_kernel_spmd as _run

    nc = _bacc.Bacc("TRN2", target_bir_lowering=False, num_devices=1)
    arrays, args, cst = {}, [], {}
    for name, shape in _INS:
        arrays[f"in_{name}_dram"] = _np.ascontiguousarray(inputs[name]).reshape(shape)
        args.append(nc.dram_tensor(f"in_{name}_dram", shape, F32, kind="ExternalInput").ap())
    for name, table in constants().items():
        arrays[f"const_{name}_dram"] = table
        cst[name] = nc.dram_tensor(f"const_{name}_dram", table.shape, F32, kind="ExternalInput").ap()
    out = nc.dram_tensor("out_0_dram", (NIMG, C, T), F32, kind="ExternalOutput").ap()
    program(nc, *args, cst, out)
    done = _run(nc, [arrays], core_ids=[0])
    return done.results[0]["out_0_dram"].reshape(NIMG, C, HW, HW)
```
